# Optimizing a Trainium2 kernel written in Bass

```python
import numpy as np
import jax
import jax.numpy as jnp

def _softmax(x, axis=-1):
    return jax.nn.softmax(x, axis=axis)

def _gelu(x):
    return jax.nn.gelu(x, approximate=True)

def _silu(x):
    return jax.nn.silu(x)

def _sigmoid(x):
    return jax.nn.sigmoid(x)

def _layernorm(x, axis=-1, eps=1e-05):
    m = jnp.mean(x, axis=axis, keepdims=True)
    v = jnp.var(x, axis=axis, keepdims=True)
    return (x - m) / jnp.sqrt(v + eps)

def _scatter_add(tgt, idx, src, axis=0):
    return tgt.at[idx].add(src)

def _segment_sum(src, seg, n):
    return jax.ops.segment_sum(src, seg, n)
kernel_name = 'mk_decoder_preln_d1_seqx_r4_de38f0'

def setup_inputs(seed: int=0):
    np.random.seed(seed)
    _w = jnp.asarray

    def _rec_inputs():
        import jax
        import jax.numpy as jnp
        _rk = jax.random.key(seed)
        x = 7.22e-05 + 1 * jax.random.normal(jax.random.fold_in(_rk, 1), (2, 1024, 256), jnp.float32)
        _lenS = 1024 - jax.random.randint(jax.random.fold_in(_rk, 7), (2,), 0, max(1, 1024 // 4) + 1, jnp.int32)
        _lenS2 = 64 - jax.random.randint(jax.random.fold_in(_rk, 8), (2,), 0, max(1, 64 // 4) + 1, jnp.int32)
        _ctx_768P = jax.random.normal(jax.random.fold_in(_rk, 11), (2, 16, 192), jnp.float32)
        _ctx_768c = jax.random.dirichlet(jax.random.fold_in(_rk, 511), 0.3 * jnp.ones((16,), jnp.float32), (2, 64))
        _ctx_768t = jnp.einsum('bsk,bkd->bsd', _ctx_768c, _ctx_768P)
        _ctx_768t = _ctx_768t * jax.lax.rsqrt(jnp.mean(jnp.square(_ctx_768t)) + 1e-12) * 0.953939
        ctx_768 = 2.09791e-05 + 1.00001 * (_ctx_768t + 0.3 * jax.random.normal(jax.random.fold_in(_rk, 611), (2, 64, 192), jnp.float32))
        return (x, ctx_768)
    x, ctx_768 = _rec_inputs()

    def _L0_attn_setup():
        import jax, jax.numpy as jnp
        import numpy as np
        D_MODEL = 256
        N_HEADS = 16
        HEAD_DIM = D_MODEL // N_HEADS
        D_LATENT = 64
        LAMBDA_DECAY = 0.01
        TIME_STEP = 0.01
        CLAMP = 10000.0

        def _reference_tuple_inner(x, Wq, Wk, Wv, Wo, W_down_kv, W_up_k, W_up_v):
            B, S, _ = x.shape
            q = x @ Wq
            k = x @ Wk
            v = x @ Wv
            latent_kv = (k + v) @ W_down_kv
            k_rec = latent_kv @ W_up_k
            v_rec = latent_kv @ W_up_v

            def heads(t):
                return t.reshape(B, S, N_HEADS, HEAD_DIM).transpose(0, 2, 1, 3)
            qh, kh, vh = (heads(q), heads(k_rec), heads(v_rec))
            scale = 1.0 / (jnp.sqrt(jnp.float32(D_MODEL)) + 1e-08)
            scores = jnp.einsum('bhqd,bhkd->bhqk', qh, kh) * scale
            scores = jnp.clip(jnp.nan_to_num(scores, nan=-1000000000.0), -CLAMP, CLAMP)
            idx = jnp.arange(S, dtype=jnp.float32)
            decay = jnp.exp(-LAMBDA_DECAY * TIME_STEP * jnp.abs(idx[:, None] - idx[None, :]))
            scores = scores * decay[None, None, :, :]
            scores = jnp.clip(jnp.nan_to_num(scores, nan=-1000000000.0), -CLAMP, CLAMP)
            attn = jax.nn.softmax(scores, axis=-1)
            out = jnp.einsum('bhqk,bhkd->bhqd', attn, vh)
            out = out.transpose(0, 2, 1, 3).reshape(B, S, D_MODEL)
            return (out @ Wo, latent_kv)
        key = jax.random.key(seed)
        ks = jax.random.split(key, 8)
        B, S = (2, 512)

        def w(k, i, o):
            return jax.random.normal(k, (i, o), dtype=jnp.float32) * 0.02
        return {'x': jax.random.normal(ks[0], (B, S, D_MODEL), dtype=jnp.float32), 'Wq': w(ks[1], D_MODEL, D_MODEL), 'Wk': w(ks[2], D_MODEL, D_MODEL), 'Wv': w(ks[3], D_MODEL, D_MODEL), 'Wo': w(ks[4], D_MODEL, D_MODEL), 'W_down_kv': w(ks[5], D_MODEL, D_LATENT), 'W_up_k': w(ks[6], D_LATENT, D_MODEL), 'W_up_v': w(ks[7], D_LATENT, D_MODEL)}
    _L0_attn_all = _L0_attn_setup()
    _L0_attn_in = {k: v for k, v in _L0_attn_all.items() if k in ('Wq', 'Wk', 'Wv', 'Wo', 'W_down_kv', 'W_up_k', 'W_up_v')}
    del _L0_attn_all

    def _L0_xattn_setup():
        import jax, jax.numpy as jnp
        import numpy as np
        NUM_HEADS = 16
        key = jax.random.key(seed)
        ks = jax.random.split(key, 8)
        dim, cond_dim = (256, 192)
        B, N, condN = (4, 512, 256)
        s = lambda k, shp, fan: jax.random.normal(k, shp, dtype=jnp.float32) * fan ** (-0.5)
        return {'x': jax.random.normal(ks[0], (B, N, dim), dtype=jnp.float32), 'cond': jax.random.normal(ks[1], (B, condN, cond_dim), dtype=jnp.float32), 'q_w': s(ks[2], (dim, dim), dim), 'q_b': jnp.zeros((dim,), jnp.float32), 'kv_w': s(ks[3], (cond_dim, 2 * dim), cond_dim), 'kv_b': jnp.zeros((2 * dim,), jnp.float32), 'proj_w': s(ks[4], (dim, dim), dim), 'proj_b': jnp.zeros((dim,), jnp.float32)}
    _L0_xattn_all = _L0_xattn_setup()
    _L0_xattn_in = {k: v for k, v in _L0_xattn_all.items() if k in ('q_w', 'q_b', 'kv_w', 'kv_b', 'proj_w', 'proj_b')}
    del _L0_xattn_all

    def _L0_ffn_setup():
        import jax, jax.numpy as jnp
        import numpy as np
        B, S, D = (2, 512, 256)
        E, K, F = (16, 2, 128)
        FS = 256
        key = jax.random.key(seed)
        ks = jax.random.split(key, 8)

        def w(k, shape, fan_in):
            return jax.random.normal(k, shape, jnp.float32) / np.sqrt(fan_in).astype(np.float32)
        return {'x': jax.random.normal(ks[0], (B, S, D), jnp.float32), 'Wr': w(ks[1], (D, E), D), 'Wg': w(ks[2], (E, D, F), D), 'Wu': w(ks[3], (E, D, F), D), 'Wd': w(ks[4], (E, F, D), F), 'Sg': w(ks[5], (D, FS), D), 'Su': w(ks[6], (D, FS), D), 'Sd': w(ks[7], (FS, D), FS)}
    _L0_ffn_all = _L0_ffn_setup()
    _L0_ffn_in = {k: v for k, v in _L0_ffn_all.items() if k in ('Wr', 'Wg', 'Wu', 'Wd', 'Sg', 'Su', 'Sd')}
    del _L0_ffn_all
    return {'x': x, 'ctx_768': ctx_768, 'L0_attn_Wq': _L0_attn_in['Wq'], 'L0_attn_Wk': _L0_attn_in['Wk'], 'L0_attn_Wv': _L0_attn_in['Wv'], 'L0_attn_Wo': _L0_attn_in['Wo'], 'L0_attn_W_down_kv': _L0_attn_in['W_down_kv'], 'L0_attn_W_up_k': _L0_attn_in['W_up_k'], 'L0_attn_W_up_v': _L0_attn_in['W_up_v'], 'L0_xattn_q_w': _L0_xattn_in['q_w'], 'L0_xattn_q_b': _L0_xattn_in['q_b'], 'L0_xattn_kv_w': _L0_xattn_in['kv_w'], 'L0_xattn_kv_b': _L0_xattn_in['kv_b'], 'L0_xattn_proj_w': _L0_xattn_in['proj_w'], 'L0_xattn_proj_b': _L0_xattn_in['proj_b'], 'L0_ffn_Wr': _L0_ffn_in['Wr'], 'L0_ffn_Wg': _L0_ffn_in['Wg'], 'L0_ffn_Wu': _L0_ffn_in['Wu'], 'L0_ffn_Wd': _L0_ffn_in['Wd'], 'L0_ffn_Sg': _L0_ffn_in['Sg'], 'L0_ffn_Su': _L0_ffn_in['Su'], 'L0_ffn_Sd': _L0_ffn_in['Sd']}

def reference(x, ctx_768, L0_attn_Wq, L0_attn_Wk, L0_attn_Wv, L0_attn_Wo, L0_attn_W_down_kv, L0_attn_W_up_k, L0_attn_W_up_v, L0_xattn_q_w, L0_xattn_q_b, L0_xattn_kv_w, L0_xattn_kv_b, L0_xattn_proj_w, L0_xattn_proj_b, L0_ffn_Wr, L0_ffn_Wg, L0_ffn_Wu, L0_ffn_Wd, L0_ffn_Sg, L0_ffn_Su, L0_ffn_Sd):
    import jax
    import jax.numpy as jnp

    def _L0_attn_ref(x, Wq, Wk, Wv, Wo, W_down_kv, W_up_k, W_up_v):
        import jax, jax.numpy as jnp
        import numpy as np
        D_MODEL = 256
        N_HEADS = 16
        HEAD_DIM = D_MODEL // N_HEADS
        D_LATENT = 64
        LAMBDA_DECAY = 0.01
        TIME_STEP = 0.01
        CLAMP = 10000.0

        def _reference_tuple_inner(x, Wq, Wk, Wv, Wo, W_down_kv, W_up_k, W_up_v):
            B, S, _ = x.shape
            q = x @ Wq
            k = x @ Wk
            v = x @ Wv
            latent_kv = (k + v) @ W_down_kv
            k_rec = latent_kv @ W_up_k
            v_rec = latent_kv @ W_up_v

            def heads(t):
                return t.reshape(B, S, N_HEADS, HEAD_DIM).transpose(0, 2, 1, 3)
            qh, kh, vh = (heads(q), heads(k_rec), heads(v_rec))
            scale = 1.0 / (jnp.sqrt(jnp.float32(D_MODEL)) + 1e-08)
            scores = jnp.einsum('bhqd,bhkd->bhqk', qh, kh) * scale
            scores = jnp.clip(jnp.nan_to_num(scores, nan=-1000000000.0), -CLAMP, CLAMP)
            idx = jnp.arange(S, dtype=jnp.float32)
            decay = jnp.exp(-LAMBDA_DECAY * TIME_STEP * jnp.abs(idx[:, None] - idx[None, :]))
            scores = scores * decay[None, None, :, :]
            scores = jnp.clip(jnp.nan_to_num(scores, nan=-1000000000.0), -CLAMP, CLAMP)
            attn = jax.nn.softmax(scores, axis=-1)
            out = jnp.einsum('bhqk,bhkd->bhqd', attn, vh)
            out = out.transpose(0, 2, 1, 3).reshape(B, S, D_MODEL)
            return (out @ Wo, latent_kv)
        return _reference_tuple_inner(x, Wq, Wk, Wv, Wo, W_down_kv, W_up_k, W_up_v)[0]

    def _L0_xattn_ref(x, cond, q_w, q_b, kv_w, kv_b, proj_w, proj_b):
        import jax, jax.numpy as jnp
        import numpy as np
        NUM_HEADS = 16
        B, N, C = x.shape
        condN = cond.shape[1]
        H = NUM_HEADS
        hd = C // H
        scale = hd ** (-0.5)
        q = (x @ q_w + q_b).reshape(B, N, H, hd).transpose(0, 2, 1, 3)
        kv = (cond @ kv_w + kv_b).reshape(B, condN, 2, H, hd)
        k = kv[:, :, 0].transpose(0, 2, 1, 3)
        v = kv[:, :, 1].transpose(0, 2, 1, 3)
        attn = jnp.einsum('bhnd,bhmd->bhnm', q * scale, k)
        attn = jax.nn.softmax(attn, axis=-1)
        out = jnp.einsum('bhnm,bhmd->bhnd', attn, v)
        out = out.transpose(0, 2, 1, 3).reshape(B, N, C)
        return out @ proj_w + proj_b

    def _L0_ffn_ref(x, Wr, Wg, Wu, Wd, Sg, Su, Sd):
        import jax, jax.numpy as jnp
        import numpy as np
        B, S, D = (2, 512, 256)
        E, K, F = (16, 2, 128)
        FS = 256
        b, s, d = x.shape
        T = b * s
        xf = x.reshape(T, d)
        shared = jax.nn.silu(xf @ Sg) * (xf @ Su) @ Sd
        probs = jax.nn.softmax(xf @ Wr, axis=-1)
        topk_p, topk_i = jax.lax.top_k(probs, K)
        n_exp = Wr.shape[1]
        cw = jnp.zeros((T, n_exp), x.dtype).at[jnp.arange(T)[:, None], topk_i].add(topk_p)

        def step(acc, ew):
            wg, wu, wd, c = ew
            y = jax.nn.silu(xf @ wg) * (xf @ wu) @ wd
            return (acc + y * c[:, None], None)
        routed, _ = jax.lax.scan(step, jnp.zeros_like(xf), (Wg, Wu, Wd, cw.T))
        return (routed + shared).reshape(b, s, d)
    x = x + _L0_attn_ref(_layernorm(x, axis=-1), L0_attn_Wq, L0_attn_Wk, L0_attn_Wv, L0_attn_Wo, L0_attn_W_down_kv, L0_attn_W_up_k, L0_attn_W_up_v)
    x = x + _L0_xattn_ref(_layernorm(x, axis=-1), ctx_768, L0_xattn_q_w, L0_xattn_q_b, L0_xattn_kv_w, L0_xattn_kv_b, L0_xattn_proj_w, L0_xattn_proj_b)
    x = x + _L0_ffn_ref(_layernorm(x, axis=-1), L0_ffn_Wr, L0_ffn_Wg, L0_ffn_Wu, L0_ffn_Wd, L0_ffn_Sg, L0_ffn_Su, L0_ffn_Sd)
    return x

_drawn_inputs = setup_inputs


def setup_inputs(seed=0):
    import zlib

    import numpy as np

    out = dict(_drawn_inputs(seed))
    spreads = {'L0_xattn_q_b': (0.0, 0.8), 'L0_xattn_kv_b': (0.0, 0.8), 'L0_xattn_proj_b': (0.0, 0.8)}
    factors = {'L0_attn_Wq': 8.0,
     'L0_attn_Wk': 8.0,
     'L0_attn_Wv': 8.0,
     'L0_attn_Wo': 8.0,
     'L0_attn_W_down_kv': 8.0,
     'L0_attn_W_up_k': 8.0,
     'L0_attn_W_up_v': 8.0,
     'ctx_768': 2.934,
     'L0_xattn_q_w': 6.502,
     'L0_ffn_Wr': 8.0,
     'L0_ffn_Wg': 8.0,
     'L0_ffn_Wu': 7.896,
     'L0_ffn_Wd': 7.943,
     'L0_ffn_Sg': 8.0,
     'L0_ffn_Su': 8.0,
     'L0_ffn_Sd': 8.0}
    for name, (base, spread) in spreads.items():
        noise = np.random.default_rng([zlib.crc32(name.encode()), seed]).standard_normal(out[name].shape)
        drawn = base * np.exp(spread * noise) if base else spread * noise
        out[name] = jnp.asarray(drawn.astype(out[name].dtype))
    for name, factor in factors.items():
        out[name] = (out[name] * factor).astype(out[name].dtype)
    return out
```

```python
from contextlib import ExitStack

import concourse.bass as bass
from concourse import mybir

ALU = mybir.AluOpType
ACT = mybir.ActivationFunctionType
F32 = mybir.dt.float32
I32 = mybir.dt.int32
U32 = mybir.dt.uint32
AX_X = mybir.AxisListType.X
ds = bass.ds

P = 128
B, S, D = 2, 1024, 256
T = B * S
TILES = T // P
CT = 4
CHUNK = CT * P
NCHUNK = T // CHUNK
KD = D // P
H, HD = 16, 16
HH = P // HD
ST = S // P
LAT = 64
CS, CD = 64, 192
E_ROUTED, F = 16, 128
FS = 256
NE = E_ROUTED + FS // F
WCOLS = KD * F * 2 + D
CLAMP = 10000.0
DECAY = 0.01 * 0.01
EPS = 1e-5
ATTN_SCALE = 1.0 / 16.0
X_SCALE = HD ** -0.5


def decoder_layer(nc, x, ctx_in, wq, wk, wv, wo, w_down, w_up_k, w_up_v, xq_w, xq_b, xkv_w, xkv_b,
                  xproj_w, xproj_b, wr, wg, wu, wd, sg, su, sd, out):
    with ExitStack() as stack:
        def sb(name, shape, dt=F32):
            return stack.enter_context(nc.sbuf_tensor(name, shape, dt))

        def sem(name):
            return stack.enter_context(nc.semaphore(name))

        ps = stack.enter_context(nc.psum_tensor("ps", [P, 8, 512], F32))

        def bank(i, n=1):
            return ps[:, i:i + n, :]

        resid = sb("resid", [P, TILES, D])
        wq_sb = sb("wq_sb", [P, KD, D])
        wkv_sb = sb("wkv_sb", [P, KD, D])
        wv_sb = sb("wv_sb", [P, KD, D])
        wdown_sb = sb("wdown_sb", [P, KD, LAT])
        wup_sb = sb("wup_sb", [LAT, 2, D])
        wo_sb = sb("wo_sb", [P, KD, D])
        xq_sb = sb("xq_sb", [P, KD, D])
        xqb_sb = sb("xqb_sb", [P, KD])
        xkv_hi = sb("xkv_hi", [P, 2 * D])
        xkv_lo = sb("xkv_lo", [CD - P, 2 * D])
        xkb_sb = sb("xkb_sb", [P, KD])
        brow = sb("brow", [1, 2, D])
        xproj_sb = sb("xproj_sb", [P, KD, D])
        wr_sb = sb("wr_sb", [P, KD, E_ROUTED])
        ident = sb("ident", [P, P])
        ones_row = sb("ones_row", [1, P])
        head_mask = sb("head_mask", [P, HH])
        decay = sb("decay", [P, 1920])
        eidx_i = sb("eidx_i", [P, E_ROUTED], I32)
        eidx = sb("eidx", [P, E_ROUTED])
        scratch = sb("scratch", [P, 1])
        stats = sb("stats", [P, CT, 6])
        mv = sb("mv", [P, CT, 2])
        std = sb("std", [P, CT])
        rstd = sb("rstd", [P, CT])
        xn = sb("xn", [P, CT, D])
        xnT = sb("xnT", [P, KD, CHUNK])
        kvT = sb("kvT", [P, KD, CHUNK])
        latT = sb("latT", [LAT, CHUNK])
        qT = sb("qT", [P, KD, T])
        kT = sb("kT", [P, KD, T])
        val = sb("val", [P, TILES, D])
        att = sb("att", [P, TILES, D])
        diff_i = att[:].rearrange("p t d -> p (t d)")[:, 0:1920].bitcast(I32)
        qm = sb("qm", [P, S])
        sc_clip = sb("sc_clip", [P, S])
        sc_dec = sb("sc_dec", [P, 2, S])
        prob = sb("prob", [P, S])
        probT = sb("probT", [P, ST, P])
        rmax = sb("rmax", [P, ST])
        nmax = sb("nmax", [P, ST])
        rsum = sb("rsum", [P, ST])
        rinv = sb("rinv", [P, ST])
        ctx_sb = sb("ctx_sb", [P, B, CD])
        ctxT_hi = sb("ctxT_hi", [P, B, P])
        ctxT_lo = sb("ctxT_lo", [CD - P, B, P])
        xkT = sb("xkT", [P, KD, B, CS])
        xk_bd = sb("xk_bd", [P, B, KD, HH, CS])
        xv_bd = sb("xv_bd", [P, B, HH, 2 * HD])
        xv_cur = sb("xv_cur", [P, HH, 2 * HD])
        att_c = sb("att_c", [P, CT, D])
        oT = sb("oT", [P, KD, CHUNK])
        spent = val[:].rearrange("p (a t) d -> p a (t d)", a=4)
        xqT = spent[:, 0, :].rearrange("p (k q) -> p k q", k=KD)
        xmax = sb("xmax", [P, H])
        xsc = spent[:, 1, :].rearrange("p (h s) -> p h s", s=CS)
        xp = spent[:, 2, :].rearrange("p (h s) -> p h s", s=CS)
        xsum = sb("xsum", [P, H])
        xinv = sb("xinv", [P, H])
        xpn = spent[:, 3, :].rearrange("p (h s) -> p h s", s=CS)
        xpT = kT[:].rearrange("p k (j q) -> p (k j) q", q=CHUNK)
        logit = sb("logit", [P, CT, E_ROUTED])
        top = sb("top", [P, CT, 8])
        topi = sb("topi", [P, CT, 8], U32)
        topf = sb("topf", [P, CT, 2])
        ntop = sb("ntop", [P, CT])
        rexp = sb("rexp", [P, CT, E_ROUTED])
        resum = sb("resum", [P, CT])
        reinv = sb("reinv", [P, CT])
        pick = sb("pick", [P, CT, 2, E_ROUTED])
        picked = sb("picked", [P, CT, E_ROUTED])
        cw = sb("cw", [P, TILES, NE])
        fT = qT
        wcur = sb("wcur", [P, 2, WCOLS])
        silu = sb("silu", [P, CHUNK])
        hid = sb("hid", [P, CHUNK])

        s_x = sem("s_x"); s_w = sem("s_w"); s_wb = sem("s_wb"); s_out = sem("s_out")
        s_const = sem("s_const"); s_mask = sem("s_mask"); s_pool = sem("s_pool")
        s_decay = sem("s_decay"); s_wkv = sem("s_wkv")
        s_ln = sem("s_ln"); s_var = sem("s_var"); s_std = sem("s_std"); s_xn = sem("s_xn")
        s_xnT_ps = sem("s_xnT_ps"); s_xnT = sem("s_xnT")
        s_q_ps = sem("s_q_ps"); s_q = sem("s_q"); s_kv_ps = sem("s_kv_ps"); s_kv = sem("s_kv")
        s_lat_ps = sem("s_lat_ps"); s_lat = sem("s_lat"); s_k_ps = sem("s_k_ps"); s_k = sem("s_k")
        s_v_ps = sem("s_v_ps"); s_v = sem("s_v")
        s_qm = sem("s_qm"); s_sc = sem("s_sc"); s_clip = sem("s_clip"); s_dec = sem("s_dec")
        s_nmax = sem("s_nmax"); s_prob = sem("s_prob"); s_pT_ps = sem("s_pT_ps"); s_pT = sem("s_pT")
        s_o_ps = sem("s_o_ps"); s_rinv = sem("s_rinv"); s_o = sem("s_o")
        s_cT_ps = sem("s_cT_ps"); s_cT = sem("s_cT"); s_ck_ps = sem("s_ck_ps"); s_ck = sem("s_ck")
        s_cv_ps = sem("s_cv_ps"); s_cv = sem("s_cv"); s_cbd = sem("s_cbd")
        s_attc = sem("s_attc"); s_xvc = sem("s_xvc"); s_oT_ps = sem("s_oT_ps"); s_oT = sem("s_oT")
        s_wo = sem("s_wo"); s_res = sem("s_res"); s_xq_ps = sem("s_xq_ps"); s_xq = sem("s_xq")
        s_xs = sem("s_xs"); s_xmax = sem("s_xmax"); s_xsub = sem("s_xsub"); s_xp = sem("s_xp")
        s_xsum = sem("s_xsum"); s_xinv = sem("s_xinv"); s_xpn = sem("s_xpn")
        s_xpT_ps = sem("s_xpT_ps"); s_xpT = sem("s_xpT"); s_xo_ps = sem("s_xo_ps"); s_xo = sem("s_xo")
        s_pj = sem("s_pj"); s_res2 = sem("s_res2"); s_fT = sem("s_fT")
        s_lg_ps = sem("s_lg_ps"); s_lg = sem("s_lg"); s_rt = sem("s_rt"); s_route = sem("s_route"); s_rexp = sem("s_rexp")
        s_wcur = [sem("s_wcur0"), sem("s_wcur1")]; s_gu = sem("s_gu"); s_silu = sem("s_silu"); s_hid = sem("s_hid")
        s_y = sem("s_y"); s_acc = sem("s_acc")

        x_d = x.rearrange("b (n p) d -> p (b n) d", p=P)
        out_d = out.rearrange("b (n p) d -> p (b n) d", p=P)
        NW = 11
        NWB = 7

        block = stack.enter_context(nc.Block())

        @block.sync
        def _(sp):
            for c in range(NCHUNK):
                sp.dma_start(resid[:, c * CT:(c + 1) * CT, :], x_d[:, c * CT:(c + 1) * CT, :]).then_inc(s_x, 16)
            sp.dma_start(wq_sb[:], wq.rearrange("(k p) n -> p k n", p=P)).then_inc(s_w, 16)
            sp.dma_start(wkv_sb[:], wk.rearrange("(k p) n -> p k n", p=P)).then_inc(s_w, 16)
            sp.dma_start(wv_sb[:], wv.rearrange("(k p) n -> p k n", p=P)).then_inc(s_w, 16)
            sp.dma_start(wdown_sb[:], w_down.rearrange("(k p) n -> p k n", p=P)).then_inc(s_w, 16)
            sp.dma_start(wup_sb[:, 0, :], w_up_k).then_inc(s_w, 16)
            sp.dma_start(wup_sb[:, 1, :], w_up_v).then_inc(s_w, 16)
            sp.dma_start(wo_sb[:], wo.rearrange("(k p) n -> p k n", p=P)).then_inc(s_w, 16)
            sp.dma_start(xq_sb[:], xq_w.rearrange("(k p) n -> p k n", p=P)).then_inc(s_w, 16)
            sp.dma_start(xproj_sb[:], xproj_w.rearrange("(k p) n -> p k n", p=P)).then_inc(s_w, 16)
            sp.dma_start(xkv_hi[:], xkv_w[0:P, :]).then_inc(s_w, 16)
            sp.dma_start(xkv_lo[:], xkv_w[P:CD, :]).then_inc(s_w, 16)
            for r in range(2):
                sp.dma_start(ctx_sb[r * CS:(r + 1) * CS, :, :], ctx_in.rearrange("b s d -> s b d")).then_inc(s_wb, 16)
            with nc.allow_non_contiguous_dma("biases, one channel to a partition"):
                sp.dma_start(xqb_sb[:], xq_b.rearrange("(k p) -> p k", p=P)).then_inc(s_wb, 16)
                sp.dma_start(xkb_sb[:], xkv_b[0:D].rearrange("(k p) -> p k", p=P)).then_inc(s_wb, 16)
                sp.dma_start(wr_sb[:], wr.rearrange("(k p) n -> p k n", p=P)).then_inc(s_wb, 16)
            sp.dma_start(brow[:, 0, :], xkv_b[D:2 * D].rearrange("(a n) -> a n", a=1)).then_inc(s_wb, 16)
            sp.dma_start(brow[:, 1, :], xproj_b.rearrange("(a n) -> a n", a=1)).then_inc(s_wb, 16)

            def load_expert(slot, gate, up, down):
                sp.dma_start(wcur[:, slot, 0:2 * F].rearrange("p (k f) -> p k f", k=KD), gate).then_inc(s_wcur[slot], 16)
                sp.dma_start(wcur[:, slot, 2 * F:4 * F].rearrange("p (k f) -> p k f", k=KD), up).then_inc(s_wcur[slot], 16)
                sp.dma_start(wcur[:, slot, 4 * F:], down).then_inc(s_wcur[slot], 16)

            def load_routed(slot, e):
                load_expert(slot, *(w[ds(e, 1), :, :].rearrange("a (k p) f -> p (a k) f", p=P) for w in (wg, wu)),
                            wd[ds(e, 1), :, :].rearrange("a f d -> f (a d)"))

            for slot in range(2):
                load_routed(slot, slot)
            with sp.Fori(1, E_ROUTED // 2) as i:
                for slot in range(2):
                    sp.wait_ge(s_y, NCHUNK * (2 * i + slot - 1) + 1)
                    load_routed(slot, 2 * i + slot)
            for slot in range(2):
                sp.wait_ge(s_y, NCHUNK * (E_ROUTED + slot - 1) + 1)
                cols = slice(slot * F, (slot + 1) * F)
                load_expert(slot, *(w[:, cols].rearrange("(k p) f -> p k f", p=P) for w in (sg, su)), sd[cols, :])
            sp.wait_ge(s_acc, NE * NCHUNK + 1)
            sp.dma_start(out_d, resid[:]).then_inc(s_out, 16)
            sp.wait_ge(s_out, 16)

        @block.gpsimd
        def _(pool):
            for s in (s_attc, s_xvc, s_fT):
                pool.sem_inc(s, 1)

            nc.gpsimd.memset(ident[:], 0.0).then_inc(s_pool, 1)
            nc.gpsimd.memset(head_mask[:], 1.0).then_inc(s_pool, 1)
            nc.gpsimd.memset(ones_row[:], 1.0).then_inc(s_const, 1)
            nc.gpsimd.memset(xv_bd[:], 0.0).then_inc(s_const, 1)
            nc.gpsimd.memset(cw[:], 1.0).then_inc(s_const, 1)
            pool.wait_ge(s_pool, 2)
            nc.gpsimd.affine_select(out=ident[:], in_=ident[:], compare_op=ALU.not_equal, fill=1.0, base=0,
                                    pattern=[[-1, P]], channel_multiplier=1).then_inc(s_const, 1)
            nc.gpsimd.affine_select(out=head_mask[:], in_=head_mask[:], compare_op=ALU.is_ge, fill=0.0, base=0,
                                    pattern=[[-HD, HH]], channel_multiplier=1).then_inc(s_pool, 1)
            pool.wait_ge(s_pool, 3)
            nc.gpsimd.affine_select(out=head_mask[:], in_=head_mask[:], compare_op=ALU.is_ge, fill=0.0, base=HD - 1,
                                    pattern=[[HD, HH]], channel_multiplier=-1).then_inc(s_const, 1)
            nc.gpsimd.iota(diff_i, pattern=[[-1, 1920]], base=S - P, channel_multiplier=1).then_inc(s_const, 1)
            nc.gpsimd.iota(eidx_i[:], pattern=[[1, E_ROUTED]], base=0, channel_multiplier=0).then_inc(s_const, 1)

            with pool.Fori(0, NCHUNK) as c:
                pool.wait_ge(s_o, B * H * ST + 1)
                pool.wait_ge(s_oT_ps, c + 1)
                nc.gpsimd.tensor_copy(att_c[:], att[:, ds(c * CT, CT), :]).then_inc(s_attc, 1)
                pool.wait_ge(s_cbd, 1)
                pool.wait_ge(s_xo_ps, c + 1)
                nc.gpsimd.tensor_copy(xv_cur[:], xv_bd[:, ds(c // 2, 1), :, :].rearrange("p a h n -> p (a h) n"))\
                    .then_inc(s_xvc, 1)
                pool.wait_ge(s_xnT, NCHUNK + 2 * c + 3)
                nc.gpsimd.tensor_copy(fT[:, :, ds(c * CHUNK, CHUNK)], xnT[:]).then_inc(s_fT, 1)

        @block.tensor
        def _(pe):
            for s in (s_xnT_ps, s_q_ps, s_kv_ps, s_lat_ps, s_k_ps, s_v_ps, s_sc, s_pT_ps, s_o_ps, s_oT_ps, s_wo,
                      s_xq_ps, s_xs, s_xpT_ps, s_xo_ps, s_pj, s_lg_ps, s_gu, s_y):
                pe.sem_inc(s, 1)

            def transposes(src):
                for k in range(KD):
                    for t in range(CT):
                        last = nc.tensor.transpose(ps[:, k, t * P:(t + 1) * P], src[:, t, k * P:(k + 1) * P], ident[:])
                return last

            def project(first, w, rhs, rows=P):
                for n in range(KD):
                    for k in range(KD):
                        last = nc.tensor.matmul(ps[0:rows, first + n, :], w[:, k, n * P:n * P + rows], rhs[:, k, :],
                                                start=(k == 0), stop=(k == KD - 1))
                return last

            pe.wait_ge(s_const, 7)
            pe.wait_ge(s_w, 16 * NW)
            pe.wait_ge(s_wkv, 1)

            with pe.Fori(0, NCHUNK) as c:
                pe.wait_ge(s_xn, c + 2)
                pe.wait_ge(s_k, c + 1)
                transposes(xn).then_inc(s_xnT_ps, 1)
                pe.wait_ge(s_xnT, c + 2)
                pe.wait_ge(s_q, c + 1)
                project(2, wq_sb, xnT).then_inc(s_q_ps, 1)
                pe.wait_ge(s_kv, c + 1)
                project(4, wkv_sb, xnT).then_inc(s_kv_ps, 1)
                pe.wait_ge(s_kv, c + 2)
                pe.wait_ge(s_v, c + 1)
                for k in range(KD):
                    mm = nc.tensor.matmul(ps[0:LAT, 6, :], wdown_sb[:, k, :], kvT[:, k, :], start=(k == 0), stop=(k == KD - 1))
                mm.then_inc(s_lat_ps, 1)
                pe.wait_ge(s_lat, c + 2)
                for n in range(KD):
                    mm = nc.tensor.matmul(ps[:, n, :], wup_sb[:, 0, n * P:(n + 1) * P], latT[:], start=True, stop=True)
                mm.then_inc(s_k_ps, 1)
                for t in range(CT):
                    mm = nc.tensor.matmul(ps[:, 6 + t // 2, (t % 2) * D:(t % 2 + 1) * D], latT[:, t * P:(t + 1) * P],
                                          wup_sb[:, 1, :], start=True, stop=True)
                mm.then_inc(s_v_ps, 1)

            pe.wait_ge(s_v, NCHUNK + 1)
            pe.wait_ge(s_q, NCHUNK + 1)
            pe.wait_ge(s_k, NCHUNK + 1)
            pe.wait_ge(s_wb, 16 * NWB)
            for b in range(B):
                nc.tensor.transpose(ps[:, 0, b * P:(b + 1) * P], ctx_sb[:, b, 0:P], ident[:])
                mm = nc.tensor.transpose(ps[0:CD - P, 1, b * P:(b + 1) * P], ctx_sb[:, b, P:CD], ident[:])
            mm.then_inc(s_cT_ps, 1)
            pe.wait_ge(s_cT, 2)
            for n in range(KD):
                dst = ps[:, 2, n * P:(n + 1) * P].rearrange("p (b s) -> p b s", b=B)
                nc.tensor.matmul(dst, xkv_hi[:, n * P:(n + 1) * P], ctxT_hi[:, :, 0:CS], start=True, stop=False)
                mm = nc.tensor.matmul(dst, xkv_lo[:, n * P:(n + 1) * P], ctxT_lo[:, :, 0:CS], start=False, stop=True)
            mm.then_inc(s_ck_ps, 1)
            for b in range(B):
                dst = ps[:, 3, b * D:(b + 1) * D]
                nc.tensor.matmul(dst, ctxT_hi[:, b, :], xkv_hi[:, D:], start=True, stop=False)
                nc.tensor.matmul(dst, ctxT_lo[:, b, :], xkv_lo[:, D:], start=False, stop=False)
                mm = nc.tensor.matmul(dst, ones_row[:], brow[:, 0, :], start=False, stop=True)
            mm.then_inc(s_cv_ps, 1)
            pe.wait_ge(s_ck, KD * HH + KD)
            pe.wait_ge(s_cv, 2)

            def scores(half, b, n, qt):
                pe.wait_ge(s_clip, (n * ST + qt - 1 + 1 if qt == 0 else n * ST + qt - 1) + 1)
                for g in range(2):
                    mm = nc.tensor.matmul(ps[:, 2 * (qt % 2) + g, :], qm[:, qt * P:(qt + 1) * P],
                                          kT[:, ds(half, 1), ds(b * S + g * 512, 512)].rearrange("p a n -> p (a n)"),
                                          start=True, stop=True)
                mm.then_inc(s_sc, 1)

            with pe.Fori(0, B) as b:
                with pe.Fori(0, KD) as half:
                    with pe.Fori(0, HH) as j:
                        n = b * H + half * HH + j
                        pe.wait_ge(s_qm, n + 2)
                        scores(half, b, n, 0)
                        for qt in range(ST):
                            if qt + 1 < ST:
                                scores(half, b, n, qt + 1)
                            pe.wait_ge(s_prob, n * ST + qt + 2)
                            pe.wait_ge(s_pT, n * ST + qt + 1)
                            for kt in range(ST):
                                mm = nc.tensor.transpose(ps[:, 4 + kt // 4, (kt % 4) * P:(kt % 4 + 1) * P],
                                                         prob[:, kt * P:(kt + 1) * P], ident[:])
                            mm.then_inc(s_pT_ps, 1)
                            pe.wait_ge(s_pT, n * ST + qt + 2)
                            pe.wait_ge(s_o, n * ST + qt + 1)
                            for kt in range(ST):
                                mm = nc.tensor.matmul(ps[:, 6, 0:HD], probT[:, kt, :],
                                                      val[:, ds(b * ST + kt, 1), ds(half * P + j * HD, HD)]
                                                      .rearrange("p a n -> p (a n)"),
                                                      start=(kt == 0), stop=(kt == ST - 1))
                            mm.then_inc(s_o_ps, 1)

            with pe.Fori(0, NCHUNK) as c:
                pe.wait_ge(s_attc, c + 2)
                pe.wait_ge(s_xnT, NCHUNK + 2 * c + 1)
                transposes(att_c).then_inc(s_oT_ps, 1)
                pe.wait_ge(s_oT, c + 2)
                pe.wait_ge(s_res2, c + 1)
                for t in range(CT):
                    for k in range(KD):
                        mm = nc.tensor.matmul(ps[:, 2 + t // 2, (t % 2) * D:(t % 2 + 1) * D], oT[:, k, t * P:(t + 1) * P],
                                              wo_sb[:, k, :], start=(k == 0), stop=(k == KD - 1))
                mm.then_inc(s_wo, 1)
                pe.wait_ge(s_xn, NCHUNK + 2 * c + 2)
                transposes(xn).then_inc(s_xnT_ps, 1)
                pe.wait_ge(s_xnT, NCHUNK + 2 * c + 2)
                pe.wait_ge(s_lg, c + 1)
                project(4, xq_sb, xnT).then_inc(s_xq_ps, 1)
                pe.wait_ge(s_xq, KD * c + KD + 1)
                for t in range(CT):
                    pe.wait_ge(s_xsub, CT * c + t + 1)
                    for k in range(KD):
                        mm = nc.tensor.matmul(ps[:, 6 + k, :], xqT[:, k, t * P:(t + 1) * P],
                                              xk_bd[:, ds(c // 2, 1), k, :, :].rearrange("p a h s -> p (a h s)"),
                                              start=True, stop=True)
                    mm.then_inc(s_xs, 1)
                    pe.wait_ge(s_xpn, CT * c + t + 2)
                    pe.wait_ge(s_xpT, CT * c + t + 1)
                    for j in range(HH):
                        mm = nc.tensor.transpose(ps[:, 4 + j // 4, (j % 4) * P:(j % 4 + 1) * P],
                                                 xpn[:, 2 * j:2 * j + 2, :].rearrange("p h s -> p (h s)"), ident[:])
                    mm.then_inc(s_xpT_ps, 1)
                pe.wait_ge(s_xpT, CT * c + CT + 1)
                pe.wait_ge(s_xvc, c + 2)
                pe.wait_ge(s_res, c + 2)
                for j in range(HH):
                    r = 2 * HD * (j % 4)
                    mm = nc.tensor.matmul(ps[r:r + 2 * HD, 2 + j // 4, :], xv_cur[:, j, :], xpT[:, j, :], start=True, stop=True,
                                          tile_position=(0, r))
                mm.then_inc(s_xo_ps, 1)
                pe.wait_ge(s_xo, c + 2)
                for t in range(CT):
                    dst = ps[:, 2 + t // 2, (t % 2) * D:(t % 2 + 1) * D]
                    for k in range(KD):
                        nc.tensor.matmul(dst, oT[:, k, t * P:(t + 1) * P], xproj_sb[:, k, :], start=(k == 0), stop=False)
                    mm = nc.tensor.matmul(dst, ones_row[:], brow[:, 1, :], start=False, stop=True)
                mm.then_inc(s_pj, 1)
                pe.wait_ge(s_xn, NCHUNK + 2 * c + 3)
                transposes(xn).then_inc(s_xnT_ps, 1)
                pe.wait_ge(s_xnT, NCHUNK + 2 * c + 3)
                for t in range(CT):
                    for k in range(KD):
                        mm = nc.tensor.matmul(ps[:, 4, t * E_ROUTED:(t + 1) * E_ROUTED], xnT[:, k, t * P:(t + 1) * P],
                                              wr_sb[:, k, :], start=(k == 0), stop=(k == KD - 1))
                mm.then_inc(s_lg_ps, 1)

            pe.wait_ge(s_lg, NCHUNK + 1)
            pe.wait_ge(s_res2, NCHUNK + 1)
            pe.wait_ge(s_fT, NCHUNK + 1)

            def expert(slot, i):
                w = wcur[:, slot, :]
                with pe.Fori(0, NCHUNK) as c:
                    pe.wait_ge(s_wcur[slot], 48 * (i + 1))
                    n = (2 * i + slot) * NCHUNK + c
                    pe.wait_ge(s_hid, n + 1)
                    for m in range(2):
                        for k in range(KD):
                            mm = nc.tensor.matmul(ps[:, m, :], w[:, (2 * m + k) * F:(2 * m + k + 1) * F],
                                                  fT[:, k, ds(c * CHUNK, CHUNK)], start=(k == 0), stop=(k == KD - 1))
                    mm.then_inc(s_gu, 1)
                    pe.wait_ge(s_hid, n + 2)
                    pe.wait_ge(s_acc, n + 1)
                    for t in range(CT):
                        mm = nc.tensor.matmul(ps[:, 2 + t // 2, (t % 2) * D:(t % 2 + 1) * D], hid[:, t * P:(t + 1) * P],
                                              w[:, 4 * F:], start=True, stop=True)
                    mm.then_inc(s_y, 1)

            with pe.Fori(0, NE // 2) as i:
                for slot in range(2):
                    expert(slot, i)

        @block.scalar
        def _(act):
            for s in (s_std, s_xnT, s_q, s_kv, s_lat, s_k, s_v, s_prob, s_pT, s_oT, s_xq, s_xp, s_xpT, s_xo, s_rexp,
                      s_silu):
                act.sem_inc(s, 1)

            def two_banks(first):
                return ps[:, first:first + 2, :]

            def root(n):
                act.wait_ge(s_var, n + 1)
                nc.scalar.activation(std[:], std[:], ACT.Sqrt).then_inc(s_std, 1)

            with act.Fori(0, NCHUNK) as c:
                root(c + 1)
                act.wait_ge(s_xnT_ps, c + 2)
                act.wait_ge(s_kv_ps, c + 1)
                nc.scalar.copy(xnT[:], two_banks(0)).then_inc(s_xnT, 1)
                act.wait_ge(s_q_ps, c + 2)
                nc.scalar.mul(qT[:, :, ds(c * CHUNK, CHUNK)], two_banks(2), ATTN_SCALE).then_inc(s_q, 1)
                act.wait_ge(s_kv_ps, c + 2)
                act.wait_ge(s_lat_ps, c + 1)
                nc.scalar.copy(kvT[:], two_banks(4)).then_inc(s_kv, 1)
                act.wait_ge(s_lat_ps, c + 2)
                act.wait_ge(s_v_ps, c + 1)
                nc.scalar.copy(latT[:], ps[0:LAT, 6, :]).then_inc(s_lat, 1)
                act.wait_ge(s_k_ps, c + 2)
                nc.scalar.copy(kT[:, :, ds(c * CHUNK, CHUNK)], two_banks(0)).then_inc(s_k, 1)
                act.wait_ge(s_v_ps, c + 2)
                nc.scalar.copy(val[:, ds(c * CT, CT), :].rearrange("p t d -> p (t d)"),
                               two_banks(6).rearrange("p a n -> p (a n)")).then_inc(s_v, 1)

            act.wait_ge(s_decay, 2)
            nc.scalar.activation(decay[:], decay[:], ACT.Exp, scale=-DECAY).then_inc(s_decay, 1)

            act.wait_ge(s_cT_ps, 1)
            nc.scalar.copy(ctxT_hi[:].rearrange("p b s -> p (b s)"), ps[:, 0, 0:B * P]).then_inc(s_cT, 1)
            nc.scalar.copy(ctxT_lo[:].rearrange("p b s -> p (b s)"), ps[0:CD - P, 1, 0:B * P]).then_inc(s_cT, 1)
            act.wait_ge(s_cv_ps, 1)
            act.wait_ge(s_const, 7)
            for r in range(2):
                src = ps[r * CS:(r + 1) * CS, 3, :].rearrange("p (b j r d) -> p b j r d", b=B, r=2, d=HD)
                nc.scalar.copy(xv_bd[r * CS:(r + 1) * CS, :, :, r * HD:(r + 1) * HD], src[:, :, :, r, :]).then_inc(s_cv, 1)

            with act.Fori(0, B * H) as n:
                for qt in range(ST):
                    act.wait_ge(s_nmax, n * ST + qt + 2)
                    act.wait_ge(s_pT_ps, n * ST + qt + 1)
                    act.wait_ge(s_o, (n * ST if qt < 2 else n * ST + qt - 1) + 1)
                    nc.scalar.activation(prob[:], sc_dec[:, qt % 2, :], ACT.Exp, bias=nmax[:, qt:qt + 1],
                                         accum_out=rsum[:, qt:qt + 1]).then_inc(s_prob, 1)
                    act.wait_ge(s_pT_ps, n * ST + qt + 2)
                    act.wait_ge(s_o_ps, n * ST + qt + 1)
                    nc.scalar.copy(probT[:].rearrange("p k q -> p (k q)"), two_banks(4).rearrange("p a n -> p (a n)"))\
                        .then_inc(s_pT, 1)

            with act.Fori(0, NCHUNK) as c:
                act.wait_ge(s_oT_ps, c + 2)
                act.wait_ge(s_pj, c + 1)
                nc.scalar.copy(oT[:], two_banks(0)).then_inc(s_oT, 1)
                root(NCHUNK + 2 * c + 1)
                act.wait_ge(s_xnT_ps, NCHUNK + 2 * c + 2)
                act.wait_ge(s_fT, c + 1)
                act.wait_ge(s_lg_ps, c + 1)
                nc.scalar.copy(xnT[:], two_banks(0)).then_inc(s_xnT, 1)
                act.wait_ge(s_cbd, 1)
                act.wait_ge(s_xq_ps, c + 2)
                for k in range(KD):
                    nc.scalar.activation(xqT[:, k, :], ps[:, 4 + k, :], ACT.Identity, bias=xqb_sb[:, k:k + 1],
                                         scale=X_SCALE).then_inc(s_xq, 1)
                for t in range(CT):
                    act.wait_ge(s_xsub, CT * c + t + 2)
                    act.wait_ge(s_xpn, CT * c + t + 1)
                    nc.scalar.activation(xp[:], xsc[:], ACT.Exp).then_inc(s_xp, 1)
                    act.wait_ge(s_xpT_ps, CT * c + t + 2)
                    act.wait_ge(s_xo_ps, c + 1)
                    nc.scalar.copy(xpT[:, :, t * P:(t + 1) * P],
                                   two_banks(4).rearrange("p a (j q) -> p (a j) q", q=P)).then_inc(s_xpT, 1)
                act.wait_ge(s_xo_ps, c + 2)
                nc.scalar.copy(oT[:], two_banks(2)).then_inc(s_xo, 1)
                root(NCHUNK + 2 * c + 2)
                act.wait_ge(s_xnT_ps, NCHUNK + 2 * c + 3)
                nc.scalar.copy(xnT[:], two_banks(0)).then_inc(s_xnT, 1)
                act.wait_ge(s_rt, 2 * c + 2)
                for t in range(CT):
                    nc.scalar.activation(rexp[:, t, :], logit[:, t, :], ACT.Exp, bias=ntop[:, t:t + 1],
                                         accum_out=resum[:, t:t + 1]).then_inc(s_rexp, 1)

            with act.Fori(0, NE * NCHUNK) as n:
                act.wait_ge(s_gu, n + 2)
                act.wait_ge(s_hid, n + 1)
                nc.scalar.activation(silu[:], ps[:, 0, :], ACT.Silu).then_inc(s_silu, 1)

        @block.vector
        def _(dve):
            for s in (s_ln, s_var, s_xn, s_route, s_rinv, s_o, s_qm, s_clip, s_dec, s_nmax, s_res, s_xmax, s_xsub,
                      s_xsum, s_xinv, s_xpn, s_res2, s_lg, s_rt, s_hid, s_acc):
                dve.sem_inc(s, 1)

            def settled():
                dve.wait_ge(s_const, 7)

            dve.wait_ge(s_w, 16 * NW)
            nc.vector.tensor_tensor(wkv_sb[:], wkv_sb[:], wv_sb[:], ALU.add).then_inc(s_wkv, 1)

            def layer_norm(c, n):
                base = n * 4
                nc.vector.memset(scratch[:], 0.0)
                for t in range(CT):
                    bn = nc.vector.bn_stats(stats[:, t, :], resid[:, ds(c * CT + t, 1), :].rearrange("p a d -> p (a d)"))
                bn.then_inc(s_ln, 1)
                nc.vector.drain()
                for t in range(CT):
                    ag = nc.vector.bn_aggr(mv[:, t, :], stats[:, t, :])
                ag.then_inc(s_ln, 1)
                dve.wait_ge(s_ln, base + 3)
                nc.vector.tensor_scalar(std[:], mv[:, :, 1], EPS, None, ALU.add).then_inc(s_var, 1)
                dve.wait_ge(s_std, n + 2)
                nc.vector.reciprocal(rstd[:], std[:]).then_inc(s_ln, 1)
                dve.wait_ge(s_ln, base + 3 + 1)
                for t in range(CT):
                    nm = nc.vector.tensor_scalar(xn[:, t, :], resid[:, ds(c * CT + t, 1), :].rearrange("p a d -> p (a d)"),
                                                 mv[:, t, 0:1], rstd[:, t:t + 1], ALU.subtract, ALU.mult)
                nm.then_inc(s_ln, 1)
                dve.wait_ge(s_ln, base + 4 + 1)

            with dve.Fori(0, NCHUNK) as c:
                settled()
                dve.wait_ge(s_x, 16 * NCHUNK)
                dve.wait_ge(s_xnT_ps, c + 1)
                layer_norm(c, c)
                nc.vector.tensor_copy(stats[:, 0, 0:1], mv[:, 0, 0:1]).then_inc(s_xn, 1)

            dve.wait_ge(s_const, 7)
            nc.vector.tensor_copy(decay[:], diff_i).then_inc(s_decay, 1)
            nc.vector.tensor_copy(eidx[:], eidx_i[:]).then_inc(s_route, 1)
            dve.wait_ge(s_decay, 1)
            nc.vector.scalar_tensor_tensor(out=decay[:], in0=decay[:], scalar=-1.0, in1=decay[:], op0=ALU.mult,
                                           op1=ALU.max).then_inc(s_decay, 1)

            dve.wait_ge(s_wb, 16 * NWB)
            dve.wait_ge(s_ck_ps, 1)
            for k in range(KD):
                nc.vector.tensor_scalar(xkT[:, k, :, :].rearrange("p b s -> p (b s)"), ps[:, 2, k * P:(k + 1) * P],
                                        xkb_sb[:, k:k + 1], None, ALU.add).then_inc(s_ck, 1)
            dve.wait_ge(s_ck, KD)
            for k in range(KD):
                for j in range(HH):
                    nc.vector.tensor_scalar(xk_bd[:, :, k, j, :], xkT[:, k, :, :], head_mask[:, j:j + 1], None,
                                            ALU.mult).then_inc(s_ck, 1)
            dve.wait_ge(s_cv, 2)
            dve.wait_ge(s_ck, KD + KD * HH)
            nc.vector.tensor_scalar(xqb_sb[:], xqb_sb[:], X_SCALE, None, ALU.mult).then_inc(s_cbd, 1)
            dve.wait_ge(s_decay, 3)
            dve.wait_ge(s_q, NCHUNK + 1)
            dve.wait_ge(s_k, NCHUNK + 1)

            def finish(b, half, j, n, qt):
                dve.wait_ge(s_prob, n * ST + qt + 2)
                nc.vector.reciprocal(rinv[:, qt:qt + 1], rsum[:, qt:qt + 1]).then_inc(s_rinv, 1)
                dve.wait_ge(s_rinv, n * ST + qt + 2)
                dve.wait_ge(s_o_ps, n * ST + qt + 2)
                nc.vector.tensor_scalar(att[:, ds(b * ST + qt, 1), ds(half * P + j * HD, HD)].rearrange("p a n -> p (a n)"),
                                        ps[:, 6, 0:HD], rinv[:, qt:qt + 1], None, ALU.mult).then_inc(s_o, 1)

            with dve.Fori(0, B) as b:
                with dve.Fori(0, KD) as half:
                    with dve.Fori(0, HH) as j:
                        n = b * H + half * HH + j
                        dve.wait_ge(s_sc, n * ST + 1)
                        nc.vector.tensor_scalar(qm[:], qT[:, ds(half, 1), ds(b * S, S)].rearrange("p a n -> p (a n)"),
                                                head_mask[:, ds(j, 1)], None, ALU.mult).then_inc(s_qm, 1)
                        for qt in range(ST):
                            dve.wait_ge(s_sc, n * ST + qt + 2)
                            dve.wait_ge(s_dec, n * ST + qt + 1)
                            nc.vector.tensor_scalar(sc_clip[:], ps[:, 2 * (qt % 2):2 * (qt % 2) + 2, :]
                                                    .rearrange("p a n -> p (a n)"), -CLAMP, CLAMP, ALU.max, ALU.min)\
                                .then_inc(s_clip, 1)
                            settled()
                            dve.wait_ge(s_clip, n * ST + qt + 2)
                            dve.wait_ge(s_prob, (n * ST if qt < 2 else n * ST + qt - 1) + 1)
                            u0 = S - P - qt * P
                            nc.vector.tensor_tensor_reduce(sc_dec[:, qt % 2, :], sc_clip[:], decay[:, u0:u0 + S], 1.0,
                                                           -3.0e38, ALU.mult, ALU.max, rmax[:, qt:qt + 1]).then_inc(s_dec, 1)
                            dve.wait_ge(s_dec, n * ST + qt + 2)
                            nc.vector.tensor_scalar(nmax[:, qt:qt + 1], rmax[:, qt:qt + 1], -1.0, None, ALU.mult)\
                                .then_inc(s_nmax, 1)
                            if qt >= 1:
                                finish(b, half, j, n, qt - 1)
                        finish(b, half, j, n, ST - 1)

            with dve.Fori(0, NCHUNK) as c:
                rc = resid[:, ds(c * CT, CT), :].rearrange("p t d -> p (t d)")
                y = ps[:, 2:4, :].rearrange("p a n -> p (a n)")
                dve.wait_ge(s_wo, c + 2)
                nc.vector.tensor_tensor(rc, rc, y, ALU.add).then_inc(s_res, 1)
                settled()
                dve.wait_ge(s_res, c + 2)
                dve.wait_ge(s_fT, c + 1)
                layer_norm(c, NCHUNK + 2 * c)
                nc.vector.tensor_copy(stats[:, 0, 0:1], mv[:, 0, 0:1]).then_inc(s_xn, 1)
                for t in range(CT):
                    sc = ps[:, 6:8, :].rearrange("p a (h s) -> p (a h) s", s=CS)
                    i = CT * c + t
                    dve.wait_ge(s_xs, i + 2)
                    nc.vector.tensor_reduce(xmax[:], sc, AX_X, ALU.max).then_inc(s_xmax, 1)
                    dve.wait_ge(s_xmax, i + 2)
                    dve.wait_ge(s_xp, i + 1)
                    nc.vector.tensor_tensor(xsc[:], sc, xmax[:].unsqueeze(2).to_broadcast([P, H, CS]), ALU.subtract)\
                        .then_inc(s_xsub, 1)
                    dve.wait_ge(s_xp, i + 2)
                    nc.vector.tensor_reduce(xsum[:], xp[:], AX_X, ALU.add).then_inc(s_xsum, 1)
                    dve.wait_ge(s_xsum, i + 2)
                    nc.vector.reciprocal(xinv[:], xsum[:]).then_inc(s_xinv, 1)
                    dve.wait_ge(s_xinv, i + 2)
                    dve.wait_ge(s_xpT_ps, i + 1)
                    nc.vector.tensor_tensor(xpn[:], xp[:], xinv[:].unsqueeze(2).to_broadcast([P, H, CS]), ALU.mult)\
                        .then_inc(s_xpn, 1)
                dve.wait_ge(s_pj, c + 2)
                nc.vector.tensor_tensor(rc, rc, y, ALU.add).then_inc(s_res2, 1)
                settled()
                dve.wait_ge(s_res2, c + 2)
                layer_norm(c, NCHUNK + 2 * c + 1)
                nc.vector.tensor_copy(stats[:, 0, 0:1], mv[:, 0, 0:1]).then_inc(s_xn, 1)
                dve.wait_ge(s_lg_ps, c + 2)
                nc.vector.tensor_copy(logit[:].rearrange("p t e -> p (t e)"), ps[:, 4, 0:CT * E_ROUTED]).then_inc(s_lg, 1)
                settled()
                dve.wait_ge(s_lg, c + 2)
                for t in range(CT):
                    mx = nc.vector.max(top[:, t, :], logit[:, t, :])
                mx.then_inc(s_route, 1)
                nc.vector.drain()
                for t in range(CT):
                    nc.vector.max_index(topi[:, t, :], top[:, t, :], logit[:, t, :])
                nc.vector.tensor_scalar(ntop[:], top[:, :, 0], -1.0, None, ALU.mult).then_inc(s_rt, 1)
                dve.wait_ge(s_rt, 2 * c + 2)
                nc.vector.tensor_copy(topf[:], topi[:, :, 0:2]).then_inc(s_route, 1)
                dve.wait_ge(s_route, 6 * c + 1 + 3)
                for t in range(CT):
                    for r in range(2):
                        pk = nc.vector.tensor_scalar(pick[:, t, r, :], eidx[:], topf[:, t, r:r + 1], None, ALU.is_equal)
                pk.then_inc(s_route, 1)
                dve.wait_ge(s_route, 6 * c + 1 + 3 + 1)
                nc.vector.tensor_tensor(picked[:], pick[:, :, 0, :], pick[:, :, 1, :], ALU.add).then_inc(s_route, 1)
                dve.wait_ge(s_rexp, CT * c + CT + 1)
                nc.vector.reciprocal(reinv[:], resum[:]).then_inc(s_route, 1)
                dve.wait_ge(s_route, 6 * c + 1 + 5 + 1)
                for t in range(CT):
                    w = nc.vector.scalar_tensor_tensor(
                        out=cw[:, ds(c * CT + t, 1), 0:E_ROUTED].rearrange("p a e -> p (a e)"), in0=rexp[:, t, :],
                        scalar=reinv[:, t:t + 1], in1=picked[:, t, :], op0=ALU.mult, op1=ALU.mult)
                w.then_inc(s_route, 1)
                dve.wait_ge(s_route, 6 * c + 1 + 6 + 1)
                nc.vector.memset(topf[:], 0.0).then_inc(s_rt, 1)

            with dve.Fori(0, NE) as e:
                with dve.Fori(0, NCHUNK) as c:
                    n = e * NCHUNK + c
                    dve.wait_ge(s_silu, n + 2)
                    dve.wait_ge(s_y, n + 1)
                    nc.vector.tensor_tensor(hid[:], silu[:], ps[:, 1, :], ALU.mult).then_inc(s_hid, 1)
                    dve.wait_ge(s_y, n + 2)
                    for t in range(CT):
                        rt = resid[:, ds(c * CT + t, 1), :].rearrange("p a d -> p (a d)")
                        ac = nc.vector.scalar_tensor_tensor(
                            out=rt, in0=ps[:, 2 + t // 2, (t % 2) * D:(t % 2 + 1) * D],
                            scalar=cw[:, ds(c * CT + t, 1), ds(e, 1)].rearrange("p a e -> p (a e)"), in1=rt,
                            op0=ALU.mult, op1=ALU.add)
                    ac.then_inc(s_acc, 1)
                    dve.wait_ge(s_acc, n + 2)


_INS = ["x", "ctx_768", "L0_attn_Wq", "L0_attn_Wk", "L0_attn_Wv", "L0_attn_Wo", "L0_attn_W_down_kv", "L0_attn_W_up_k",
        "L0_attn_W_up_v", "L0_xattn_q_w", "L0_xattn_q_b", "L0_xattn_kv_w", "L0_xattn_kv_b", "L0_xattn_proj_w",
        "L0_xattn_proj_b", "L0_ffn_Wr", "L0_ffn_Wg", "L0_ffn_Wu", "L0_ffn_Wd", "L0_ffn_Sg", "L0_ffn_Su", "L0_ffn_Sd"]
_OUTS = [((B, S, D), "float32")]


def kernel(**inputs):
    import numpy as _np
    import concourse.bacc as _bacc
    from concourse import mybir as _mybir
    from concourse.bass_utils import run_bass_kernel_spmd as _run

    nc = _bacc.Bacc("TRN2", target_bir_lowering=False, num_devices=1)
    arrays, args = {}, []
    for name in _INS:
        a = _np.ascontiguousarray(inputs[name])
        arrays[f"in_{name}_dram"] = a
        args.append(nc.dram_tensor(f"in_{name}_dram", a.shape, _mybir.dt.from_np(a.dtype), kind="ExternalInput").ap())
    for i, (shape, dtype) in enumerate(_OUTS):
        dt = _mybir.dt.from_np(_np.dtype(dtype))
        args.append(nc.dram_tensor(f"out_{i}_dram", shape, dt, kind="ExternalOutput").ap())
    decoder_layer(nc, *args)
    r = _run(nc, [arrays], core_ids=[0])
    return r.results[0]["out_0_dram"]
```

```python
from contextlib import ExitStack

import concourse.bass as bass
from concourse import mybir

ALU = mybir.AluOpType
ACT = mybir.ActivationFunctionType
F32 = mybir.dt.float32
BF16 = mybir.dt.bfloat16
I32 = mybir.dt.int32
U32 = mybir.dt.uint32
AX_X = mybir.AxisListType.X
RMAX = bass.bass_isa.ReduceOp.max
ds = bass.ds

P = 128
B, S, D = 2, 1024, 256
T = B * S
TILES = T // P
CT = 4
CHUNK = CT * P
NCHUNK = T // CHUNK
KD = D // P
H, HD = 16, 16
HH = P // HD
ST = S // P
LAT = 64
CS, CD = 64, 192
E_ROUTED, F = 16, 128
FS = 256
NE = E_ROUTED + FS // F
WCOLS = KD * F * 2 + D
CLAMP = 10000.0
DECAY = 0.01 * 0.01
EPS = 1e-5
ATTN_SCALE = 1.0 / 16.0
X_SCALE = HD ** -0.5
NPART = 3
NPROD = 6
SROWS = NPROD * HD
PRODUCTS = ((0, 0, 0, 1, 1, 2), (0, 1, 2, 0, 1, 0))
NB = 2 * (SROWS // HD)
UNITS = B * KD
SPAN = 72.0
SPAN_LOW = 70.0
VAL_MIN, VAL_MAX = 0.1, 1000.0


def decoder_layer(nc, x, ctx_in, wq, wk, wv, wo, w_down, w_up_k, w_up_v, xq_w, xq_b, xkv_w, xkv_b,
                  xproj_w, xproj_b, wr, wg, wu, wd, sg, su, sd, out):
    with ExitStack() as stack:
        def sb(name, shape, dt=F32):
            return stack.enter_context(nc.sbuf_tensor(name, shape, dt))

        def sem(name):
            return stack.enter_context(nc.semaphore(name))

        ps = stack.enter_context(nc.psum_tensor("ps", [P, 8, 512], F32))

        def bank(i, n=1):
            return ps[:, i:i + n, :]

        resid = sb("resid", [P, TILES, D])
        wq_sb = sb("wq_sb", [P, KD, D])
        wkv_sb = sb("wkv_sb", [P, KD, D])
        xk_bd = sb("xk_bd", [P, B, KD, HH, CS])
        wv_sb = xk_bd[:, 0, 0, :, :].rearrange("p h s -> p (h s)").rearrange("p (k n) -> p k n", k=KD)
        wdown_sb = sb("wdown_sb", [P, KD, LAT])
        wup_sb = sb("wup_sb", [LAT, 2, D])
        wo_sb = sb("wo_sb", [P, KD, D])
        xq_sb = sb("xq_sb", [P, KD, D])
        xqb_sb = sb("xqb_sb", [P, KD])
        xkv_hi = sb("xkv_hi", [P, 2 * D])
        xkv_lo = sb("xkv_lo", [CD - P, 2 * D])
        xkb_sb = sb("xkb_sb", [P, KD])
        brow = sb("brow", [1, 2, D])
        xproj_sb = sb("xproj_sb", [P, KD, D])
        wr_sb = sb("wr_sb", [P, KD, E_ROUTED])
        ident = sb("ident", [P, P])
        ones_row = sb("ones_row", [1, P])
        head_mask = sb("head_mask", [P, HH])
        eidx_i = sb("eidx_i", [P, E_ROUTED], I32)
        eidx = sb("eidx", [P, E_ROUTED])
        scratch = sb("scratch", [P, 1])
        act_scratch = sb("act_scratch", [P, 1])
        stats = sb("stats", [P, CT, 6])
        mv = sb("mv", [P, CT, 2])
        std = sb("std", [P, CT])
        rstd = sb("rstd", [P, CT])
        xn = sb("xn", [P, CT, D])
        xnT = sb("xnT", [P, KD, CHUNK])
        att_c = sb("att_c", [P, CT, D])
        oT = sb("oT", [P, KD, CHUNK])
        grow = [att_c[:].rearrange("p t d -> p (t d)"), oT[:].rearrange("p k q -> p (k q)")]
        wcur = sb("wcur", [P, 2, WCOLS])
        kvT = wcur[:].rearrange("p a n -> p (a n)")[:, 0:KD * CHUNK].rearrange("p (k q) -> p k q", k=KD)
        latT = sb("latT", [LAT, CHUNK])
        qT = sb("qT", [P, KD, T])
        kT = sb("kT", [P, KD, T])
        val = sb("val", [P, TILES, D])
        att = val
        parts = sb("parts", [P, 2, 2, NPART, 2, S], BF16)
        words = parts[:, 0, :, :, :, :].rearrange("p t c v s -> p (t c v s)").bitcast(F32)
        pos_i, within_i = words[:, 0:S].bitcast(I32), words[:, S:S + P].bitcast(I32)
        att_g = words[:, 0:TILES * D].rearrange("p (t d) -> p t d", t=TILES)
        diff_i = words[:, TILES * D:TILES * D + 1920].bitcast(I32)
        spare = parts[:, 1, :, :, :, :].rearrange("p t c v s -> p (t c v s)")
        squares = spare[:, 0:2 * KD * T].rearrange("p (t k n) -> p t k n", t=2, k=KD)
        general = spare.bitcast(F32)
        qm = general[:, 0:S]
        sc_clip = general[:, S:2 * S]
        sc_dec = general[:, 2 * S:4 * S].rearrange("p (a s) -> p a s", a=2)
        prob = general[:, 4 * S:5 * S]
        probT = general[:, 5 * S:6 * S].rearrange("p (k q) -> p k q", q=P)
        qstack = sb("qstack", [SROWS, 2, 2, S], BF16)
        kstack = sb("kstack", [SROWS, 2, 2, S], BF16)
        ftmp = sb("ftmp", [P, 2, 512])
        pT = sb("pT", [P, 2, S])
        decay = pT[:].rearrange("p a s -> p (a s)")[:, 0:1920]
        vcur = sb("vcur", [P, 2, ST, 2 * HD])
        obT = sb("obT", [P, 256])
        rinv8 = sb("rinv8", [P, ST])
        within = sb("within", [P, P])
        head_ind = sb("head_ind", [P, 2 * HD])
        head_ind_bf = sb("head_ind_bf", [P, 2 * HD], BF16)
        ksum = sb("ksum", [P, NCHUNK, KD])
        ksq = sb("ksq", [P, B, KD])
        vsq = pT[:, 1, :]
        red = sb("red", [P, 8])
        reda = sb("reda", [P, 8])
        sums = sb("sums", [P, 2])
        fl = sb("fl", [P, 12])
        shift = sb("shift", [P, 1])
        flag_i = sb("flag_i", [P, 1], I32)
        junk = qstack[0:4 * HD, :, :, :].rearrange("p a v s -> p a (v s)")
        rmax = sb("rmax", [P, ST])
        nmax = sb("nmax", [P, ST])
        rsum = sb("rsum", [P, ST])
        rinv = sb("rinv", [P, ST])
        ctx_sb = sb("ctx_sb", [P, B, CD])
        ctxT_hi = sb("ctxT_hi", [P, B, P])
        ctxT_lo = sb("ctxT_lo", [CD - P, B, P])
        xkT = sb("xkT", [P, KD, B, CS])
        xv_bd = sb("xv_bd", [P, B, HH, 2 * HD])
        xv_cur = sb("xv_cur", [P, HH, 2 * HD])
        spent = words[:, 0:4 * KD * CHUNK].rearrange("p (a n) -> p a n", a=4)
        xqT = spent[:, 0, :].rearrange("p (k q) -> p k q", k=KD)
        xmax = sb("xmax", [P, H])
        xsc = spent[:, 1, :].rearrange("p (h s) -> p h s", s=CS)
        xp = spent[:, 2, :].rearrange("p (h s) -> p h s", s=CS)
        xsum = sb("xsum", [P, H])
        xinv = sb("xinv", [P, H])
        xpn = spent[:, 3, :].rearrange("p (h s) -> p h s", s=CS)
        xpT = kT[:].rearrange("p k (j q) -> p (k j) q", q=CHUNK)
        logit = sb("logit", [P, CT, E_ROUTED])
        top = sb("top", [P, CT, 8])
        topi = sb("topi", [P, CT, 8], U32)
        topf = sb("topf", [P, CT, 2])
        ntop = sb("ntop", [P, CT])
        rexp = sb("rexp", [P, CT, E_ROUTED])
        resum = sb("resum", [P, CT])
        reinv = sb("reinv", [P, CT])
        pick = sb("pick", [P, CT, 2, E_ROUTED])
        picked = sb("picked", [P, CT, E_ROUTED])
        cw = sb("cw", [P, TILES, NE])
        fT = qT
        silu = xn[:].rearrange("p t d -> p (t d)")[:, 0:CHUNK]
        hid = xn[:].rearrange("p t d -> p (t d)")[:, CHUNK:2 * CHUNK]

        s_x = sem("s_x"); s_w = sem("s_w"); s_wb = sem("s_wb"); s_out = sem("s_out")
        s_const = sem("s_const"); s_mask = sem("s_mask"); s_pool = sem("s_pool")
        s_decay = sem("s_decay"); s_wkv = sem("s_wkv")
        s_ln = sem("s_ln"); s_var = sem("s_var"); s_std = sem("s_std"); s_xn = sem("s_xn")
        s_xnT_ps = sem("s_xnT_ps"); s_xnT = sem("s_xnT")
        s_q_ps = sem("s_q_ps"); s_q = sem("s_q"); s_kv_ps = sem("s_kv_ps"); s_kv = sem("s_kv")
        s_lat_ps = sem("s_lat_ps"); s_lat = sem("s_lat"); s_k_ps = sem("s_k_ps"); s_k = sem("s_k")
        s_v_ps = sem("s_v_ps"); s_v = sem("s_v")
        s_qm = sem("s_qm"); s_sc = sem("s_sc"); s_clip = sem("s_clip"); s_dec = sem("s_dec")
        s_nmax = sem("s_nmax"); s_prob = sem("s_prob"); s_pT_ps = sem("s_pT_ps"); s_pT = sem("s_pT")
        s_o_ps = sem("s_o_ps"); s_rinv = sem("s_rinv"); s_o = sem("s_o")
        s_sq = sem("s_sq"); s_vmax = sem("s_vmax"); s_norm_ps = sem("s_norm_ps"); s_sums = sem("s_sums")
        s_red = sem("s_red"); s_reda = sem("s_reda"); s_root = sem("s_root"); s_fl = sem("s_fl"); s_flag = sem("s_flag")
        s_grow = sem("s_grow"); s_split = sem("s_split"); s_split0 = sem("s_split0"); s_parts = sem("s_parts")
        s_parts0 = sem("s_parts0")
        s_stack = [sem("s_stack0"), sem("s_stack1")]
        s_fs = sem("s_fs"); s_diag = sem("s_diag"); s_exp = sem("s_exp"); s_pv = sem("s_pv"); s_vcur = sem("s_vcur")
        s_ob = sem("s_ob"); s_ot = sem("s_ot"); s_on = sem("s_on"); s_att = sem("s_att")
        s_cT_ps = sem("s_cT_ps"); s_cT = sem("s_cT"); s_ck_ps = sem("s_ck_ps"); s_ck = sem("s_ck")
        s_cv_ps = sem("s_cv_ps"); s_cv = sem("s_cv"); s_cbd = sem("s_cbd")
        s_attc = sem("s_attc"); s_xvc = sem("s_xvc"); s_oT_ps = sem("s_oT_ps"); s_oT = sem("s_oT")
        s_wo = sem("s_wo"); s_res = sem("s_res"); s_xq_ps = sem("s_xq_ps"); s_xq = sem("s_xq")
        s_xs = sem("s_xs"); s_xmax = sem("s_xmax"); s_xsub = sem("s_xsub"); s_xp = sem("s_xp")
        s_xsum = sem("s_xsum"); s_xinv = sem("s_xinv"); s_xpn = sem("s_xpn")
        s_xpT_ps = sem("s_xpT_ps"); s_xpT = sem("s_xpT"); s_xo_ps = sem("s_xo_ps"); s_xo = sem("s_xo")
        s_pj = sem("s_pj"); s_res2 = sem("s_res2"); s_fT = sem("s_fT")
        s_lg_ps = sem("s_lg_ps"); s_lg = sem("s_lg"); s_rt = sem("s_rt"); s_route = sem("s_route"); s_rexp = sem("s_rexp")
        s_wcur = [sem("s_wcur0"), sem("s_wcur1")]; s_gu = sem("s_gu"); s_silu = sem("s_silu"); s_hid = sem("s_hid")
        s_y = sem("s_y"); s_acc = sem("s_acc")

        x_d = x.rearrange("b (n p) d -> p (b n) d", p=P)
        out_d = out.rearrange("b (n p) d -> p (b n) d", p=P)
        def split(eng, nceng, step, tmp, buf, u, t, sign, cols):
            b, half = u // KD, u % KD
            src = (qT, kT)[t][:, half, b * S + cols.start:b * S + cols.stop]
            dst = parts[:, buf, t, :, sign, cols]
            step(nceng.tensor_tensor(tmp[:, 0, :], src, grow[sign][:, cols], ALU.mult))
            step(nceng.tensor_copy(dst[:, 0, :], tmp[:, 0, :]))
            step(nceng.tensor_tensor(tmp[:, 1, :], tmp[:, 0, :], dst[:, 0, :], ALU.subtract))
            step(nceng.tensor_copy(dst[:, 1, :], tmp[:, 1, :]))
            return nceng.tensor_tensor(dst[:, 2, :], tmp[:, 1, :], dst[:, 1, :], ALU.subtract)

        def after(eng, semaphore, count):
            if not isinstance(count, int) or count > 0:
                eng.wait_ge(semaphore, count)

        NW = 11
        NWB = 7

        block = stack.enter_context(nc.Block())

        @block.sync
        def _(sp):
            for c in range(NCHUNK):
                sp.dma_start(resid[:, c * CT:(c + 1) * CT, :], x_d[:, c * CT:(c + 1) * CT, :]).then_inc(s_x, 16)
            sp.dma_start(wq_sb[:], wq.rearrange("(k p) n -> p k n", p=P)).then_inc(s_w, 16)
            sp.dma_start(wkv_sb[:], wk.rearrange("(k p) n -> p k n", p=P)).then_inc(s_w, 16)
            sp.dma_start(wv_sb, wv.rearrange("(k p) n -> p k n", p=P)).then_inc(s_w, 16)
            sp.dma_start(wdown_sb[:], w_down.rearrange("(k p) n -> p k n", p=P)).then_inc(s_w, 16)
            sp.dma_start(wup_sb[:, 0, :], w_up_k).then_inc(s_w, 16)
            sp.dma_start(wup_sb[:, 1, :], w_up_v).then_inc(s_w, 16)
            sp.dma_start(wo_sb[:], wo.rearrange("(k p) n -> p k n", p=P)).then_inc(s_w, 16)
            sp.dma_start(xq_sb[:], xq_w.rearrange("(k p) n -> p k n", p=P)).then_inc(s_w, 16)
            sp.dma_start(xproj_sb[:], xproj_w.rearrange("(k p) n -> p k n", p=P)).then_inc(s_w, 16)
            sp.dma_start(xkv_hi[:], xkv_w[0:P, :]).then_inc(s_w, 16)
            sp.dma_start(xkv_lo[:], xkv_w[P:CD, :]).then_inc(s_w, 16)
            for r in range(2):
                sp.dma_start(ctx_sb[r * CS:(r + 1) * CS, :, :], ctx_in.rearrange("b s d -> s b d")).then_inc(s_wb, 16)
            with nc.allow_non_contiguous_dma("biases, one channel to a partition"):
                sp.dma_start(xqb_sb[:], xq_b.rearrange("(k p) -> p k", p=P)).then_inc(s_wb, 16)
                sp.dma_start(xkb_sb[:], xkv_b[0:D].rearrange("(k p) -> p k", p=P)).then_inc(s_wb, 16)
                sp.dma_start(wr_sb[:], wr.rearrange("(k p) n -> p k n", p=P)).then_inc(s_wb, 16)
            sp.dma_start(brow[:, 0, :], xkv_b[D:2 * D].rearrange("(a n) -> a n", a=1)).then_inc(s_wb, 16)
            sp.dma_start(brow[:, 1, :], xproj_b.rearrange("(a n) -> a n", a=1)).then_inc(s_wb, 16)

            def load_expert(slot, gate, up, down):
                sp.dma_start(wcur[:, slot, 0:2 * F].rearrange("p (k f) -> p k f", k=KD), gate).then_inc(s_wcur[slot], 16)
                sp.dma_start(wcur[:, slot, 2 * F:4 * F].rearrange("p (k f) -> p k f", k=KD), up).then_inc(s_wcur[slot], 16)
                sp.dma_start(wcur[:, slot, 4 * F:], down).then_inc(s_wcur[slot], 16)

            def load_routed(slot, e):
                load_expert(slot, *(w[ds(e, 1), :, :].rearrange("a (k p) f -> p (a k) f", p=P) for w in (wg, wu)),
                            wd[ds(e, 1), :, :].rearrange("a f d -> f (a d)"))

            sp.wait_ge(s_flag, 1)
            for slot in range(2):
                load_routed(slot, slot)

            sp.wait_ge(s_flag, 1)
            short = sp.value_load(flag_i[0:1, 0:1], min_val=0, max_val=1)
            with sp.If(short == 1):
                def load_head(u, j):
                    r = j % 2
                    after(sp, s_fs, 2 * ST * (u * HH + j - 1))
                    head = parts[j * HD:(j + 1) * HD, u % 2, :, :, :, :]
                    for t, stk in ((0, qstack), (1, kstack)):
                        for row in range(NPROD):
                            sp.dma_start(stk[row * HD:(row + 1) * HD, r, :, :], head[:, t, PRODUCTS[t][row], :, :])\
                                .then_inc(s_stack[r], 16)

                sp.wait_ge(s_parts0, 1)
                for u in range(UNITS):
                    sp.wait_ge(s_parts, u + 1)
                    for j in range(HH):
                        load_head(u, j)
            with sp.Fori(1, E_ROUTED // 2) as i:
                for slot in range(2):
                    sp.wait_ge(s_y, NCHUNK * (2 * i + slot - 1) + 1)
                    load_routed(slot, 2 * i + slot)
            for slot in range(2):
                sp.wait_ge(s_y, NCHUNK * (E_ROUTED + slot - 1) + 1)
                cols = slice(slot * F, (slot + 1) * F)
                load_expert(slot, *(w[:, cols].rearrange("(k p) f -> p k f", p=P) for w in (sg, su)), sd[cols, :])
            sp.wait_ge(s_acc, NE * NCHUNK + 1)
            sp.dma_start(out_d, resid[:]).then_inc(s_out, 16)
            sp.wait_ge(s_out, 16)

        @block.gpsimd
        def _(pool):
            for s in (s_attc, s_xvc, s_fT):
                pool.sem_inc(s, 1)

            nc.gpsimd.memset(ident[:], 0.0).then_inc(s_pool, 1)
            nc.gpsimd.memset(head_mask[:], 1.0).then_inc(s_pool, 1)
            nc.gpsimd.memset(vcur[:], 0.0).then_inc(s_pool, 1)
            nc.gpsimd.memset(head_ind[:], 0.0).then_inc(s_pool, 1)
            nc.gpsimd.memset(ones_row[:], 1.0).then_inc(s_const, 1)
            nc.gpsimd.memset(xv_bd[:], 0.0).then_inc(s_const, 1)
            nc.gpsimd.memset(cw[:], 1.0).then_inc(s_const, 1)
            pool.wait_ge(s_pool, 4)
            nc.gpsimd.affine_select(out=ident[:], in_=ident[:], compare_op=ALU.not_equal, fill=1.0, base=0,
                                    pattern=[[-1, P]], channel_multiplier=1).then_inc(s_const, 1)
            nc.gpsimd.affine_select(out=head_mask[:], in_=head_mask[:], compare_op=ALU.is_ge, fill=0.0, base=0,
                                    pattern=[[-HD, HH]], channel_multiplier=1).then_inc(s_pool, 1)
            pool.wait_ge(s_pool, 5)
            nc.gpsimd.affine_select(out=head_mask[:], in_=head_mask[:], compare_op=ALU.is_ge, fill=0.0, base=HD - 1,
                                    pattern=[[HD, HH]], channel_multiplier=-1).then_inc(s_const, 1)
            nc.gpsimd.iota(eidx_i[:], pattern=[[1, E_ROUTED]], base=0, channel_multiplier=0).then_inc(s_const, 1)

            nc.gpsimd.iota(pos_i, pattern=[[1, S]], base=0, channel_multiplier=0).then_inc(s_grow, 1)
            nc.gpsimd.iota(within_i, pattern=[[-1, P]], base=0, channel_multiplier=1).then_inc(s_grow, 1)
            nc.gpsimd.memset(vcur[:, :, :, HD:HD + 1], 1.0).then_inc(s_pool, 1)
            pool.wait_ge(s_const, 6)
            nc.gpsimd.tensor_copy(head_ind[:, 0:HH], head_mask[:]).then_inc(s_pool, 1)
            pool.wait_ge(s_pool, 7)
            nc.gpsimd.tensor_copy(head_ind_bf[:], head_ind[:]).then_inc(s_pool, 1)

            for c in range(NCHUNK):
                for t, (src, ready) in enumerate(((qT, s_q), (kT, s_k))):
                    part = src[:, :, c * CHUNK:(c + 1) * CHUNK]
                    pool.wait_ge(ready, c + 2 if t == 0 else KD * (c + 1) + 1)
                    nc.gpsimd.tensor_tensor(squares[:, t, :, c * CHUNK:(c + 1) * CHUNK], part, part, ALU.mult)                        .then_inc(s_sq, 1)
                pool.wait_ge(s_v, c + 2)
                v = val[:, c * CT:(c + 1) * CT, :].rearrange("p t d -> p (t d)")
                fresh = ftmp[:].rearrange("p a n -> p (a n)")
                after(pool, s_vmax, 2 * c - 1)
                nc.gpsimd.tensor_tensor(fresh if c else vsq, v, v, ALU.mult).then_inc(s_vmax, 1)
                if c:
                    pool.wait_ge(s_vmax, 2 * c)
                    nc.gpsimd.tensor_tensor(vsq, vsq, fresh, ALU.add).then_inc(s_vmax, 1)
            pool.wait_ge(s_red, 2)
            nc.gpsimd.partition_all_reduce(reda[:], red[:], P, RMAX).then_inc(s_reda, 1)

            def count(instruction):
                done[0] += 1
                instruction.then_inc(s_split, 1)
                pool.wait_ge(s_split, done[0])

            done = [0]
            pool.wait_ge(s_grow, 5)
            pool.wait_ge(s_vmax, 2 * NCHUNK - 1)
            for sign in range(2):
                for cols in (slice(0, 512), slice(512, S)):
                    count(split(pool, nc.gpsimd, count, ftmp, 0, 0, 1, sign, cols))
            pool.wait_ge(s_flag, 1)
            short = pool.value_load(flag_i[0:1, 0:1], min_val=0, max_val=1)
            with pool.If(short == 1):
                pool.sem_inc(s_parts, 1)
                for u in range(UNITS):
                    for j in range(HH):
                        n = u * HH + j
                        after(pool, s_pv, ST * (n - 1))
                        b, h = n // H, n % H
                        nc.gpsimd.tensor_copy(vcur[:, n % 2, :, 0:HD],
                                              val[:, b * ST:(b + 1) * ST, h * HD:(h + 1) * HD]).then_inc(s_vcur, 1)
                        if u + 1 < UNITS:
                            if j == 0:
                                for r in range(2):
                                    after(pool, s_stack[r], 16 * NB * (HH // 2) * u)
                            t, sign, c = j // 4, j // 2 % 2, j % 2
                            count(split(pool, nc.gpsimd, count, ftmp, (u + 1) % 2, u + 1, t, sign,
                                        slice(512 * c, 512 * (c + 1))))
                            if j == HH - 1:
                                pool.sem_inc(s_parts, 1)

            with pool.If(short == 0):
                pool.wait_ge(s_parts0, 1)
                nc.gpsimd.iota(diff_i, pattern=[[-1, 1920]], base=S - P, channel_multiplier=1).then_inc(s_decay, 1)

            with pool.Fori(0, NCHUNK) as c:
                pool.wait_ge(s_att, 1)
                pool.wait_ge(s_oT_ps, c + 1)
                nc.gpsimd.tensor_copy(att_c[:], att[:, ds(c * CT, CT), :]).then_inc(s_attc, 1)
                pool.wait_ge(s_cbd, 1)
                pool.wait_ge(s_xo_ps, c + 1)
                nc.gpsimd.tensor_copy(xv_cur[:], xv_bd[:, ds(c // 2, 1), :, :].rearrange("p a h n -> p (a h) n"))\
                    .then_inc(s_xvc, 1)
                pool.wait_ge(s_xnT, NCHUNK + 2 * c + 3)
                nc.gpsimd.tensor_copy(fT[:, :, ds(c * CHUNK, CHUNK)], xnT[:]).then_inc(s_fT, 1)

        @block.tensor
        def _(pe):
            for s in (s_xnT_ps, s_q_ps, s_kv_ps, s_lat_ps, s_k_ps, s_v_ps, s_sc, s_pT_ps, s_o_ps, s_oT_ps, s_wo,
                      s_xq_ps, s_xs, s_xpT_ps, s_xo_ps, s_pj, s_lg_ps, s_gu, s_y):
                pe.sem_inc(s, 1)

            def transposes(src):
                for k in range(KD):
                    for t in range(CT):
                        last = nc.tensor.transpose(ps[:, k, t * P:(t + 1) * P], src[:, t, k * P:(k + 1) * P], ident[:])
                return last

            def project(first, w, rhs, rows=P):
                for n in range(KD):
                    for k in range(KD):
                        last = nc.tensor.matmul(ps[0:rows, first + n, :], w[:, k, n * P:n * P + rows], rhs[:, k, :],
                                                start=(k == 0), stop=(k == KD - 1))
                return last

            pe.wait_ge(s_const, 6)
            pe.wait_ge(s_w, 16 * NW)
            pe.wait_ge(s_wkv, 1)

            with pe.Fori(0, NCHUNK) as c:
                pe.wait_ge(s_xn, c + 2)
                pe.wait_ge(s_k, KD * c + 1)
                transposes(xn).then_inc(s_xnT_ps, 1)
                pe.wait_ge(s_xnT, c + 2)
                pe.wait_ge(s_q, c + 1)
                project(2, wq_sb, xnT).then_inc(s_q_ps, 1)
                pe.wait_ge(s_kv, c + 1)
                project(4, wkv_sb, xnT).then_inc(s_kv_ps, 1)
                pe.wait_ge(s_kv, c + 2)
                pe.wait_ge(s_v, c + 1)
                for k in range(KD):
                    mm = nc.tensor.matmul(ps[0:LAT, 6, :], wdown_sb[:, k, :], kvT[:, k, :], start=(k == 0), stop=(k == KD - 1))
                mm.then_inc(s_lat_ps, 1)
                pe.wait_ge(s_lat, c + 2)
                for n in range(KD):
                    mm = nc.tensor.matmul(ps[:, n, :], wup_sb[:, 0, n * P:(n + 1) * P], latT[:], start=True, stop=True)
                mm.then_inc(s_k_ps, 1)
                for t in range(CT):
                    mm = nc.tensor.matmul(ps[:, 6 + t // 2, (t % 2) * D:(t % 2 + 1) * D], latT[:, t * P:(t + 1) * P],
                                          wup_sb[:, 1, :], start=True, stop=True)
                mm.then_inc(s_v_ps, 1)

            pe.wait_ge(s_v, NCHUNK + 1)
            pe.wait_ge(s_q, NCHUNK + 1)
            pe.wait_ge(s_k, KD * NCHUNK + 1)
            pe.wait_ge(s_sq, 2 * NCHUNK)
            pe.wait_ge(s_pool, 8)
            for t in range(2):
                for k in range(KD):
                    r = 2 * HD * k
                    for c in range(NCHUNK):
                        mm = nc.tensor.matmul(ps[r:r + 2 * HD, NCHUNK * t + c, :], head_ind_bf[:],
                                              squares[:, t, k, c * CHUNK:(c + 1) * CHUNK], start=True, stop=True,
                                              tile_position=(0, r))
            mm.then_inc(s_norm_ps, 1)
            pe.wait_ge(s_sums, 2)
            pe.wait_ge(s_fl, 3)
            nc.tensor.matmul(ps[0:2 * HD, 7, 0:B * KD], head_ind[:], ksq[:].rearrange("p b k -> p (b k)"),
                             start=True, stop=True).then_inc(s_norm_ps, 1)

            pe.wait_ge(s_wb, 16 * NWB)
            for b in range(B):
                nc.tensor.transpose(ps[:, 0, b * P:(b + 1) * P], ctx_sb[:, b, 0:P], ident[:])
                mm = nc.tensor.transpose(ps[0:CD - P, 1, b * P:(b + 1) * P], ctx_sb[:, b, P:CD], ident[:])
            mm.then_inc(s_cT_ps, 1)
            pe.wait_ge(s_cT, 2)
            for n in range(KD):
                dst = ps[:, 2, n * P:(n + 1) * P].rearrange("p (b s) -> p b s", b=B)
                nc.tensor.matmul(dst, xkv_hi[:, n * P:(n + 1) * P], ctxT_hi[:, :, 0:CS], start=True, stop=False)
                mm = nc.tensor.matmul(dst, xkv_lo[:, n * P:(n + 1) * P], ctxT_lo[:, :, 0:CS], start=False, stop=True)
            mm.then_inc(s_ck_ps, 1)
            for b in range(B):
                dst = ps[:, 3, b * D:(b + 1) * D]
                nc.tensor.matmul(dst, ctxT_hi[:, b, :], xkv_hi[:, D:], start=True, stop=False)
                nc.tensor.matmul(dst, ctxT_lo[:, b, :], xkv_lo[:, D:], start=False, stop=False)
                mm = nc.tensor.matmul(dst, ones_row[:], brow[:, 0, :], start=False, stop=True)
            mm.then_inc(s_cv_ps, 1)
            pe.wait_ge(s_ck, KD * HH + KD)
            pe.wait_ge(s_cv, 2)

            pe.wait_ge(s_flag, 1)
            short = pe.value_load(flag_i[0:1, 0:1], min_val=0, max_val=1)

            def head_scores(m, kt, r):
                after(pe, s_exp, m - 1)
                first = kt // 4
                for g in (first, 1 - first):
                    lo, hi = 512 * g, 512 * (g + 1)
                    cut = min(max(kt * P, lo), hi)
                    for a, z, sign in ((lo, cut, 0), (cut, hi, 1)):
                        if a < z:
                            mm = nc.tensor.matmul(ps[:, 2 * (kt % 2) + g, a - lo:z - lo],
                                                  kstack[:, r, 1 - sign, kt * P:(kt + 1) * P],
                                                  qstack[:, r, sign, a:z], start=True, stop=True)
                    mm.then_inc(s_fs, 1)

            def weighted(n, m, kt, r):
                pe.wait_ge(s_exp, m + 1)
                if kt == 0:
                    pe.wait_ge(s_vcur, n + 1)
                    after(pe, s_ob, n - 1)
                for g in range(4):
                    mm = nc.tensor.matmul(ps[2 * HD * g:2 * HD * (g + 1), 4 + r, 0:256], vcur[:, r, kt, :],
                                          pT[:, kt % 2, 256 * g:256 * (g + 1)], start=(kt == 0), stop=(kt == ST - 1),
                                          tile_position=(0, 2 * HD * g))
                mm.then_inc(s_pv, 1)

            def out_transposes(n):
                pe.wait_ge(s_ob, n + 1)
                after(pe, s_on, n)
                for c in range(2):
                    mm = nc.tensor.transpose(ps[:, 6, c * P:(c + 1) * P], obT[:, c * P:(c + 1) * P], ident[:])
                mm.then_inc(s_ot, 1)

            def head_steps(i, r, first=False):
                n = 2 * i + r
                for kt in range(ST):
                    m = ST * n + kt
                    if kt == 0:
                        pe.wait_ge(s_stack[r], 16 * NB * (i + 1))
                    head_scores(m, kt, r)
                    if kt >= 2:
                        weighted(n, m - 2, kt - 2, r)
                    elif not first:
                        weighted(n - 1, m - 2, ST - 2 + kt, 1 - r)
                    if kt == 3 and not first:
                        out_transposes(n - 1)

            with pe.If(short == 1):
                head_steps(0, 0, first=True)
                head_steps(0, 1)
                with pe.Fori(1, B * H // 2) as i:
                    head_steps(i, 0)
                    head_steps(i, 1)
                n = B * H - 1
                for kt in (ST - 2, ST - 1):
                    weighted(n, ST * n + kt, kt, 1)
                out_transposes(n)

            def scores(half, b, n, qt):
                pe.wait_ge(s_clip, (n * ST + qt - 1 + 1 if qt == 0 else n * ST + qt - 1) + 1)
                for g in range(2):
                    mm = nc.tensor.matmul(ps[:, 2 * (qt % 2) + g, :], qm[:, qt * P:(qt + 1) * P],
                                          kT[:, ds(half, 1), ds(b * S + g * 512, 512)].rearrange("p a n -> p (a n)"),
                                          start=True, stop=True)
                mm.then_inc(s_sc, 1)

            with pe.If(short == 0):
                with pe.Fori(0, B) as b:
                    with pe.Fori(0, KD) as half:
                        with pe.Fori(0, HH) as j:
                            n = b * H + half * HH + j
                            pe.wait_ge(s_qm, n + 2)
                            scores(half, b, n, 0)
                            for qt in range(ST):
                                if qt + 1 < ST:
                                    scores(half, b, n, qt + 1)
                                pe.wait_ge(s_prob, n * ST + qt + 2)
                                pe.wait_ge(s_pT, n * ST + qt + 1)
                                for kt in range(ST):
                                    mm = nc.tensor.transpose(ps[:, 4 + kt // 4, (kt % 4) * P:(kt % 4 + 1) * P],
                                                             prob[:, kt * P:(kt + 1) * P], ident[:])
                                mm.then_inc(s_pT_ps, 1)
                                pe.wait_ge(s_pT, n * ST + qt + 2)
                                pe.wait_ge(s_o, n * ST + qt + 1)
                                for kt in range(ST):
                                    mm = nc.tensor.matmul(ps[:, 6, 0:HD], probT[:, kt, :],
                                                          val[:, ds(b * ST + kt, 1), ds(half * P + j * HD, HD)]
                                                          .rearrange("p a n -> p (a n)"),
                                                          start=(kt == 0), stop=(kt == ST - 1))
                                mm.then_inc(s_o_ps, 1)

            with pe.Fori(0, NCHUNK) as c:
                pe.wait_ge(s_attc, c + 2)
                pe.wait_ge(s_xnT, NCHUNK + 2 * c + 1)
                transposes(att_c).then_inc(s_oT_ps, 1)
                pe.wait_ge(s_oT, c + 2)
                pe.wait_ge(s_res2, c + 1)
                for t in range(CT):
                    for k in range(KD):
                        mm = nc.tensor.matmul(ps[:, 2 + t // 2, (t % 2) * D:(t % 2 + 1) * D], oT[:, k, t * P:(t + 1) * P],
                                              wo_sb[:, k, :], start=(k == 0), stop=(k == KD - 1))
                mm.then_inc(s_wo, 1)
                pe.wait_ge(s_xn, NCHUNK + 2 * c + 2)
                transposes(xn).then_inc(s_xnT_ps, 1)
                pe.wait_ge(s_xnT, NCHUNK + 2 * c + 2)
                pe.wait_ge(s_lg, c + 1)
                project(4, xq_sb, xnT).then_inc(s_xq_ps, 1)
                pe.wait_ge(s_xq, KD * c + KD + 1)
                for t in range(CT):
                    pe.wait_ge(s_xsub, CT * c + t + 1)
                    for k in range(KD):
                        mm = nc.tensor.matmul(ps[:, 6 + k, :], xqT[:, k, t * P:(t + 1) * P],
                                              xk_bd[:, ds(c // 2, 1), k, :, :].rearrange("p a h s -> p (a h s)"),
                                              start=True, stop=True)
                    mm.then_inc(s_xs, 1)
                    pe.wait_ge(s_xpn, CT * c + t + 2)
                    pe.wait_ge(s_xpT, CT * c + t + 1)
                    for j in range(HH):
                        mm = nc.tensor.transpose(ps[:, 4 + j // 4, (j % 4) * P:(j % 4 + 1) * P],
                                                 xpn[:, 2 * j:2 * j + 2, :].rearrange("p h s -> p (h s)"), ident[:])
                    mm.then_inc(s_xpT_ps, 1)
                pe.wait_ge(s_xpT, CT * c + CT + 1)
                pe.wait_ge(s_xvc, c + 2)
                pe.wait_ge(s_res, c + 2)
                for j in range(HH):
                    r = 2 * HD * (j % 4)
                    mm = nc.tensor.matmul(ps[r:r + 2 * HD, 2 + j // 4, :], xv_cur[:, j, :], xpT[:, j, :], start=True, stop=True,
                                          tile_position=(0, r))
                mm.then_inc(s_xo_ps, 1)
                pe.wait_ge(s_xo, c + 2)
                for t in range(CT):
                    dst = ps[:, 2 + t // 2, (t % 2) * D:(t % 2 + 1) * D]
                    for k in range(KD):
                        nc.tensor.matmul(dst, oT[:, k, t * P:(t + 1) * P], xproj_sb[:, k, :], start=(k == 0), stop=False)
                    mm = nc.tensor.matmul(dst, ones_row[:], brow[:, 1, :], start=False, stop=True)
                mm.then_inc(s_pj, 1)
                pe.wait_ge(s_xn, NCHUNK + 2 * c + 3)
                transposes(xn).then_inc(s_xnT_ps, 1)
                pe.wait_ge(s_xnT, NCHUNK + 2 * c + 3)
                for t in range(CT):
                    for k in range(KD):
                        mm = nc.tensor.matmul(ps[:, 4, t * E_ROUTED:(t + 1) * E_ROUTED], xnT[:, k, t * P:(t + 1) * P],
                                              wr_sb[:, k, :], start=(k == 0), stop=(k == KD - 1))
                mm.then_inc(s_lg_ps, 1)

            pe.wait_ge(s_lg, NCHUNK + 1)
            pe.wait_ge(s_res2, NCHUNK + 1)
            pe.wait_ge(s_fT, NCHUNK + 1)

            def expert(slot, i):
                w = wcur[:, slot, :]
                with pe.Fori(0, NCHUNK) as c:
                    pe.wait_ge(s_wcur[slot], 48 * (i + 1))
                    n = (2 * i + slot) * NCHUNK + c
                    pe.wait_ge(s_hid, n + 1)
                    for m in range(2):
                        for k in range(KD):
                            mm = nc.tensor.matmul(ps[:, m, :], w[:, (2 * m + k) * F:(2 * m + k + 1) * F],
                                                  fT[:, k, ds(c * CHUNK, CHUNK)], start=(k == 0), stop=(k == KD - 1))
                    mm.then_inc(s_gu, 1)
                    pe.wait_ge(s_hid, n + 2)
                    pe.wait_ge(s_acc, n + 1)
                    for t in range(CT):
                        mm = nc.tensor.matmul(ps[:, 2 + t // 2, (t % 2) * D:(t % 2 + 1) * D], hid[:, t * P:(t + 1) * P],
                                              w[:, 4 * F:], start=True, stop=True)
                    mm.then_inc(s_y, 1)

            with pe.Fori(0, NE // 2) as i:
                for slot in range(2):
                    expert(slot, i)

        @block.scalar
        def _(act):
            for s in (s_std, s_xnT, s_q, s_kv, s_lat, s_k, s_v, s_prob, s_pT, s_oT, s_xq, s_xp, s_xpT, s_xo, s_rexp,
                      s_silu):
                act.sem_inc(s, 1)

            def two_banks(first):
                return ps[:, first:first + 2, :]

            def root(n):
                act.wait_ge(s_var, n + 1)
                nc.scalar.activation(std[:], std[:], ACT.Sqrt).then_inc(s_std, 1)

            act.wait_ge(s_pool, 8)
            nc.scalar.activation(act_scratch[:], head_ind[:, 0:1], ACT.Sqrt)
            with act.Fori(0, NCHUNK) as c:
                root(c + 1)
                act.wait_ge(s_xnT_ps, c + 2)
                act.wait_ge(s_kv_ps, c + 1)
                nc.scalar.copy(xnT[:], two_banks(0)).then_inc(s_xnT, 1)
                act.wait_ge(s_q_ps, c + 2)
                nc.scalar.mul(qT[:, :, ds(c * CHUNK, CHUNK)], two_banks(2), ATTN_SCALE).then_inc(s_q, 1)
                act.wait_ge(s_kv_ps, c + 2)
                act.wait_ge(s_lat_ps, c + 1)
                nc.scalar.copy(kvT, two_banks(4)).then_inc(s_kv, 1)
                act.wait_ge(s_lat_ps, c + 2)
                act.wait_ge(s_v_ps, c + 1)
                nc.scalar.copy(latT[:], ps[0:LAT, 6, :]).then_inc(s_lat, 1)
                act.wait_ge(s_k_ps, c + 2)
                for k in range(KD):
                    nc.scalar.activation(kT[:, k, ds(c * CHUNK, CHUNK)], ps[:, k, :], ACT.Identity,
                                         accum_out=ksum[:, ds(c, 1), k:k + 1].rearrange("p a k -> p (a k)")).then_inc(s_k, 1)
                act.wait_ge(s_v_ps, c + 2)
                nc.scalar.copy(val[:, ds(c * CT, CT), :].rearrange("p t d -> p (t d)"),
                               two_banks(6).rearrange("p a n -> p (a n)")).then_inc(s_v, 1)

            act.wait_ge(s_norm_ps, 1)
            for t in (1, 0):
                if t == 0:
                    act.wait_ge(s_fl, 2)
                nc.scalar.activation(junk[:, t, :], ps[0:4 * HD, NCHUNK * t:NCHUNK * (t + 1), :].rearrange("p c n -> p (c n)"),
                                     ACT.Identity, accum_out=sums[0:4 * HD, t:t + 1]).then_inc(s_sums, 1)

            act.wait_ge(s_grow, 4)
            nc.scalar.activation(grow[0], pT[:, 0, :], ACT.Exp, scale=DECAY).then_inc(s_root, 1)
            nc.scalar.activation(grow[1], pT[:, 0, :], ACT.Exp, scale=-DECAY).then_inc(s_root, 1)
            nc.scalar.activation(within[:], within[:], ACT.Exp, scale=-2 * DECAY).then_inc(s_grow, 1)

            act.wait_ge(s_cT_ps, 1)
            nc.scalar.copy(ctxT_hi[:].rearrange("p b s -> p (b s)"), ps[:, 0, 0:B * P]).then_inc(s_cT, 1)
            nc.scalar.copy(ctxT_lo[:].rearrange("p b s -> p (b s)"), ps[0:CD - P, 1, 0:B * P]).then_inc(s_cT, 1)
            act.wait_ge(s_cv_ps, 1)
            act.wait_ge(s_const, 6)
            for r in range(2):
                src = ps[r * CS:(r + 1) * CS, 3, :].rearrange("p (b j r d) -> p b j r d", b=B, r=2, d=HD)
                nc.scalar.copy(xv_bd[r * CS:(r + 1) * CS, :, :, r * HD:(r + 1) * HD], src[:, :, :, r, :]).then_inc(s_cv, 1)

            act.wait_ge(s_fl, 5)
            nc.scalar.activation(fl[:, 2:4], fl[:, 0:2], ACT.Sqrt).then_inc(s_root, 1)
            act.wait_ge(s_flag, 1)
            short = act.value_load(flag_i[0:1, 0:1], min_val=0, max_val=1)

            def step_exp(m, kt):
                act.wait_ge(s_fs, 2 * m + 2)
                act.wait_ge(s_diag, m + 1)
                after(act, s_pv, m - 1)
                nc.scalar.activation(pT[:, kt % 2, :], two_banks(2 * (kt % 2)).rearrange("p a n -> p (a n)"), ACT.Exp,
                                     bias=shift[:]).then_inc(s_exp, 1)

            with act.If(short == 1):
                for m in range(ST):
                    step_exp(m, m)
                with act.Fori(1, B * H) as n:
                    for kt in range(ST):
                        step_exp(ST * n + kt, kt)

            with act.If(short == 0):
                act.wait_ge(s_decay, 3)
                nc.scalar.activation(decay, decay, ACT.Exp, scale=-DECAY).then_inc(s_decay, 1)

                with act.Fori(0, B * H) as n:
                    for qt in range(ST):
                        act.wait_ge(s_nmax, n * ST + qt + 2)
                        act.wait_ge(s_pT_ps, n * ST + qt + 1)
                        act.wait_ge(s_o, (n * ST if qt < 2 else n * ST + qt - 1) + 1)
                        nc.scalar.activation(prob, sc_dec[:, qt % 2, :], ACT.Exp, bias=nmax[:, qt:qt + 1],
                                             accum_out=rsum[:, qt:qt + 1]).then_inc(s_prob, 1)
                        act.wait_ge(s_pT_ps, n * ST + qt + 2)
                        act.wait_ge(s_o_ps, n * ST + qt + 1)
                        nc.scalar.copy(probT.rearrange("p k q -> p (k q)"), two_banks(4).rearrange("p a n -> p (a n)"))\
                            .then_inc(s_pT, 1)

            with act.Fori(0, NCHUNK) as c:
                act.wait_ge(s_oT_ps, c + 2)
                act.wait_ge(s_pj, c + 1)
                nc.scalar.copy(oT[:], two_banks(0)).then_inc(s_oT, 1)
                root(NCHUNK + 2 * c + 1)
                act.wait_ge(s_xnT_ps, NCHUNK + 2 * c + 2)
                act.wait_ge(s_fT, c + 1)
                act.wait_ge(s_lg_ps, c + 1)
                nc.scalar.copy(xnT[:], two_banks(0)).then_inc(s_xnT, 1)
                act.wait_ge(s_cbd, 1)
                act.wait_ge(s_xq_ps, c + 2)
                for k in range(KD):
                    nc.scalar.activation(xqT[:, k, :], ps[:, 4 + k, :], ACT.Identity, bias=xqb_sb[:, k:k + 1],
                                         scale=X_SCALE).then_inc(s_xq, 1)
                for t in range(CT):
                    act.wait_ge(s_xsub, CT * c + t + 2)
                    act.wait_ge(s_xpn, CT * c + t + 1)
                    nc.scalar.activation(xp[:], xsc[:], ACT.Exp).then_inc(s_xp, 1)
                    act.wait_ge(s_xpT_ps, CT * c + t + 2)
                    act.wait_ge(s_xo_ps, c + 1)
                    nc.scalar.copy(xpT[:, :, t * P:(t + 1) * P],
                                   two_banks(4).rearrange("p a (j q) -> p (a j) q", q=P)).then_inc(s_xpT, 1)
                act.wait_ge(s_xo_ps, c + 2)
                nc.scalar.copy(oT[:], two_banks(2)).then_inc(s_xo, 1)
                root(NCHUNK + 2 * c + 2)
                act.wait_ge(s_xnT_ps, NCHUNK + 2 * c + 3)
                nc.scalar.copy(xnT[:], two_banks(0)).then_inc(s_xnT, 1)
                act.wait_ge(s_rt, 2 * c + 2)
                for t in range(CT):
                    nc.scalar.activation(rexp[:, t, :], logit[:, t, :], ACT.Exp, bias=ntop[:, t:t + 1],
                                         accum_out=resum[:, t:t + 1]).then_inc(s_rexp, 1)

            act.wait_ge(s_pool, 8)
            nc.scalar.activation(act_scratch[:], head_ind[:, 0:1], ACT.Silu)
            with act.Fori(0, NE * NCHUNK) as n:
                act.wait_ge(s_gu, n + 2)
                act.wait_ge(s_hid, n + 1)
                nc.scalar.activation(silu, ps[:, 0, :], ACT.Silu).then_inc(s_silu, 1)

        @block.vector
        def _(dve):
            for s in (s_ln, s_var, s_xn, s_route, s_rinv, s_o, s_qm, s_clip, s_dec, s_nmax, s_res, s_xmax, s_xsub,
                      s_xsum, s_xinv, s_xpn, s_res2, s_lg, s_rt, s_hid, s_acc):
                dve.sem_inc(s, 1)

            def settled():
                dve.wait_ge(s_const, 6)

            dve.wait_ge(s_w, 16 * NW)
            nc.vector.tensor_tensor(wkv_sb[:], wkv_sb[:], wv_sb, ALU.add).then_inc(s_wkv, 1)

            def layer_norm(c, n):
                base = n * 4
                nc.vector.memset(scratch[:], 0.0)
                for t in range(CT):
                    bn = nc.vector.bn_stats(stats[:, t, :], resid[:, ds(c * CT + t, 1), :].rearrange("p a d -> p (a d)"))
                bn.then_inc(s_ln, 1)
                nc.vector.drain()
                for t in range(CT):
                    ag = nc.vector.bn_aggr(mv[:, t, :], stats[:, t, :])
                ag.then_inc(s_ln, 1)
                dve.wait_ge(s_ln, base + 3)
                nc.vector.tensor_scalar(std[:], mv[:, :, 1], EPS, None, ALU.add).then_inc(s_var, 1)
                dve.wait_ge(s_std, n + 2)
                nc.vector.reciprocal(rstd[:], std[:]).then_inc(s_ln, 1)
                dve.wait_ge(s_ln, base + 3 + 1)
                for t in range(CT):
                    nm = nc.vector.tensor_scalar(xn[:, t, :], resid[:, ds(c * CT + t, 1), :].rearrange("p a d -> p (a d)"),
                                                 mv[:, t, 0:1], rstd[:, t:t + 1], ALU.subtract, ALU.mult)
                nm.then_inc(s_ln, 1)
                dve.wait_ge(s_ln, base + 4 + 1)

            with dve.Fori(0, NCHUNK) as c:
                settled()
                dve.wait_ge(s_x, 16 * NCHUNK)
                dve.wait_ge(s_xnT_ps, c + 1)
                layer_norm(c, c)
                nc.vector.tensor_copy(stats[:, 0, 0:1], mv[:, 0, 0:1]).then_inc(s_xn, 1)

            dve.wait_ge(s_grow, 2)
            nc.vector.tensor_copy(pT[:, 0, :], pos_i).then_inc(s_grow, 1)
            nc.vector.tensor_copy(within[:], within_i)
            nc.vector.drain()
            nc.vector.tensor_scalar(within[:], within[:], 0.0, None, ALU.max).then_inc(s_grow, 1)

            nc.vector.memset(red[:], 0.0)
            dve.wait_ge(s_k, KD * NCHUNK + 1)
            for b in range(B):
                nc.vector.tensor_tensor(ksq[:, b, :], ksum[:, 2 * b, :], ksum[:, 2 * b + 1, :], ALU.add)
            dve.wait_ge(s_vmax, 2 * NCHUNK - 1)
            nc.vector.drain()
            nc.vector.tensor_tensor(ksq[:], ksq[:], ksq[:], ALU.mult).then_inc(s_fl, 1)
            nc.vector.tensor_reduce(red[:, 4:5], vsq, AX_X, ALU.max)
            dve.wait_ge(s_norm_ps, 1)
            for t in range(2):
                after(dve, s_sums, t)
                nc.vector.tensor_reduce(red[0:4 * HD, t:t + 1],
                                        ps[0:4 * HD, NCHUNK * t:NCHUNK * (t + 1), :].rearrange("p c n -> p (c n)"),
                                        AX_X, ALU.max).then_inc(s_fl, 1)
            dve.wait_ge(s_sums, 2)
            nc.vector.tensor_scalar(sums[0:4 * HD, :], sums[0:4 * HD, :], 1e37, -1.0, ALU.is_le, ALU.mult)
            nc.vector.drain()
            nc.vector.tensor_scalar(red[0:4 * HD, 5:7], sums[0:4 * HD, :], 1.0, None, ALU.add).then_inc(s_red, 1)
            dve.wait_ge(s_norm_ps, 2)
            nc.vector.tensor_reduce(red[0:2 * HD, 3:4], ps[0:2 * HD, 7, 0:B * KD], AX_X, ALU.max).then_inc(s_red, 1)
            dve.wait_ge(s_reda, 1)
            nc.vector.tensor_tensor(fl[:, 0:1], reda[:, 0:1], reda[:, 1:2], ALU.mult)
            nc.vector.tensor_tensor(fl[:, 1:2], reda[:, 0:1], reda[:, 3:4], ALU.mult)
            nc.vector.drain()
            nc.vector.tensor_scalar(fl[:, 1:2], fl[:, 1:2], 1.0 / S / S, None, ALU.mult)
            nc.vector.drain()
            nc.vector.tensor_scalar(fl[:, 0:2], fl[:, 0:2], 1.02, 1e-30, ALU.mult, ALU.max)
            nc.vector.drain()
            nc.vector.tensor_scalar(fl[:, 0:2], fl[:, 0:2], 1e30, None, ALU.min).then_inc(s_fl, 1)
            dve.wait_ge(s_fl, 4)
            nc.vector.memset(fl[:, 8:9], 0.0).then_inc(s_fl, 1)
            dve.wait_ge(s_root, 3)
            nc.vector.tensor_scalar(fl[:, 4:5], fl[:, 2:3], -SPAN, 0.0, ALU.add, ALU.max)
            nc.vector.tensor_scalar(fl[:, 5:6], reda[:, 4:5], NCHUNK * VAL_MIN ** 2, None, ALU.is_ge)
            nc.vector.tensor_scalar(fl[:, 6:7], reda[:, 4:5], VAL_MAX ** 2, None, ALU.is_le)
            nc.vector.tensor_tensor(fl[:, 7:8], reda[:, 5:6], reda[:, 6:7], ALU.max)
            nc.vector.drain()
            nc.vector.tensor_tensor(fl[:, 3:4], fl[:, 4:5], fl[:, 3:4], ALU.add)
            nc.vector.tensor_scalar(shift[:], fl[:, 4:5], -1.0, None, ALU.mult)
            nc.vector.tensor_scalar(fl[:, 7:8], fl[:, 7:8], 0.5, None, ALU.is_le)
            nc.vector.tensor_tensor(fl[:, 5:6], fl[:, 5:6], fl[:, 6:7], ALU.mult)
            nc.vector.drain()
            nc.vector.tensor_scalar(fl[:, 3:4], fl[:, 3:4], SPAN_LOW, None, ALU.is_le)
            nc.vector.tensor_tensor(fl[:, 5:6], fl[:, 5:6], fl[:, 7:8], ALU.mult)
            nc.vector.drain()
            nc.vector.tensor_tensor(fl[:, 3:4], fl[:, 3:4], fl[:, 5:6], ALU.mult)
            nc.vector.drain()
            nc.vector.tensor_copy(flag_i[:], fl[:, 3:4]).then_inc(s_flag, 1)

            def count(instruction):
                done[0] += 1
                instruction.then_inc(s_split0, 1)
                dve.wait_ge(s_split0, done[0])

            done = [0]
            dve.wait_ge(s_grow, 5)
            for sign in range(2):
                for cols in (slice(0, 512), slice(512, S)):
                    tmp = pT[:, 1, :].rearrange("p (a n) -> p a n", a=2)
                    count(split(dve, nc.vector, count, tmp, 0, 0, 0, sign, cols))
            nc.vector.memset(fl[:, 8:9], 0.0).then_inc(s_parts0, 1)

            dve.wait_ge(s_const, 6)
            nc.vector.tensor_copy(eidx[:], eidx_i[:]).then_inc(s_route, 1)

            dve.wait_ge(s_wb, 16 * NWB)
            dve.wait_ge(s_ck_ps, 1)
            for k in range(KD):
                nc.vector.tensor_scalar(xkT[:, k, :, :].rearrange("p b s -> p (b s)"), ps[:, 2, k * P:(k + 1) * P],
                                        xkb_sb[:, k:k + 1], None, ALU.add).then_inc(s_ck, 1)
            dve.wait_ge(s_ck, KD)
            for k in range(KD):
                for j in range(HH):
                    nc.vector.tensor_scalar(xk_bd[:, :, k, j, :], xkT[:, k, :, :], head_mask[:, j:j + 1], None,
                                            ALU.mult).then_inc(s_ck, 1)
            dve.wait_ge(s_cv, 2)
            dve.wait_ge(s_ck, KD + KD * HH)
            nc.vector.tensor_scalar(xqb_sb[:], xqb_sb[:], X_SCALE, None, ALU.mult).then_inc(s_cbd, 1)
            dve.wait_ge(s_q, NCHUNK + 1)
            dve.wait_ge(s_k, KD * NCHUNK + 1)
            dve.wait_ge(s_flag, 1)
            short = dve.value_load(flag_i[0:1, 0:1], min_val=0, max_val=1)

            def diagonal(m, kt):
                dve.wait_ge(s_fs, 2 * m + 1)
                blk = ps[:, 2 * (kt % 2) + kt // 4, (kt % 4) * P:(kt % 4 + 1) * P]
                nc.vector.tensor_tensor(blk, blk, within[:], ALU.mult).then_inc(s_diag, 1)

            def read_out(n, r):
                dve.wait_ge(s_pv, ST * (n + 1))
                after(dve, s_ot, n)
                nc.vector.tensor_copy(obT[:], ps[:, 4 + r, 0:256]).then_inc(s_ob, 1)

            def normalise(n):
                dve.wait_ge(s_ot, n + 1)
                o = ps[:, 6, 0:256].rearrange("p (c g d) -> p g c d", c=2, g=4)
                nc.vector.reciprocal(rinv8[:].rearrange("p (g c) -> p g c", c=2), o[:, :, :, HD])
                nc.vector.drain()
                nc.vector.tensor_tensor(att[:, ds(n // H * ST, ST), ds(n % H * HD, HD)].rearrange("p (g c) d -> p g c d", c=2),
                                        o[:, :, :, 0:HD],
                                        rinv8[:].rearrange("p (g c) -> p g c", c=2).unsqueeze(3).to_broadcast([P, 4, 2, HD]),
                                        ALU.mult).then_inc(s_on, 1)

            def head_steps(n, r, first=False):
                for kt in range(ST):
                    diagonal(ST * n + kt, kt)
                    if kt == 2 and not first:
                        read_out(n - 1, 1 - r)
                    if kt == 4 and not first:
                        normalise(n - 1)

            with dve.If(short == 1):
                head_steps(0, 0, first=True)
                head_steps(1, 1)
                with dve.Fori(1, B * H // 2) as i:
                    head_steps(2 * i, 0)
                    head_steps(2 * i + 1, 1)
                read_out(B * H - 1, 1)
                normalise(B * H - 1)

            def finish(b, half, j, n, qt):
                dve.wait_ge(s_prob, n * ST + qt + 2)
                nc.vector.reciprocal(rinv[:, qt:qt + 1], rsum[:, qt:qt + 1]).then_inc(s_rinv, 1)
                dve.wait_ge(s_rinv, n * ST + qt + 2)
                dve.wait_ge(s_o_ps, n * ST + qt + 2)
                nc.vector.tensor_scalar(att_g[:, ds(b * ST + qt, 1), ds(half * P + j * HD, HD)].rearrange("p a n -> p (a n)"),
                                        ps[:, 6, 0:HD], rinv[:, qt:qt + 1], None, ALU.mult).then_inc(s_o, 1)

            with dve.If(short == 0):
                dve.wait_ge(s_decay, 1)
                nc.vector.tensor_copy(decay, diff_i).then_inc(s_decay, 1)
                dve.wait_ge(s_decay, 2)
                nc.vector.scalar_tensor_tensor(out=decay, in0=decay, scalar=-1.0, in1=decay, op0=ALU.mult,
                                               op1=ALU.max).then_inc(s_decay, 1)
                dve.wait_ge(s_decay, 4)
                with dve.Fori(0, B) as b:
                    with dve.Fori(0, KD) as half:
                        with dve.Fori(0, HH) as j:
                            n = b * H + half * HH + j
                            dve.wait_ge(s_sc, n * ST + 1)
                            nc.vector.tensor_scalar(qm, qT[:, ds(half, 1), ds(b * S, S)].rearrange("p a n -> p (a n)"),
                                                    head_mask[:, ds(j, 1)], None, ALU.mult).then_inc(s_qm, 1)
                            for qt in range(ST):
                                dve.wait_ge(s_sc, n * ST + qt + 2)
                                dve.wait_ge(s_dec, n * ST + qt + 1)
                                nc.vector.tensor_scalar(sc_clip, ps[:, 2 * (qt % 2):2 * (qt % 2) + 2, :]
                                                        .rearrange("p a n -> p (a n)"), -CLAMP, CLAMP, ALU.max, ALU.min)\
                                    .then_inc(s_clip, 1)
                                settled()
                                dve.wait_ge(s_clip, n * ST + qt + 2)
                                dve.wait_ge(s_prob, (n * ST if qt < 2 else n * ST + qt - 1) + 1)
                                u0 = S - P - qt * P
                                nc.vector.tensor_tensor_reduce(sc_dec[:, qt % 2, :], sc_clip, decay[:, u0:u0 + S], 1.0,
                                                               -3.0e38, ALU.mult, ALU.max, rmax[:, qt:qt + 1]).then_inc(s_dec, 1)
                                dve.wait_ge(s_dec, n * ST + qt + 2)
                                nc.vector.tensor_scalar(nmax[:, qt:qt + 1], rmax[:, qt:qt + 1], -1.0, None, ALU.mult)\
                                    .then_inc(s_nmax, 1)
                                if qt >= 1:
                                    finish(b, half, j, n, qt - 1)
                            finish(b, half, j, n, ST - 1)
                nc.vector.drain()
                nc.vector.tensor_copy(att[:], att_g)
            nc.vector.drain()
            nc.vector.memset(fl[:, 8:9], 0.0).then_inc(s_att, 1)

            with dve.Fori(0, NCHUNK) as c:
                rc = resid[:, ds(c * CT, CT), :].rearrange("p t d -> p (t d)")
                y = ps[:, 2:4, :].rearrange("p a n -> p (a n)")
                dve.wait_ge(s_wo, c + 2)
                nc.vector.tensor_tensor(rc, rc, y, ALU.add).then_inc(s_res, 1)
                settled()
                dve.wait_ge(s_res, c + 2)
                dve.wait_ge(s_fT, c + 1)
                layer_norm(c, NCHUNK + 2 * c)
                nc.vector.tensor_copy(stats[:, 0, 0:1], mv[:, 0, 0:1]).then_inc(s_xn, 1)
                for t in range(CT):
                    sc = ps[:, 6:8, :].rearrange("p a (h s) -> p (a h) s", s=CS)
                    i = CT * c + t
                    dve.wait_ge(s_xs, i + 2)
                    nc.vector.tensor_reduce(xmax[:], sc, AX_X, ALU.max).then_inc(s_xmax, 1)
                    dve.wait_ge(s_xmax, i + 2)
                    dve.wait_ge(s_xp, i + 1)
                    nc.vector.tensor_tensor(xsc[:], sc, xmax[:].unsqueeze(2).to_broadcast([P, H, CS]), ALU.subtract)\
                        .then_inc(s_xsub, 1)
                    dve.wait_ge(s_xp, i + 2)
                    nc.vector.tensor_reduce(xsum[:], xp[:], AX_X, ALU.add).then_inc(s_xsum, 1)
                    dve.wait_ge(s_xsum, i + 2)
                    nc.vector.reciprocal(xinv[:], xsum[:]).then_inc(s_xinv, 1)
                    dve.wait_ge(s_xinv, i + 2)
                    dve.wait_ge(s_xpT_ps, i + 1)
                    nc.vector.tensor_tensor(xpn[:], xp[:], xinv[:].unsqueeze(2).to_broadcast([P, H, CS]), ALU.mult)\
                        .then_inc(s_xpn, 1)
                dve.wait_ge(s_pj, c + 2)
                nc.vector.tensor_tensor(rc, rc, y, ALU.add).then_inc(s_res2, 1)
                settled()
                dve.wait_ge(s_res2, c + 2)
                layer_norm(c, NCHUNK + 2 * c + 1)
                nc.vector.tensor_copy(stats[:, 0, 0:1], mv[:, 0, 0:1]).then_inc(s_xn, 1)
                dve.wait_ge(s_lg_ps, c + 2)
                nc.vector.tensor_copy(logit[:].rearrange("p t e -> p (t e)"), ps[:, 4, 0:CT * E_ROUTED]).then_inc(s_lg, 1)
                settled()
                dve.wait_ge(s_lg, c + 2)
                for t in range(CT):
                    mx = nc.vector.max(top[:, t, :], logit[:, t, :])
                mx.then_inc(s_route, 1)
                nc.vector.drain()
                for t in range(CT):
                    nc.vector.max_index(topi[:, t, :], top[:, t, :], logit[:, t, :])
                nc.vector.tensor_scalar(ntop[:], top[:, :, 0], -1.0, None, ALU.mult).then_inc(s_rt, 1)
                dve.wait_ge(s_rt, 2 * c + 2)
                nc.vector.tensor_copy(topf[:], topi[:, :, 0:2]).then_inc(s_route, 1)
                dve.wait_ge(s_route, 6 * c + 1 + 3)
                for t in range(CT):
                    for r in range(2):
                        pk = nc.vector.tensor_scalar(pick[:, t, r, :], eidx[:], topf[:, t, r:r + 1], None, ALU.is_equal)
                pk.then_inc(s_route, 1)
                dve.wait_ge(s_route, 6 * c + 1 + 3 + 1)
                nc.vector.tensor_tensor(picked[:], pick[:, :, 0, :], pick[:, :, 1, :], ALU.add).then_inc(s_route, 1)
                dve.wait_ge(s_rexp, CT * c + CT + 1)
                nc.vector.reciprocal(reinv[:], resum[:]).then_inc(s_route, 1)
                dve.wait_ge(s_route, 6 * c + 1 + 5 + 1)
                for t in range(CT):
                    w = nc.vector.scalar_tensor_tensor(
                        out=cw[:, ds(c * CT + t, 1), 0:E_ROUTED].rearrange("p a e -> p (a e)"), in0=rexp[:, t, :],
                        scalar=reinv[:, t:t + 1], in1=picked[:, t, :], op0=ALU.mult, op1=ALU.mult)
                w.then_inc(s_route, 1)
                dve.wait_ge(s_route, 6 * c + 1 + 6 + 1)
                nc.vector.memset(topf[:], 0.0).then_inc(s_rt, 1)

            with dve.Fori(0, NE) as e:
                with dve.Fori(0, NCHUNK) as c:
                    n = e * NCHUNK + c
                    dve.wait_ge(s_silu, n + 2)
                    dve.wait_ge(s_y, n + 1)
                    nc.vector.tensor_tensor(hid, silu, ps[:, 1, :], ALU.mult).then_inc(s_hid, 1)
                    dve.wait_ge(s_y, n + 2)
                    for t in range(CT):
                        rt = resid[:, ds(c * CT + t, 1), :].rearrange("p a d -> p (a d)")
                        ac = nc.vector.scalar_tensor_tensor(
                            out=rt, in0=ps[:, 2 + t // 2, (t % 2) * D:(t % 2 + 1) * D],
                            scalar=cw[:, ds(c * CT + t, 1), ds(e, 1)].rearrange("p a e -> p (a e)"), in1=rt,
                            op0=ALU.mult, op1=ALU.add)
                    ac.then_inc(s_acc, 1)
                    dve.wait_ge(s_acc, n + 2)


_INS = ["x", "ctx_768", "L0_attn_Wq", "L0_attn_Wk", "L0_attn_Wv", "L0_attn_Wo", "L0_attn_W_down_kv", "L0_attn_W_up_k",
        "L0_attn_W_up_v", "L0_xattn_q_w", "L0_xattn_q_b", "L0_xattn_kv_w", "L0_xattn_kv_b", "L0_xattn_proj_w",
        "L0_xattn_proj_b", "L0_ffn_Wr", "L0_ffn_Wg", "L0_ffn_Wu", "L0_ffn_Wd", "L0_ffn_Sg", "L0_ffn_Su", "L0_ffn_Sd"]
_OUTS = [((B, S, D), "float32")]


def kernel(**inputs):
    import numpy as _np
    import concourse.bacc as _bacc
    from concourse import mybir as _mybir
    from concourse.bass_utils import run_bass_kernel_spmd as _run

    nc = _bacc.Bacc("TRN2", target_bir_lowering=False, num_devices=1)
    arrays, args = {}, []
    for name in _INS:
        a = _np.ascontiguousarray(inputs[name])
        arrays[f"in_{name}_dram"] = a
        args.append(nc.dram_tensor(f"in_{name}_dram", a.shape, _mybir.dt.from_np(a.dtype), kind="ExternalInput").ap())
    for i, (shape, dtype) in enumerate(_OUTS):
        dt = _mybir.dt.from_np(_np.dtype(dtype))
        args.append(nc.dram_tensor(f"out_{i}_dram", shape, dt, kind="ExternalOutput").ap())
    decoder_layer(nc, *args)
    r = _run(nc, [arrays], core_ids=[0])
    return r.results[0]["out_0_dram"]
```

```python
from contextlib import ExitStack

import concourse.bass as bass
from concourse import mybir

ALU = mybir.AluOpType
ACT = mybir.ActivationFunctionType
F32 = mybir.dt.float32
BF16 = mybir.dt.bfloat16
I32 = mybir.dt.int32
U32 = mybir.dt.uint32
AX_X = mybir.AxisListType.X
RMAX = bass.bass_isa.ReduceOp.max
ds = bass.ds

P = 128
B, S, D = 2, 1024, 256
T = B * S
TILES = T // P
CT = 4
CHUNK = CT * P
NCHUNK = T // CHUNK
KD = D // P
H, HD = 16, 16
HH = P // HD
ST = S // P
LAT = 64
CS, CD = 64, 192
E_ROUTED, F = 16, 128
FS = 256
WCOLS = KD * F * 2 + D
TOPK = 2
SLOT_TILES = -(-(TOPK * T // P + E_ROUTED - 1) // 4) * 4
YG = 8
CLAMP = 10000.0
DECAY = 0.01 * 0.01
EPS = 1e-5
ATTN_SCALE = 1.0 / 16.0
X_SCALE = HD ** -0.5
NPART = 3
NPROD = 6
SROWS = NPROD * HD
PRODUCTS = ((0, 0, 0, 1, 1, 2), (0, 1, 2, 0, 1, 0))
NB = 2 * (SROWS // HD)
UNITS = B * KD
SPAN = 72.0
SPAN_LOW = 70.0
VAL_MIN, VAL_MAX = 0.1, 1000.0


def decoder_layer(nc, x, ctx_in, wq, wk, wv, wo, w_down, w_up_k, w_up_v, xq_w, xq_b, xkv_w, xkv_b,
                  xproj_w, xproj_b, wr, wg, wu, wd, sg, su, sd, out):
    with ExitStack() as stack:
        def sb(name, shape, dt=F32):
            return stack.enter_context(nc.sbuf_tensor(name, shape, dt))

        def sem(name):
            return stack.enter_context(nc.semaphore(name))

        ps = stack.enter_context(nc.psum_tensor("ps", [P, 8, 512], F32))

        def bank(i, n=1):
            return ps[:, i:i + n, :]

        resid = sb("resid", [P, TILES, D])
        wq_sb = sb("wq_sb", [P, KD, D])
        wkv_sb = sb("wkv_sb", [P, KD, D])
        xk_bd = sb("xk_bd", [P, B, KD, HH, CS])
        wv_sb = xk_bd[:, 0, 0, :, :].rearrange("p h s -> p (h s)").rearrange("p (k n) -> p k n", k=KD)
        wdown_sb = sb("wdown_sb", [P, KD, LAT])
        wup_sb = sb("wup_sb", [LAT, 2, D])
        wo_sb = sb("wo_sb", [P, KD, D])
        xq_sb = sb("xq_sb", [P, KD, D])
        xqb_sb = sb("xqb_sb", [P, KD])
        xkv_hi = sb("xkv_hi", [P, 2 * D])
        xkv_lo = sb("xkv_lo", [CD - P, 2 * D])
        xkb_sb = sb("xkb_sb", [P, KD])
        brow = sb("brow", [1, 2, D])
        xproj_sb = sb("xproj_sb", [P, KD, D])
        wr_sb = sb("wr_sb", [P, KD, E_ROUTED])
        ident = sb("ident", [P, P])
        ones_row = sb("ones_row", [1, P])
        head_mask = sb("head_mask", [P, HH])
        eidx_i = sb("eidx_i", [P, E_ROUTED], I32)
        eidx = sb("eidx", [P, E_ROUTED])
        act_scratch = sb("act_scratch", [P, 7])
        stats = sb("stats", [P, TILES, 6])
        mv = sb("mv", [P, TILES, 2])
        std = sb("std", [P, TILES])
        rstd = sb("rstd", [P, TILES])
        xn = sb("xn", [P, CT, D])
        xnT = sb("xnT", [P, KD, CHUNK])
        att_c = sb("att_c", [P, CT, D])
        oT = sb("oT", [P, KD, CHUNK])
        grow = [att_c[:].rearrange("p t d -> p (t d)"), oT[:].rearrange("p k q -> p (k q)")]
        wcur = sb("wcur", [P, 2, WCOLS])
        kvT = wcur[:].rearrange("p a n -> p (a n)")[:, 0:KD * CHUNK].rearrange("p (k q) -> p k q", k=KD)
        latT = sb("latT", [LAT, CHUNK])
        qT = sb("qT", [P, KD, T])
        kT = sb("kT", [P, KD, T])
        val = sb("val", [P, TILES, D])
        att = val
        parts = sb("parts", [P, 2, 2, NPART, 2, S], BF16)
        words = parts[:, 0, :, :, :, :].rearrange("p t c v s -> p (t c v s)").bitcast(F32)
        pos_i, within_i = words[:, 0:S].bitcast(I32), words[:, S:S + P].bitcast(I32)
        att_g = words[:, 0:TILES * D].rearrange("p (t d) -> p t d", t=TILES)
        diff_i = words[:, TILES * D:TILES * D + 1920].bitcast(I32)
        spare = parts[:, 1, :, :, :, :].rearrange("p t c v s -> p (t c v s)")
        squares = spare[:, 0:2 * KD * T].rearrange("p (t k n) -> p t k n", t=2, k=KD)
        general = spare.bitcast(F32)
        qm = general[:, 0:S]
        sc_clip = general[:, S:2 * S]
        sc_dec = general[:, 2 * S:4 * S].rearrange("p (a s) -> p a s", a=2)
        prob = general[:, 4 * S:5 * S]
        probT = general[:, 5 * S:6 * S].rearrange("p (k q) -> p k q", q=P)
        qstack = sb("qstack", [SROWS, 2, 2, S], BF16)
        kstack = sb("kstack", [SROWS, 2, 2, S], BF16)
        ftmp = sb("ftmp", [P, 2, 512])
        pT = sb("pT", [P, 2, S])
        decay = pT[:].rearrange("p a s -> p (a s)")[:, 0:1920]
        vcur = sb("vcur", [P, 2, ST, 2 * HD])
        obT = sb("obT", [P, 256])
        rinv8 = sb("rinv8", [P, ST])
        within = sb("within", [P, P])
        head_ind = sb("head_ind", [P, 2 * HD])
        head_ind_bf = sb("head_ind_bf", [P, 2 * HD], BF16)
        ksum = sb("ksum", [P, NCHUNK, KD])
        ksq = sb("ksq", [P, B, KD])
        vsq = pT[:, 1, :]
        red = sb("red", [P, 8])
        reda = sb("reda", [P, 8])
        sums = sb("sums", [P, 2])
        fl = sb("fl", [P, 12])
        shift = sb("shift", [P, 1])
        flag_i = sb("flag_i", [P, 1], I32)
        junk = qstack[0:4 * HD, :, :, :].rearrange("p a v s -> p a (v s)")
        rmax = sb("rmax", [P, ST])
        nmax = sb("nmax", [P, ST])
        rsum = sb("rsum", [P, ST])
        rinv = sb("rinv", [P, ST])
        ctx_sb = sb("ctx_sb", [P, B, CD])
        ctxT_hi = sb("ctxT_hi", [P, B, P])
        ctxT_lo = sb("ctxT_lo", [CD - P, B, P])
        xkT = sb("xkT", [P, KD, B, CS])
        xv_bd = sb("xv_bd", [P, B, HH, 2 * (HD + 1)])
        keys = kT[:].rearrange("p k n -> p (k n)")
        xsc = keys[:, H * CS:2 * H * CS].rearrange("p (h s) -> p h s", s=CS)
        xp = [keys[:, (2 + r) * H * CS:(3 + r) * H * CS].rearrange("p (h s) -> p h s", s=CS) for r in range(2)]
        xpT = pT[:, 0, :].rearrange("p (j q) -> p j q", q=P)
        xqT = qT
        xq_cur = [keys[:, r * KD * P:(r + 1) * KD * P].rearrange("p (k q) -> p k q", k=KD) for r in range(2)]
        xo_n = keys[:, 2 * D:3 * D]
        xoT = keys[:, 3 * D:4 * D]
        xmax = sb("xmax", [P, 2, H])
        xinv = sb("xinv", [P, H])
        TE = TILES * E_ROUTED

        def table(place, rows, cols):
            return keys[:, place:place + rows * cols].rearrange("p (a e) -> p a e", e=cols)

        logit = pT[:, 1, 0:TE].rearrange("p (t e) -> p t e", e=E_ROUTED)
        below = pT[:, 1, TE:2 * TE].rearrange("p (t e) -> p t e", e=E_ROUTED)
        rexp = pT[:, 1, 2 * TE:3 * TE].rearrange("p (t e) -> p t e", e=E_ROUTED)
        picked = pT[:, 1, 3 * TE:4 * TE].rearrange("p (t e) -> p t e", e=E_ROUTED)
        pick = [table(r * TE, TILES, E_ROUTED) for r in range(2)]
        place_of = table(2 * TE, TILES, E_ROUTED)
        mine = table(3 * TE, TILES, E_ROUTED)
        over = table(4 * TE, E_ROUTED, E_ROUTED)
        before = table(5 * TE, TILES + 1, E_ROUTED)
        ended = table(6 * TE + E_ROUTED, SLOT_TILES, E_ROUTED)
        xt = [keys[:, 10 * TE + r * D:10 * TE + (r + 1) * D] for r in range(4)]
        xtT = [oT[:, 0, r * D:(r + 1) * D].rearrange("p (k q) -> p k q", k=KD) for r in range(2)]
        hT = [oT[:, 1, r * F:(r + 1) * F] for r in range(2)]
        hid_s = [oT[:, 1, (2 + r) * F:(3 + r) * F] for r in range(2)]
        silu_s = [xnT[:, 0, r * F:(r + 1) * F] for r in range(2)]
        yt = [ftmp[:, r // 2, r % 2 * D:(r % 2 + 1) * D] for r in range(4)]
        xe = val
        wres = parts[:].rearrange("p u t c v s -> p (u t c v s)").bitcast(F32).rearrange("p (e n) -> p e n", n=WCOLS)
        wflat = parts[:].rearrange("p u t c v s -> p (u t c v s)").bitcast(F32)
        zeros = wcur[:].rearrange("p a n -> p (a n)")[:, KD * CHUNK:KD * CHUNK + D]
        tri = sb("tri", [P, P])
        ones_sq = sb("ones_sq", [P, P])
        earlier = obT[:].rearrange("p (a e) -> p a e", e=E_ROUTED)
        jidx_i = sb("jidx_i", [P, SLOT_TILES], I32)
        jidx = sb("jidx", [P, SLOT_TILES])
        ntiles = sb("ntiles", [P, E_ROUTED])
        start = sb("start", [P, E_ROUTED])
        stop = sb("stop", [P, E_ROUTED])
        start_slot = sb("start_slot", [P, E_ROUTED])
        limit = sb("limit", [P, E_ROUTED])
        owner = sb("owner", [P, SLOT_TILES])
        owner_i = sb("owner_i", [P, SLOT_TILES], I32)
        place = sb("place", [P, TOPK, TILES])
        place_i = sb("place_i", [P, TOPK, TILES], U32)
        wtop = sb("wtop", [P, TILES, TOPK])
        x_slots = nc.dram_tensor("x_slots", [SLOT_TILES * P, D], F32, kind="Internal").ap()
        y_slots = nc.dram_tensor("y_slots", [SLOT_TILES * P, D], F32, kind="Internal").ap()
        heads_v = vcur[:].rearrange("p a t n -> p (a t n)")
        top = heads_v[:, 0:TILES * 8].rearrange("p (t n) -> p t n", n=8)
        topi = heads_v[:, TILES * 8:2 * TILES * 8].rearrange("p (t n) -> p t n", n=8).bitcast(U32)
        topf = sb("topf", [P, TILES, 2])
        resum = sb("resum", [P, TILES])
        reinv = sb("reinv", [P, TILES])
        fT = qT
        silu = xn[:].rearrange("p t d -> p (t d)").rearrange("p (a n) -> p a n", a=2)
        hid = att_c[:].rearrange("p t d -> p (t d)").rearrange("p (a n) -> p a n", a=2)

        s_x = sem("s_x"); s_w = sem("s_w"); s_wb = sem("s_wb"); s_out = sem("s_out")
        s_const = sem("s_const"); s_pool = sem("s_pool")
        s_decay = sem("s_decay"); s_ones = sem("s_ones"); s_wkv = sem("s_wkv")
        s_ln = sem("s_ln"); s_var = sem("s_var"); s_std = sem("s_std"); s_xn = sem("s_xn")
        s_xnT_ps = sem("s_xnT_ps"); s_xnT = sem("s_xnT")
        s_q_ps = sem("s_q_ps"); s_q = sem("s_q"); s_kv_ps = sem("s_kv_ps"); s_kv = sem("s_kv")
        s_lat_ps = sem("s_lat_ps"); s_lat = sem("s_lat"); s_k_ps = sem("s_k_ps"); s_k = sem("s_k")
        s_v_ps = sem("s_v_ps"); s_v = sem("s_v")
        s_qm = sem("s_qm"); s_sc = sem("s_sc"); s_clip = sem("s_clip"); s_dec = sem("s_dec")
        s_nmax = sem("s_nmax"); s_prob = sem("s_prob"); s_pT_ps = sem("s_pT_ps"); s_pT = sem("s_pT")
        s_o_ps = sem("s_o_ps"); s_rinv = sem("s_rinv"); s_o = sem("s_o")
        s_sq = sem("s_sq"); s_vmax = sem("s_vmax"); s_norm_ps = sem("s_norm_ps"); s_sums = sem("s_sums")
        s_red = sem("s_red"); s_reda = sem("s_reda"); s_root = sem("s_root"); s_fl = sem("s_fl"); s_flag = sem("s_flag")
        s_grow = sem("s_grow"); s_split = sem("s_split"); s_split0 = sem("s_split0"); s_parts = sem("s_parts")
        s_parts0 = sem("s_parts0")
        s_stack = [sem("s_stack0"), sem("s_stack1")]
        s_fs = sem("s_fs"); s_diag = sem("s_diag"); s_exp = sem("s_exp"); s_pv = sem("s_pv"); s_vcur = sem("s_vcur")
        s_ob = sem("s_ob"); s_ot = sem("s_ot"); s_on = sem("s_on"); s_att = sem("s_att")
        s_cT_ps = sem("s_cT_ps"); s_cT = sem("s_cT"); s_ck_ps = sem("s_ck_ps"); s_ck = sem("s_ck")
        s_cv_ps = sem("s_cv_ps"); s_cv = sem("s_cv"); s_cbd = sem("s_cbd")
        s_attc = sem("s_attc"); s_xqc = sem("s_xqc"); s_oT_ps = sem("s_oT_ps"); s_oT = sem("s_oT")
        s_wo = sem("s_wo"); s_res = sem("s_res"); s_xq_ps = sem("s_xq_ps"); s_xq = sem("s_xq")
        s_xs = sem("s_xs"); s_xmax = sem("s_xmax"); s_xsub = sem("s_xsub"); s_xp = sem("s_xp")
        s_xpT_ps = sem("s_xpT_ps"); s_xpT = sem("s_xpT"); s_xo_ps = sem("s_xo_ps"); s_xon = sem("s_xon")
        s_xoT_ps = sem("s_xoT_ps"); s_xoT = sem("s_xoT")
        s_pj = sem("s_pj"); s_res2 = sem("s_res2"); s_fT = sem("s_fT")
        s_lg_ps = sem("s_lg_ps"); s_lg = sem("s_lg"); s_below = sem("s_below"); s_rexp = sem("s_rexp")
        s_eidx = sem("s_eidx"); s_zero = sem("s_zero"); s_tri = sem("s_tri"); s_picked = sem("s_picked"); s_count_ps = sem("s_count_ps")
        s_place = sem("s_place"); s_scatter = sem("s_scatter"); s_wres = sem("s_wres")
        s_xt = [sem(f"s_xt{r}") for r in range(4)]; s_tT_ps = sem("s_tT_ps"); s_tT = sem("s_tT"); s_tgu = sem("s_tgu")
        s_tsilu = sem("s_tsilu"); s_thid = sem("s_thid"); s_hT_ps = sem("s_hT_ps"); s_hT = sem("s_hT")
        s_ty_ps = sem("s_ty_ps"); s_yt = sem("s_yt"); s_yst = [sem(f"s_yst{r}") for r in range(4)]
        s_yg = [sem(f"s_yg{r}") for r in range(YG)]; s_comb = sem("s_comb")
        s_wcur = [sem("s_wcur0"), sem("s_wcur1")]; s_gu = sem("s_gu"); s_silu = sem("s_silu"); s_hid = sem("s_hid")
        s_y = sem("s_y"); s_acc = sem("s_acc")

        x_d = x.rearrange("b (n p) d -> p (b n) d", p=P)
        out_d = out.rearrange("b (n p) d -> p (b n) d", p=P)
        def split(eng, nceng, step, tmp, buf, u, t, sign, cols):
            b, half = u // KD, u % KD
            src = (qT, kT)[t][:, half, b * S + cols.start:b * S + cols.stop]
            dst = parts[:, buf, t, :, sign, cols]
            step(nceng.tensor_tensor(tmp[:, 0, :], src, grow[sign][:, cols], ALU.mult))
            step(nceng.tensor_copy(dst[:, 0, :], tmp[:, 0, :]))
            step(nceng.tensor_tensor(tmp[:, 1, :], tmp[:, 0, :], dst[:, 0, :], ALU.subtract))
            step(nceng.tensor_copy(dst[:, 1, :], tmp[:, 1, :]))
            return nceng.tensor_tensor(dst[:, 2, :], tmp[:, 1, :], dst[:, 1, :], ALU.subtract)

        def after(eng, semaphore, count):
            if not isinstance(count, int) or count > 0:
                eng.wait_ge(semaphore, count)

        def score_bank(g, kt):
            return 2 * ((ST * g + kt) % 3)

        NW = 11
        NWB = 7

        RING = 2
        block = stack.enter_context(nc.Block())

        @block.sync
        def _(sp):
            for c in range(NCHUNK):
                sp.dma_start(resid[:, c * CT:(c + 1) * CT, :], x_d[:, c * CT:(c + 1) * CT, :]).then_inc(s_x, 16)
            sp.dma_start(wq_sb[:], wq.rearrange("(k p) n -> p k n", p=P)).then_inc(s_w, 16)
            sp.dma_start(wkv_sb[:], wk.rearrange("(k p) n -> p k n", p=P)).then_inc(s_w, 16)
            sp.dma_start(wv_sb, wv.rearrange("(k p) n -> p k n", p=P)).then_inc(s_w, 16)
            sp.dma_start(wdown_sb[:], w_down.rearrange("(k p) n -> p k n", p=P)).then_inc(s_w, 16)
            sp.dma_start(wup_sb[:, 0, :], w_up_k).then_inc(s_w, 16)
            sp.dma_start(wup_sb[:, 1, :], w_up_v).then_inc(s_w, 16)
            sp.dma_start(wo_sb[:], wo.rearrange("(k p) n -> p k n", p=P)).then_inc(s_w, 16)
            sp.dma_start(xq_sb[:], xq_w.rearrange("(k p) n -> p k n", p=P)).then_inc(s_w, 16)
            sp.dma_start(xproj_sb[:], xproj_w.rearrange("(k p) n -> p k n", p=P)).then_inc(s_w, 16)
            sp.dma_start(xkv_hi[:], xkv_w[0:P, :]).then_inc(s_w, 16)
            sp.dma_start(xkv_lo[:], xkv_w[P:CD, :]).then_inc(s_w, 16)
            for r in range(2):
                sp.dma_start(ctx_sb[r * CS:(r + 1) * CS, :, :], ctx_in.rearrange("b s d -> s b d")).then_inc(s_wb, 16)
            with nc.allow_non_contiguous_dma("biases, one channel to a partition"):
                sp.dma_start(xqb_sb[:], xq_b.rearrange("(k p) -> p k", p=P)).then_inc(s_wb, 16)
                sp.dma_start(xkb_sb[:], xkv_b[0:D].rearrange("(k p) -> p k", p=P)).then_inc(s_wb, 16)
                sp.dma_start(wr_sb[:], wr.rearrange("(k p) n -> p k n", p=P)).then_inc(s_wb, 16)
            sp.dma_start(brow[:, 0, :], xkv_b[D:2 * D].rearrange("(a n) -> a n", a=1)).then_inc(s_wb, 16)
            sp.dma_start(brow[:, 1, :], xproj_b.rearrange("(a n) -> a n", a=1)).then_inc(s_wb, 16)

            sp.wait_ge(s_zero, 1)
            sp.dma_start(x_slots.rearrange("(n p) d -> p n d", p=P), zeros.unsqueeze(1).to_broadcast([P, SLOT_TILES, D]))\
                .then_inc(s_zero, 16)

            def load_head(u, j):
                r = j % 2
                after(sp, s_fs, 2 * ST * (u * HH + j - 1))
                head = parts[j * HD:(j + 1) * HD, u % 2, :, :, :, :]
                for t, stk in ((0, qstack), (1, kstack)):
                    for row in range(NPROD):
                        sp.dma_start(stk[row * HD:(row + 1) * HD, r, :, :], head[:, t, PRODUCTS[t][row], :, :])\
                            .then_inc(s_stack[r], 16)

            sp.wait_ge(s_parts0, 1)
            sp.wait_ge(s_sums, 2)
            load_head(0, 0)
            load_head(0, 1)
            sp.wait_ge(s_flag, 1)
            short = sp.value_load(flag_i[0:1, 0:1], min_val=0, max_val=1)
            with sp.If(short == 1):
                for u in range(UNITS):
                    sp.wait_ge(s_parts, u + 1)
                    for j in range(HH):
                        if u * HH + j >= 2:
                            load_head(u, j)
            sp.wait_ge(s_zero, 17)
            for m in range(2):
                cols = slice(m * F, (m + 1) * F)
                for a, w in ((0, sg), (2, su)):
                    sp.dma_start(wcur[:, m, a * F:(a + 2) * F].rearrange("p (k f) -> p k f", k=KD),
                                 w[:, cols].rearrange("(k p) f -> p k f", p=P)).then_inc(s_wcur[m], 16)
                sp.dma_start(wcur[:, m, 4 * F:], sd[cols, :]).then_inc(s_wcur[m], 16)
            sp.wait_ge(s_att, 1)
            with sp.Fori(0, E_ROUTED) as e:
                gu = wres[:, ds(e, 1), 0:4 * F].rearrange("p a (k m f) -> p (a k) m f", k=KD, m=2)
                for m, w in enumerate((wg, wu)):
                    sp.dma_start(gu[:, :, m, :], w[ds(e, 1), :, :].rearrange("a (k p) f -> p (a k) f", p=P)).then_inc(s_wres, 16)
                sp.dma_start(wres[:, ds(e, 1), 4 * F:].rearrange("p a n -> p (a n)"),
                             wd[ds(e, 1), :, :].rearrange("a f d -> f (a d)")).then_inc(s_wres, 16)

            def load_tile(j, r):
                after(sp, s_tT_ps, j - 3)
                sp.dma_start(xt[r], x_slots[ds(j * P, P), :]).then_inc(s_xt[r], 16)

            def store_tile(j, r):
                sp.wait_ge(s_yt, j + 1)
                sp.dma_start(y_slots[ds(j * P, P), :], yt[r]).then_inc(s_yst[r], 16)

            sp.wait_ge(s_scatter, 16 * TOPK * TILES)
            for r in range(4):
                load_tile(r, r)
            with sp.Fori(0, SLOT_TILES // 4 - 1) as i:
                for r in range(4):
                    load_tile(4 * i + r + 4, r)
                    store_tile(4 * i + r, r)
            for r in range(4):
                store_tile(SLOT_TILES - 4 + r, r)
            for c in range(NCHUNK):
                sp.wait_ge(s_acc, RING + NCHUNK + c + 1)
                sp.wait_ge(s_comb, TOPK * CT * (c + 1))
                sp.dma_start(out_d[:, c * CT:(c + 1) * CT, :], resid[:, c * CT:(c + 1) * CT, :]).then_inc(s_out, 16)
            sp.wait_ge(s_out, 16 * NCHUNK)

        @block.gpsimd
        def _(pool):
            pool.sem_inc(s_attc, 1)

            nc.gpsimd.memset(ident[:], 0.0).then_inc(s_pool, 1)
            nc.gpsimd.memset(head_mask[:], 1.0).then_inc(s_pool, 1)
            nc.gpsimd.memset(vcur[:], 0.0).then_inc(s_pool, 1)
            nc.gpsimd.memset(head_ind[:], 0.0).then_inc(s_pool, 1)
            nc.gpsimd.memset(ones_row[:], 1.0).then_inc(s_const, 1)
            nc.gpsimd.memset(xv_bd[:], 0.0).then_inc(s_const, 1)
            nc.gpsimd.memset(ones_sq[:], 1.0).then_inc(s_const, 1)
            nc.gpsimd.memset(zeros, 0.0).then_inc(s_zero, 1)
            pool.wait_ge(s_pool, 4)
            nc.gpsimd.affine_select(out=ident[:], in_=ident[:], compare_op=ALU.not_equal, fill=1.0, base=0,
                                    pattern=[[-1, P]], channel_multiplier=1).then_inc(s_const, 1)
            nc.gpsimd.affine_select(out=head_mask[:], in_=head_mask[:], compare_op=ALU.is_ge, fill=0.0, base=0,
                                    pattern=[[-HD, HH]], channel_multiplier=1).then_inc(s_pool, 1)
            pool.wait_ge(s_pool, 5)
            nc.gpsimd.affine_select(out=head_mask[:], in_=head_mask[:], compare_op=ALU.is_ge, fill=0.0, base=HD - 1,
                                    pattern=[[HD, HH]], channel_multiplier=-1).then_inc(s_const, 1)
            nc.gpsimd.iota(eidx_i[:], pattern=[[1, E_ROUTED]], base=0, channel_multiplier=0).then_inc(s_const, 1)

            nc.gpsimd.iota(pos_i, pattern=[[1, S]], base=0, channel_multiplier=0).then_inc(s_grow, 1)
            nc.gpsimd.iota(within_i, pattern=[[-1, P]], base=0, channel_multiplier=1).then_inc(s_grow, 1)
            nc.gpsimd.memset(vcur[:, :, :, HD:HD + 1], 1.0).then_inc(s_pool, 1)
            pool.wait_ge(s_const, 6)
            nc.gpsimd.tensor_copy(head_ind[:, 0:HH], head_mask[:]).then_inc(s_pool, 1)
            pool.wait_ge(s_pool, 7)
            nc.gpsimd.tensor_copy(head_ind_bf[:], head_ind[:]).then_inc(s_pool, 1)
            pool.wait_ge(s_pool, 8)
            for r in range(2):
                nc.gpsimd.memset(xv_bd[r * CS:(r + 1) * CS, :, :, r * (HD + 1) + HD:(r + 1) * (HD + 1)], 1.0)                    .then_inc(s_ones, 1)
                pool.wait_ge(s_ones, r + 1)
            nc.gpsimd.affine_select(out=tri[:], in_=ones_sq[:], compare_op=ALU.is_gt, fill=0.0, base=0,
                                    pattern=[[1, P]], channel_multiplier=-1).then_inc(s_tri, 1)
            nc.gpsimd.iota(jidx_i[:], pattern=[[1, SLOT_TILES]], base=0, channel_multiplier=0).then_inc(s_tri, 1)

            for c in range(NCHUNK):
                for t, (src, ready) in enumerate(((qT, s_q), (kT, s_k))):
                    part = src[:, :, c * CHUNK:(c + 1) * CHUNK]
                    pool.wait_ge(ready, c + 2 if t == 0 else KD * (c + 1) + 1)
                    nc.gpsimd.tensor_tensor(squares[:, t, :, c * CHUNK:(c + 1) * CHUNK], part, part, ALU.mult)\
                        .then_inc(s_sq, 1)
                pool.wait_ge(s_v, c + 2)
                v = val[:, c * CT:(c + 1) * CT, :].rearrange("p t d -> p (t d)")
                fresh = ftmp[:].rearrange("p a n -> p (a n)")
                after(pool, s_vmax, 2 * c - 1)
                nc.gpsimd.tensor_tensor(fresh if c else vsq, v, v, ALU.mult).then_inc(s_vmax, 1)
                if c:
                    pool.wait_ge(s_vmax, 2 * c)
                    nc.gpsimd.tensor_tensor(vsq, vsq, fresh, ALU.add).then_inc(s_vmax, 1)
            pool.wait_ge(s_red, 2)
            nc.gpsimd.partition_all_reduce(reda[:], red[:], P, RMAX).then_inc(s_reda, 1)

            def count(instruction):
                done[0] += 1
                instruction.then_inc(s_split, 1)
                pool.wait_ge(s_split, done[0])

            done = [0]
            pool.wait_ge(s_grow, 5)
            pool.wait_ge(s_vmax, 2 * NCHUNK - 1)
            pool.wait_ge(s_flag, 1)
            short = pool.value_load(flag_i[0:1, 0:1], min_val=0, max_val=1)
            with pool.If(short == 1):
                pool.sem_inc(s_parts, 1)
                for u in range(1, UNITS):
                    for r in range(2):
                        after(pool, s_stack[r], 16 * NB * (HH // 2) * (u - 1))
                    for t in range(2):
                        for sign in range(2):
                            for c in range(2):
                                count(split(pool, nc.gpsimd, count, ftmp, u % 2, u, t, sign, slice(512 * c, 512 * (c + 1))))
                    pool.sem_inc(s_parts, 1)

            with pool.If(short == 0):
                pool.wait_ge(s_parts0, 1)
                for r in range(2):
                    pool.wait_ge(s_stack[r], 16 * NB)
                nc.gpsimd.iota(diff_i, pattern=[[-1, 1920]], base=S - P, channel_multiplier=1).then_inc(s_decay, 1)

            pool.wait_ge(s_att, 1)
            with pool.Fori(0, NCHUNK) as c:
                pool.wait_ge(s_oT_ps, c + 1)
                nc.gpsimd.tensor_copy(att_c[:], att[:, ds(c * CT, CT), :]).then_inc(s_attc, 1)
            with pool.Fori(0, TILES // 2) as i:
                for r in range(2):
                    t = 2 * i + r
                    pool.wait_ge(s_xq, KD * NCHUNK + 1)
                    pool.wait_ge(s_xs, RING + t - 1)
                    nc.gpsimd.tensor_copy(xq_cur[r], xqT[:, :, ds(t * P, P)]).then_inc(s_xqc, 1)

            pool.wait_ge(s_place, 1)
            pool.wait_ge(s_zero, 17)
            for t in range(TILES):
                for r in range(TOPK):
                    nc.gpsimd.indirect_dma_start(x_slots, bass.IndirectOffsetOnAxis(ap=place_i[:, r, t:t + 1], axis=0),
                                                 xe[:, t, :], None).then_inc(s_scatter, 16)
            for r in range(4):
                pool.wait_ge(s_yst[r], 16 * (SLOT_TILES // 4))
            pool.wait_ge(s_scatter, 16 * TOPK * TILES)
            for g in range(TOPK * TILES):
                t, r = g // TOPK, g % TOPK
                after(pool, s_comb, g - YG + 1)
                nc.gpsimd.indirect_dma_start(xe[:, g % YG, :], None, y_slots,
                                             bass.IndirectOffsetOnAxis(ap=place_i[:, r, t:t + 1], axis=0))\
                    .then_inc(s_yg[g % YG], 16)

        @block.tensor
        def _(pe):
            for s in (s_xnT_ps, s_q_ps, s_kv_ps, s_lat_ps, s_k_ps, s_v_ps, s_sc, s_pT_ps, s_o_ps, s_oT_ps, s_wo,
                      s_xq_ps, s_gu):
                pe.sem_inc(s, 1)
            for s in (s_xs, s_xpT_ps, s_xo_ps, s_xoT_ps, s_pj, s_y):
                pe.sem_inc(s, RING)

            def transposes(src, first=0):
                for k in range(KD):
                    for t in range(CT):
                        last = nc.tensor.transpose(ps[:, first + k, t * P:(t + 1) * P], src[:, t, k * P:(k + 1) * P], ident[:])
                return last

            def project(first, w, rhs, rows=P):
                for n in range(KD):
                    for k in range(KD):
                        last = nc.tensor.matmul(ps[0:rows, first + n, :], w[:, k, n * P:n * P + rows], rhs[:, k, :],
                                                start=(k == 0), stop=(k == KD - 1))
                return last

            pe.wait_ge(s_const, 6)
            pe.wait_ge(s_w, 16 * NW)
            pe.wait_ge(s_wkv, 1)

            pe.wait_ge(s_wb, 16 * NWB)
            for b in range(B):
                nc.tensor.transpose(ps[:, 4, b * P:(b + 1) * P], ctx_sb[:, b, 0:P], ident[:])
                mm = nc.tensor.transpose(ps[0:CD - P, 5, b * P:(b + 1) * P], ctx_sb[:, b, P:CD], ident[:])
            mm.then_inc(s_cT_ps, 1)
            pe.wait_ge(s_cT, 2)
            for n in range(KD):
                dst = ps[:, 6, n * P:(n + 1) * P].rearrange("p (b s) -> p b s", b=B)
                nc.tensor.matmul(dst, xkv_hi[:, n * P:(n + 1) * P], ctxT_hi[:, :, 0:CS], start=True, stop=False)
                mm = nc.tensor.matmul(dst, xkv_lo[:, n * P:(n + 1) * P], ctxT_lo[:, :, 0:CS], start=False, stop=True)
            mm.then_inc(s_ck_ps, 1)
            for b in range(B):
                dst = ps[:, 7, b * D:(b + 1) * D]
                nc.tensor.matmul(dst, ctxT_hi[:, b, :], xkv_hi[:, D:], start=True, stop=False)
                nc.tensor.matmul(dst, ctxT_lo[:, b, :], xkv_lo[:, D:], start=False, stop=False)
                mm = nc.tensor.matmul(dst, ones_row[:], brow[:, 0, :], start=False, stop=True)
            mm.then_inc(s_cv_ps, 1)
            def queries_in(c):
                pe.wait_ge(s_xn, c + 2)
                after(pe, s_k, KD * (c - 1) + 1)
                transposes(xn).then_inc(s_xnT_ps, 1)

            def queries(c):
                pe.wait_ge(s_xnT, c + 2)
                pe.wait_ge(s_q, c + 1)
                project(2, wq_sb, xnT).then_inc(s_q_ps, 1)

            def keys_and_values(c, last=False):
                pe.wait_ge(s_kv, c + 1)
                project(4, wkv_sb, xnT).then_inc(s_kv_ps, 1)
                if not last:
                    queries_in(c + 1)
                pe.wait_ge(s_kv, c + 2)
                pe.wait_ge(s_v, c + 1)
                for k in range(KD):
                    mm = nc.tensor.matmul(ps[0:LAT, 6, :], wdown_sb[:, k, :], kvT[:, k, :], start=(k == 0), stop=(k == KD - 1))
                mm.then_inc(s_lat_ps, 1)
                if not last:
                    queries(c + 1)
                pe.wait_ge(s_lat, c + 2)
                for n in range(KD):
                    mm = nc.tensor.matmul(ps[:, n, :], wup_sb[:, 0, n * P:(n + 1) * P], latT[:], start=True, stop=True)
                mm.then_inc(s_k_ps, 1)
                for t in range(CT):
                    mm = nc.tensor.matmul(ps[:, 6 + t // 2, (t % 2) * D:(t % 2 + 1) * D], latT[:, t * P:(t + 1) * P],
                                          wup_sb[:, 1, :], start=True, stop=True)
                mm.then_inc(s_v_ps, 1)

            queries_in(0)
            queries(0)
            pe.wait_ge(s_cT, 2)
            pe.wait_ge(s_ck, KD)
            pe.wait_ge(s_cv, 2)
            with pe.Fori(0, NCHUNK - 1) as c:
                keys_and_values(c)
            keys_and_values(NCHUNK - 1, last=True)

            pe.wait_ge(s_v, NCHUNK + 1)
            pe.wait_ge(s_q, NCHUNK + 1)
            pe.wait_ge(s_k, KD * NCHUNK + 1)
            pe.wait_ge(s_sq, 2 * NCHUNK)
            pe.wait_ge(s_pool, 8)
            for t in range(2):
                for k in range(KD):
                    r = 2 * HD * k
                    for c in range(NCHUNK):
                        mm = nc.tensor.matmul(ps[r:r + 2 * HD, NCHUNK * t + c, :], head_ind_bf[:],
                                              squares[:, t, k, c * CHUNK:(c + 1) * CHUNK], start=True, stop=True,
                                              tile_position=(0, r))
            mm.then_inc(s_norm_ps, 1)
            pe.wait_ge(s_sums, 2)
            pe.wait_ge(s_fl, 3)
            nc.tensor.matmul(ps[0:2 * HD, 7, 0:B * KD], head_ind[:], ksq[:].rearrange("p b k -> p (b k)"),
                             start=True, stop=True).then_inc(s_norm_ps, 1)

            pe.wait_ge(s_flag, 1)
            short = pe.value_load(flag_i[0:1, 0:1], min_val=0, max_val=1)

            def head_scores(m, kt, r, g3):
                after(pe, s_exp, m - 2)
                first = kt // 4
                for g in (first, 1 - first):
                    lo, hi = 512 * g, 512 * (g + 1)
                    cut = min(max(kt * P, lo), hi)
                    for a, z, sign in ((lo, cut, 0), (cut, hi, 1)):
                        if a < z:
                            mm = nc.tensor.matmul(ps[:, score_bank(g3, kt) + g, a - lo:z - lo],
                                                  kstack[:, r, 1 - sign, kt * P:(kt + 1) * P],
                                                  qstack[:, r, sign, a:z], start=True, stop=True)
                    mm.then_inc(s_fs, 1)

            def weighted(n, m, kt, r):
                pe.wait_ge(s_exp, m + 1)
                if kt == 0:
                    pe.wait_ge(s_vcur, n + 1)
                    after(pe, s_on, n - 1)
                for g in range(4):
                    mm = nc.tensor.matmul(ps[2 * HD * g:2 * HD * (g + 1), 6 + r, 0:256], vcur[:, r, kt, :],
                                          pT[:, kt % 2, 256 * g:256 * (g + 1)], start=(kt == 0), stop=(kt == ST - 1),
                                          tile_position=(0, 2 * HD * g))
                mm.then_inc(s_pv, 1)

            def out_transposes(n, r):
                pe.wait_ge(s_ob, n + 1)
                for c in range(2):
                    mm = nc.tensor.transpose(ps[:, 6 + r, 256 + c * P:256 + (c + 1) * P], obT[:, c * P:(c + 1) * P], ident[:])
                mm.then_inc(s_ot, 1)

            def head_steps(n, r, g3, pairs, first=False):
                for kt in range(ST):
                    m = ST * n + kt
                    if kt == 0:
                        pe.wait_ge(s_stack[r], 16 * NB * (pairs + 1))
                    head_scores(m, kt, r, g3)
                    if kt >= 2:
                        weighted(n, m - 2, kt - 2, r)
                    elif not first:
                        weighted(n - 1, m - 2, ST - 2 + kt, 1 - r)
                    if kt == 3 and not first:
                        out_transposes(n - 1, 1 - r)

            with pe.If(short == 1):
                head_steps(0, 0, 0, 0, first=True)
                head_steps(1, 1, 1, 0)
                with pe.Fori(0, (B * H - 2) // 6) as i:
                    for h in range(2, 8):
                        head_steps(6 * i + h, h % 2, h % 3, 3 * i + h // 2)
                n = B * H - 1
                for kt in (ST - 2, ST - 1):
                    weighted(n, ST * n + kt, kt, 1)
                out_transposes(n, 1)

            def scores(half, b, n, qt):
                pe.wait_ge(s_clip, (n * ST + qt - 1 + 1 if qt == 0 else n * ST + qt - 1) + 1)
                for g in range(2):
                    mm = nc.tensor.matmul(ps[:, 2 * (qt % 2) + g, :], qm[:, qt * P:(qt + 1) * P],
                                          kT[:, ds(half, 1), ds(b * S + g * 512, 512)].rearrange("p a n -> p (a n)"),
                                          start=True, stop=True)
                mm.then_inc(s_sc, 1)

            with pe.If(short == 0):
                with pe.Fori(0, B) as b:
                    with pe.Fori(0, KD) as half:
                        with pe.Fori(0, HH) as j:
                            n = b * H + half * HH + j
                            pe.wait_ge(s_qm, n + 2)
                            scores(half, b, n, 0)
                            for qt in range(ST):
                                if qt + 1 < ST:
                                    scores(half, b, n, qt + 1)
                                pe.wait_ge(s_prob, n * ST + qt + 2)
                                pe.wait_ge(s_pT, n * ST + qt + 1)
                                for kt in range(ST):
                                    mm = nc.tensor.transpose(ps[:, 4 + kt // 4, (kt % 4) * P:(kt % 4 + 1) * P],
                                                             prob[:, kt * P:(kt + 1) * P], ident[:])
                                mm.then_inc(s_pT_ps, 1)
                                pe.wait_ge(s_pT, n * ST + qt + 2)
                                pe.wait_ge(s_o, n * ST + qt + 1)
                                for kt in range(ST):
                                    mm = nc.tensor.matmul(ps[:, 6, 0:HD], probT[:, kt, :],
                                                          val[:, ds(b * ST + kt, 1), ds(half * P + j * HD, HD)]
                                                          .rearrange("p a n -> p (a n)"),
                                                          start=(kt == 0), stop=(kt == ST - 1))
                                mm.then_inc(s_o_ps, 1)

            def out_in(c):
                pe.wait_ge(s_attc, c + 2)
                pe.wait_ge(s_oT, c + 1)
                transposes(att_c).then_inc(s_oT_ps, 1)

            def project_out(c):
                pe.wait_ge(s_oT, c + 2)
                pe.wait_ge(s_res, c + 1)
                for t in range(CT):
                    for k in range(KD):
                        mm = nc.tensor.matmul(ps[:, 2 + t // 2, (t % 2) * D:(t % 2 + 1) * D], oT[:, k, t * P:(t + 1) * P],
                                              wo_sb[:, k, :], start=(k == 0), stop=(k == KD - 1))
                mm.then_inc(s_wo, 1)

            def cross_in(c):
                pe.wait_ge(s_xn, NCHUNK + c + 2)
                pe.wait_ge(s_xnT, NCHUNK + c + 1)
                transposes(xn, 4).then_inc(s_xnT_ps, 1)

            def cross_queries(c):
                pe.wait_ge(s_xnT, NCHUNK + c + 2)
                pe.wait_ge(s_xq, KD * c + 1)
                project(6, xq_sb, xnT).then_inc(s_xq_ps, 1)

            out_in(0)
            project_out(0)
            with pe.Fori(0, NCHUNK - 1) as c:
                out_in(c + 1)
                cross_in(c)
                project_out(c + 1)
                cross_queries(c)
            cross_in(NCHUNK - 1)
            cross_queries(NCHUNK - 1)

            def cross_scores(t, r):
                pe.wait_ge(s_xqc, t + 1)
                pe.wait_ge(s_xsub, RING + t - 1)
                for k in range(KD):
                    mm = nc.tensor.matmul(ps[:, 2 * r + k, :], xq_cur[r][:, k, :],
                                          xk_bd[:, ds(t // ST, 1), k, :, :].rearrange("p a h s -> p (a h s)"),
                                          start=True, stop=True)
                mm.then_inc(s_xs, 1)

            def cross_transposes(t, r):
                pe.wait_ge(s_xp, RING + t + 1)
                pe.wait_ge(s_xpT, RING + t)
                for j in range(HH):
                    mm = nc.tensor.transpose(ps[:, 4 + j // 4, (j % 4) * P:(j % 4 + 1) * P],
                                             xp[r][:, 2 * j:2 * j + 2, :].rearrange("p h s -> p (h s)"), ident[:])
                mm.then_inc(s_xpT_ps, 1)

            def cross_values(t):
                pe.wait_ge(s_xpT, RING + t + 1)
                pe.wait_ge(s_xon, RING + t)
                w = 2 * (HD + 1)
                for j in range(HH):
                    mm = nc.tensor.matmul(ps[:, 6, j * w:(j + 1) * w], xpT[:, j, :],
                                          xv_bd[:, ds(t // ST, 1), j, :].rearrange("p a n -> p (a n)"), start=True, stop=True)
                mm.then_inc(s_xo_ps, 1)

            def cross_out_transposes(t):
                pe.wait_ge(s_xon, RING + t + 1)
                pe.wait_ge(s_res2, RING + t)
                for k in range(KD):
                    mm = nc.tensor.transpose(ps[:, 7, k * P:(k + 1) * P], xo_n[:, k * P:(k + 1) * P], ident[:])
                mm.then_inc(s_xoT_ps, 1)

            def cross_project(t):
                pe.wait_ge(s_xoT, RING + t + 1)
                for k in range(KD):
                    nc.tensor.matmul(ps[:, 7, D:2 * D], xoT[:, k * P:(k + 1) * P], xproj_sb[:, k, :], start=(k == 0), stop=False)
                nc.tensor.matmul(ps[:, 7, D:2 * D], ones_row[:], brow[:, 1, :], start=False, stop=True).then_inc(s_pj, 1)

            def cross_step(t, r, first=False, last=False):
                cross_transposes(t, r)
                if not first:
                    cross_out_transposes(t - 1)
                if not last:
                    cross_scores(t + 2, r)
                if not first:
                    cross_project(t - 1)
                cross_values(t)

            pe.wait_ge(s_cbd, 1)
            pe.wait_ge(s_ones, 2)
            pe.wait_ge(s_res, NCHUNK + 1)
            pe.wait_ge(s_xq, KD * NCHUNK + 1)
            cross_scores(0, 0)
            cross_scores(1, 1)
            cross_step(0, 0, first=True)
            cross_step(1, 1)
            with pe.Fori(1, TILES // 2 - 1) as i:
                cross_step(2 * i, 0)
                cross_step(2 * i + 1, 1)
            cross_step(TILES - 2, 0, last=True)
            cross_step(TILES - 1, 1, last=True)
            cross_out_transposes(TILES - 1)
            cross_project(TILES - 1)

            def expert_in(c):
                pe.wait_ge(s_xn, 2 * NCHUNK + c + 2)
                after(pe, s_fT, c - 1)
                transposes(xe[:, c * CT:(c + 1) * CT, :], 2 * (c % 2)).then_inc(s_xnT_ps, 1)

            expert_in(0)
            for c in range(NCHUNK):
                if c + 1 < NCHUNK:
                    expert_in(c + 1)
                pe.wait_ge(s_xnT, 2 * NCHUNK + c + 2)
                for t in range(CT):
                    for k in range(KD):
                        i = c * CT + t
                        mm = nc.tensor.matmul(ps[:, 4, i * E_ROUTED:(i + 1) * E_ROUTED],
                                              (xnT, oT)[c % 2][:, k, t * P:(t + 1) * P],
                                              wr_sb[:, k, :], start=(k == 0), stop=(k == KD - 1))
                mm.then_inc(s_lg_ps, 1)

            def counts():
                pe.wait_ge(s_tri, 1)
                pe.wait_ge(s_picked, 1)
                for k, m in enumerate((tri, ones_sq)):
                    mm = nc.tensor.matmul(ps[:, 5, k * TE:(k + 1) * TE], m[:], picked.rearrange("p t e -> p (t e)"),
                                          start=True, stop=True)
                mm.then_inc(s_count_ps, 1)

            def gate_up(n):
                m, c = n // NCHUNK, n % NCHUNK
                pe.wait_ge(s_wcur[m], 48)
                after(pe, s_hid, RING + n - 1)
                pe.wait_ge(s_fT, c + 1)
                for a in range(2):
                    for k in range(KD):
                        mm = nc.tensor.matmul(ps[:, 4 * (c % 2) + a, :], wcur[:, m, (2 * a + k) * F:(2 * a + k + 1) * F],
                                              fT[:, k, c * CHUNK:(c + 1) * CHUNK], start=(k == 0), stop=(k == KD - 1))
                mm.then_inc(s_gu, 1)

            def down(n):
                m, c = n // NCHUNK, n % NCHUNK
                pe.wait_ge(s_hid, RING + n + 1)
                pe.wait_ge(s_acc, RING + n - 1)
                for t in range(CT):
                    mm = nc.tensor.matmul(ps[:, 4 * (c % 2) + 2 + t // 2, (t % 2) * D:(t % 2 + 1) * D],
                                          hid[:, c % 2, t * P:(t + 1) * P], wcur[:, m, 4 * F:], start=True, stop=True)
                mm.then_inc(s_y, 1)

            def shared_half(m):
                n = m * NCHUNK
                gate_up(n)
                for c in range(NCHUNK - 1):
                    gate_up(n + c + 1)
                    down(n + c)
                down(n + NCHUNK - 1)

            pe.wait_ge(s_fT, NCHUNK)
            counts()
            pe.wait_ge(s_place, 1)
            pe.wait_ge(s_res2, RING + TILES)
            shared_half(0)

            def tile_weights(j):
                return pe.value_load(owner_i[0:1, ds(j, 1)], min_val=0, max_val=(E_ROUTED - 1) * WCOLS)

            def tile_transposes(j, r):
                pe.wait_ge(s_xt[r], 16 * (j // 4 + 1))
                after(pe, s_tT, j - 1)
                for k in range(KD):
                    mm = nc.tensor.transpose(ps[:, r % 2, k * P:(k + 1) * P], xt[r][:, k * P:(k + 1) * P], ident[:])
                mm.then_inc(s_tT_ps, 1)

            def tile_gate_up(j, r, w):
                pe.wait_ge(s_tT, j + 1)
                after(pe, s_thid, j - 1)
                for k in range(KD):
                    mm = nc.tensor.matmul(ps[:, 2 + r % 2, 0:2 * F], xtT[r % 2][:, k, :],
                                          wflat[:, ds(w + k * 2 * F, 2 * F)],
                                          start=(k == 0), stop=(k == KD - 1))
                mm.then_inc(s_tgu, 1)

            def tile_hidden_transpose(j, r):
                pe.wait_ge(s_thid, j + 1)
                after(pe, s_hT, j - 1)
                nc.tensor.transpose(ps[:, 4 + r % 2, 0:F], hid_s[r % 2], ident[:]).then_inc(s_hT_ps, 1)

            def tile_down(j, r, w):
                pe.wait_ge(s_hT, j + 1)
                after(pe, s_yt, j - 1)
                nc.tensor.matmul(ps[:, 6 + r % 2, 0:D], hT[r % 2],
                                 wflat[:, ds(w + 4 * F, D)], start=True, stop=True)\
                    .then_inc(s_ty_ps, 1)

            def tile_steps(first, n):
                w = {}
                for i in range(n):
                    j, peeled = first + i, isinstance(first, int)
                    if not peeled or j + 1 < SLOT_TILES:
                        w[i + 1] = tile_weights(j + 1)
                        tile_gate_up(j + 1, (i + 1) % 4, w[i + 1])
                    tile_hidden_transpose(j, i % 4)
                    if not peeled or j + 2 < SLOT_TILES:
                        tile_transposes(j + 2, (i + 2) % 4)
                    if not peeled or j > 0:
                        if i - 1 not in w:
                            w[i - 1] = tile_weights(j - 1)
                        tile_down(j - 1, (i - 1) % 4, w[i - 1])

            pe.wait_ge(s_wres, 48 * E_ROUTED)
            pe.wait_ge(s_acc, RING + NCHUNK)
            tile_transposes(0, 0)
            tile_transposes(1, 1)
            tile_gate_up(0, 0, tile_weights(0))
            tile_steps(0, 4)
            with pe.Fori(0, (SLOT_TILES - 8) // 8) as i:
                tile_steps(8 * i + 4, 8)
            tile_steps(SLOT_TILES - 4, 4)
            tile_down(SLOT_TILES - 1, 3, tile_weights(SLOT_TILES - 1))

            pe.wait_ge(s_yt, SLOT_TILES)
            shared_half(1)

        @block.scalar
        def _(act):
            for s in (s_std, s_xnT, s_q, s_kv, s_lat, s_k, s_v, s_prob, s_pT, s_oT, s_xq, s_silu):
                act.sem_inc(s, 1)
            for s in (s_xp, s_xpT, s_xoT):
                act.sem_inc(s, RING)

            def two_banks(first):
                return ps[:, first:first + 2, :]

            def bring_in(function, place):
                nc.scalar.activation(act_scratch[:, place:place + 1], head_ind[:, 0:1], function)

            def root(n, tiles):
                act.wait_ge(s_var, n + 2)
                nc.scalar.activation(std[:, 0:tiles], std[:, 0:tiles], ACT.Sqrt).then_inc(s_std, 1)

            act.wait_ge(s_grow, 4)
            nc.scalar.activation(grow[0], pT[:, 0, :], ACT.Exp, scale=DECAY).then_inc(s_root, 1)
            nc.scalar.activation(grow[1], pT[:, 0, :], ACT.Exp, scale=-DECAY).then_inc(s_root, 1)
            nc.scalar.activation(within[:], within[:], ACT.Exp, scale=-2 * DECAY).then_inc(s_grow, 1)

            act.wait_ge(s_pool, 8)
            bring_in(ACT.Sqrt, 0)
            act.wait_ge(s_cT_ps, 1)
            nc.scalar.copy(ctxT_hi[:].rearrange("p b s -> p (b s)"), ps[:, 4, 0:B * P]).then_inc(s_cT, 1)
            nc.scalar.copy(ctxT_lo[:].rearrange("p b s -> p (b s)"), ps[0:CD - P, 5, 0:B * P]).then_inc(s_cT, 1)
            act.wait_ge(s_cv_ps, 1)
            act.wait_ge(s_const, 6)
            for r in range(2):
                src = ps[r * CS:(r + 1) * CS, 7, :].rearrange("p (b j r d) -> p b j r d", b=B, r=2, d=HD)
                nc.scalar.copy(xv_bd[r * CS:(r + 1) * CS, :, :, r * (HD + 1):r * (HD + 1) + HD], src[:, :, :, r, :])\
                    .then_inc(s_cv, 1)

            root(0, TILES)

            def queries_in(c):
                act.wait_ge(s_xnT_ps, c + 2)
                act.wait_ge(s_kv_ps, c + 1)
                nc.scalar.copy(xnT[:], two_banks(0)).then_inc(s_xnT, 1)

            def queries(c):
                act.wait_ge(s_q_ps, c + 2)
                nc.scalar.mul(qT[:, :, ds(c * CHUNK, CHUNK)], two_banks(2), ATTN_SCALE).then_inc(s_q, 1)

            def keys_and_values(c, last=False):
                act.wait_ge(s_kv_ps, c + 2)
                act.wait_ge(s_lat_ps, c + 1)
                nc.scalar.copy(kvT, two_banks(4)).then_inc(s_kv, 1)
                if not last:
                    queries_in(c + 1)
                act.wait_ge(s_lat_ps, c + 2)
                act.wait_ge(s_v_ps, c + 1)
                nc.scalar.copy(latT[:], ps[0:LAT, 6, :]).then_inc(s_lat, 1)
                if not last:
                    queries(c + 1)
                act.wait_ge(s_k_ps, c + 2)
                for k in range(KD):
                    nc.scalar.activation(kT[:, k, ds(c * CHUNK, CHUNK)], ps[:, k, :], ACT.Identity,
                                         accum_out=ksum[:, ds(c, 1), k:k + 1].rearrange("p a k -> p (a k)")).then_inc(s_k, 1)
                act.wait_ge(s_v_ps, c + 2)
                nc.scalar.copy(val[:, ds(c * CT, CT), :].rearrange("p t d -> p (t d)"),
                               two_banks(6).rearrange("p a n -> p (a n)")).then_inc(s_v, 1)

            queries_in(0)
            queries(0)
            with act.Fori(0, NCHUNK - 1) as c:
                keys_and_values(c)
            keys_and_values(NCHUNK - 1, last=True)

            act.wait_ge(s_norm_ps, 1)
            for t in (1, 0):
                if t == 0:
                    act.wait_ge(s_fl, 2)
                nc.scalar.activation(junk[:, t, :], ps[0:4 * HD, NCHUNK * t:NCHUNK * (t + 1), :].rearrange("p c n -> p (c n)"),
                                     ACT.Identity, accum_out=sums[0:4 * HD, t:t + 1]).then_inc(s_sums, 1)

            act.wait_ge(s_fl, 5)
            nc.scalar.activation(fl[:, 2:4], fl[:, 0:2], ACT.Sqrt).then_inc(s_root, 1)
            bring_in(ACT.Exp, 6)
            act.wait_ge(s_flag, 1)
            short = act.value_load(flag_i[0:1, 0:1], min_val=0, max_val=1)

            def head_exps(n, g3):
                for kt in range(ST):
                    m = ST * n + kt
                    act.wait_ge(s_fs, 2 * m + 2)
                    act.wait_ge(s_diag, m + 1)
                    after(act, s_pv, m - 1)
                    nc.scalar.activation(pT[:, kt % 2, :], two_banks(score_bank(g3, kt)).rearrange("p a n -> p (a n)"),
                                         ACT.Exp, bias=shift[:]).then_inc(s_exp, 1)

            with act.If(short == 1):
                head_exps(0, 0)
                head_exps(1, 1)
                with act.Fori(0, (B * H - 2) // 3) as i:
                    for h in range(2, 5):
                        head_exps(3 * i + h, h % 3)

            with act.If(short == 0):
                act.wait_ge(s_decay, 3)
                nc.scalar.activation(decay, decay, ACT.Exp, scale=-DECAY).then_inc(s_decay, 1)

                with act.Fori(0, B * H) as n:
                    for qt in range(ST):
                        act.wait_ge(s_nmax, n * ST + qt + 2)
                        act.wait_ge(s_pT_ps, n * ST + qt + 1)
                        act.wait_ge(s_o, (n * ST if qt < 2 else n * ST + qt - 1) + 1)
                        nc.scalar.activation(prob, sc_dec[:, qt % 2, :], ACT.Exp, bias=nmax[:, qt:qt + 1],
                                             accum_out=rsum[:, qt:qt + 1]).then_inc(s_prob, 1)
                        act.wait_ge(s_pT_ps, n * ST + qt + 2)
                        act.wait_ge(s_o_ps, n * ST + qt + 1)
                        nc.scalar.copy(probT.rearrange("p k q -> p (k q)"), two_banks(4).rearrange("p a n -> p (a n)"))\
                            .then_inc(s_pT, 1)

            def out_in(c):
                act.wait_ge(s_oT_ps, c + 2)
                act.wait_ge(s_wo, c + 1)
                nc.scalar.copy(oT[:], two_banks(0)).then_inc(s_oT, 1)

            def cross_in(c):
                act.wait_ge(s_xnT_ps, NCHUNK + c + 2)
                act.wait_ge(s_xq_ps, c + 1)
                nc.scalar.copy(xnT[:], two_banks(4)).then_inc(s_xnT, 1)

            def cross_queries(c):
                act.wait_ge(s_xq_ps, c + 2)
                for k in range(KD):
                    nc.scalar.activation(xqT[:, k, ds(c * CHUNK, CHUNK)], ps[:, 6 + k, :], ACT.Identity,
                                         bias=xqb_sb[:, k:k + 1], scale=X_SCALE).then_inc(s_xq, 1)

            act.wait_ge(s_cbd, 1)
            bring_in(ACT.Sqrt, 1)
            out_in(0)
            root(1, CT)
            with act.Fori(0, NCHUNK - 1) as c:
                out_in(c + 1)
                cross_in(c)
                root(c + 2, CT)
                cross_queries(c)
            cross_in(NCHUNK - 1)
            bring_in(ACT.Exp, 2)
            cross_queries(NCHUNK - 1)

            def cross_exp(t, r):
                act.wait_ge(s_xsub, RING + t + 1)
                act.wait_ge(s_xpT_ps, RING + t - 1)
                nc.scalar.activation(xp[r], xsc, ACT.Exp).then_inc(s_xp, 1)

            def cross_step(t, r, first=False, last=False):
                act.wait_ge(s_xpT_ps, RING + t + 1)
                act.wait_ge(s_xo_ps, RING + t)
                nc.scalar.copy(xpT, two_banks(4).rearrange("p a (j q) -> p (a j) q", q=P)).then_inc(s_xpT, 1)
                if not first:
                    cross_out(t - 1)
                if not last:
                    cross_exp(t + 1, 1 - r)

            def cross_out(t):
                act.wait_ge(s_xoT_ps, RING + t + 1)
                act.wait_ge(s_pj, RING + t)
                nc.scalar.copy(xoT, ps[:, 7, 0:D]).then_inc(s_xoT, 1)

            cross_exp(0, 0)
            cross_step(0, 0, first=True)
            cross_step(1, 1)
            with act.Fori(1, TILES // 2 - 1) as i:
                cross_step(2 * i, 0)
                cross_step(2 * i + 1, 1)
            cross_step(TILES - 2, 0)
            cross_step(TILES - 1, 1, last=True)
            cross_out(TILES - 1)

            bring_in(ACT.Sqrt, 3)
            root(NCHUNK + 1, TILES)
            for c in range(NCHUNK):
                act.wait_ge(s_xnT_ps, 2 * NCHUNK + c + 2)
                after(act, s_lg_ps, c - 1)
                nc.scalar.copy((xnT, oT)[c % 2][:], two_banks(2 * (c % 2))).then_inc(s_xnT, 1)
                nc.scalar.copy(fT[:, :, c * CHUNK:(c + 1) * CHUNK], two_banks(2 * (c % 2))).then_inc(s_fT, 1)
            bring_in(ACT.Exp, 4)
            act.wait_ge(s_below, 1)
            nc.scalar.activation(rexp, below, ACT.Exp).then_inc(s_rexp, 1)
            nc.scalar.activation(wtop[:], wtop[:], ACT.Exp).then_inc(s_rexp, 1)

            def shared_half(m):
                for c in range(NCHUNK):
                    n = m * NCHUNK + c
                    act.wait_ge(s_gu, n + 2)
                    act.wait_ge(s_hid, RING + n - 1)
                    nc.scalar.activation(silu[:, c % 2, :], ps[:, 4 * (c % 2), :], ACT.Silu).then_inc(s_silu, 1)

            bring_in(ACT.Silu, 5)
            shared_half(0)

            def tile_in(j, r):
                act.wait_ge(s_tT_ps, j + 1)
                after(act, s_tgu, j - 1)
                nc.scalar.copy(xtT[r % 2].rearrange("p k q -> p (k q)"), ps[:, r % 2, 0:D]).then_inc(s_tT, 1)

            def tile_silu(j, r):
                act.wait_ge(s_tgu, j + 1)
                after(act, s_thid, j - 1)
                nc.scalar.activation(silu_s[r % 2], ps[:, 2 + r % 2, 0:F], ACT.Silu).then_inc(s_tsilu, 1)

            def tile_step(j, r):
                if not isinstance(j, int) or j + 1 < SLOT_TILES:
                    tile_silu(j + 1, r + 1)
                if not isinstance(j, int) or j + 2 < SLOT_TILES:
                    tile_in(j + 2, r + 2)

            tile_in(0, 0)
            tile_in(1, 1)
            tile_silu(0, 0)
            for j in range(4):
                tile_step(j, j)
            with act.Fori(1, SLOT_TILES // 4 - 1) as i:
                for r in range(4):
                    tile_step(4 * i + r, r)
            for r in range(4):
                tile_step(SLOT_TILES - 4 + r, r)

            shared_half(1)

        @block.vector
        def _(dve):
            for s in (s_ln, s_var, s_xn, s_rinv, s_o, s_qm, s_clip, s_dec, s_nmax, s_res):
                dve.sem_inc(s, 1)
            for s in (s_xmax, s_xsub, s_xon, s_res2, s_hid, s_acc):
                dve.sem_inc(s, RING)

            def settled():
                dve.wait_ge(s_const, 6)

            dve.wait_ge(s_grow, 2)
            nc.vector.tensor_copy(pT[:, 0, :], pos_i).then_inc(s_grow, 1)
            nc.vector.tensor_copy(within[:], within_i)
            nc.vector.drain()
            nc.vector.tensor_scalar(within[:], within[:], 0.0, None, ALU.max).then_inc(s_grow, 1)

            dve.wait_ge(s_w, 16 * NW)
            nc.vector.tensor_tensor(wkv_sb[:], wkv_sb[:], wv_sb, ALU.add).then_inc(s_wkv, 1)

            def tile_stats(i, slot):
                return nc.vector.bn_stats(stats[:, ds(slot, 1), :].rearrange("p a n -> p (a n)"),
                                          resid[:, ds(i, 1), :].rearrange("p a d -> p (a d)"))

            def rstds(n, tiles):
                nc.vector.drain()
                for t in range(tiles):
                    nc.vector.bn_aggr(mv[:, t, :], stats[:, t, :])
                nc.vector.drain()
                nc.vector.tensor_scalar(std[:, 0:tiles], mv[:, 0:tiles, 1], EPS, None, ALU.add).then_inc(s_var, 1)
                dve.wait_ge(s_std, n + 2)
                nc.vector.reciprocal(rstd[:, 0:tiles], std[:, 0:tiles]).then_inc(s_ln, 1)
                dve.wait_ge(s_ln, n + 2)

            def normed(c, n, slot, dst=xn):
                if dst is xn:
                    dve.wait_ge(s_xnT_ps, n + 1)
                for t in range(CT):
                    i = slot + t
                    nm = nc.vector.tensor_scalar(dst[:, t, :], resid[:, ds(c * CT + t, 1), :].rearrange("p a d -> p (a d)"),
                                                 mv[:, i, 0:1], rstd[:, i:i + 1], ALU.subtract, ALU.mult)
                nm.then_inc(s_xn, 1)

            for c in range(NCHUNK):
                dve.wait_ge(s_x, 16 * (c + 1))
                for t in range(CT):
                    tile_stats(c * CT + t, c * CT + t)
            rstds(0, TILES)
            normed(0, 0, 0)

            dve.wait_ge(s_wb, 16 * NWB)
            dve.wait_ge(s_ck_ps, 1)
            for k in range(KD):
                nc.vector.tensor_scalar(xkT[:, k, :, :].rearrange("p b s -> p (b s)"), ps[:, 6, k * P:(k + 1) * P],
                                        xkb_sb[:, k:k + 1], None, ALU.add).then_inc(s_ck, 1)
            for c in range(1, NCHUNK):
                normed(c, c, c * CT)

            dve.wait_ge(s_const, 6)
            nc.vector.tensor_copy(eidx[:], eidx_i[:]).then_inc(s_eidx, 1)

            dve.wait_ge(s_wkv, 1)
            dve.wait_ge(s_ck, KD)
            for k in range(KD):
                for j in range(HH):
                    nc.vector.tensor_scalar(xk_bd[:, :, k, j, :], xkT[:, k, :, :], head_mask[:, j:j + 1], None,
                                            ALU.mult).then_inc(s_ck, 1)
            dve.wait_ge(s_cv, 2)
            dve.wait_ge(s_ck, KD + KD * HH)
            nc.vector.tensor_scalar(xqb_sb[:], xqb_sb[:], X_SCALE, None, ALU.mult).then_inc(s_cbd, 1)
            def count(instruction):
                done[0] += 1
                instruction.then_inc(s_split0, 1)
                dve.wait_ge(s_split0, done[0])

            done = [0]
            dve.wait_ge(s_grow, 5)
            tmp = pT[:, 0, :].rearrange("p (a n) -> p a n", a=2)
            for t in range(2):
                for c in range(S // CHUNK):
                    dve.wait_ge(*((s_q, c + 2) if t == 0 else (s_k, KD * (c + 1) + 1)))
                    for sign in range(2):
                        count(split(dve, nc.vector, count, tmp, 0, 0, t, sign, slice(c * CHUNK, (c + 1) * CHUNK)))
            nc.vector.memset(fl[:, 8:9], 0.0).then_inc(s_parts0, 1)

            nc.vector.memset(red[:], 0.0)
            dve.wait_ge(s_k, KD * NCHUNK + 1)
            for b in range(B):
                nc.vector.tensor_tensor(ksq[:, b, :], ksum[:, 2 * b, :], ksum[:, 2 * b + 1, :], ALU.add)
            dve.wait_ge(s_vmax, 2 * NCHUNK - 1)
            nc.vector.drain()
            nc.vector.tensor_tensor(ksq[:], ksq[:], ksq[:], ALU.mult).then_inc(s_fl, 1)
            nc.vector.tensor_reduce(red[:, 4:5], vsq, AX_X, ALU.max)
            dve.wait_ge(s_norm_ps, 1)
            for t in range(2):
                after(dve, s_sums, t)
                nc.vector.tensor_reduce(red[0:4 * HD, t:t + 1],
                                        ps[0:4 * HD, NCHUNK * t:NCHUNK * (t + 1), :].rearrange("p c n -> p (c n)"),
                                        AX_X, ALU.max).then_inc(s_fl, 1)
            dve.wait_ge(s_sums, 2)
            nc.vector.tensor_scalar(sums[0:4 * HD, :], sums[0:4 * HD, :], 1e37, -1.0, ALU.is_le, ALU.mult)
            nc.vector.drain()
            nc.vector.tensor_scalar(red[0:4 * HD, 5:7], sums[0:4 * HD, :], 1.0, None, ALU.add).then_inc(s_red, 1)
            dve.wait_ge(s_norm_ps, 2)
            nc.vector.tensor_reduce(red[0:2 * HD, 3:4], ps[0:2 * HD, 7, 0:B * KD], AX_X, ALU.max).then_inc(s_red, 1)
            dve.wait_ge(s_reda, 1)
            nc.vector.tensor_tensor(fl[:, 0:1], reda[:, 0:1], reda[:, 1:2], ALU.mult)
            nc.vector.tensor_tensor(fl[:, 1:2], reda[:, 0:1], reda[:, 3:4], ALU.mult)
            nc.vector.drain()
            nc.vector.tensor_scalar(fl[:, 1:2], fl[:, 1:2], 1.0 / S / S, None, ALU.mult)
            nc.vector.drain()
            nc.vector.tensor_scalar(fl[:, 0:2], fl[:, 0:2], 1.02, 1e-30, ALU.mult, ALU.max)
            nc.vector.drain()
            nc.vector.tensor_scalar(fl[:, 0:2], fl[:, 0:2], 1e30, None, ALU.min).then_inc(s_fl, 1)
            dve.wait_ge(s_fl, 4)
            nc.vector.memset(fl[:, 8:9], 0.0).then_inc(s_fl, 1)
            dve.wait_ge(s_root, 3)
            nc.vector.tensor_scalar(fl[:, 4:5], fl[:, 2:3], -SPAN, 0.0, ALU.add, ALU.max)
            nc.vector.tensor_scalar(fl[:, 5:6], reda[:, 4:5], NCHUNK * VAL_MIN ** 2, None, ALU.is_ge)
            nc.vector.tensor_scalar(fl[:, 6:7], reda[:, 4:5], VAL_MAX ** 2, None, ALU.is_le)
            nc.vector.tensor_tensor(fl[:, 7:8], reda[:, 5:6], reda[:, 6:7], ALU.max)
            nc.vector.drain()
            nc.vector.tensor_tensor(fl[:, 3:4], fl[:, 4:5], fl[:, 3:4], ALU.add)
            nc.vector.tensor_scalar(shift[:], fl[:, 4:5], -1.0, None, ALU.mult)
            nc.vector.tensor_scalar(fl[:, 7:8], fl[:, 7:8], 0.5, None, ALU.is_le)
            nc.vector.tensor_tensor(fl[:, 5:6], fl[:, 5:6], fl[:, 6:7], ALU.mult)
            nc.vector.drain()
            nc.vector.tensor_scalar(fl[:, 3:4], fl[:, 3:4], SPAN_LOW, None, ALU.is_le)
            nc.vector.tensor_tensor(fl[:, 5:6], fl[:, 5:6], fl[:, 7:8], ALU.mult)
            nc.vector.drain()
            nc.vector.tensor_tensor(fl[:, 3:4], fl[:, 3:4], fl[:, 5:6], ALU.mult)
            nc.vector.drain()
            nc.vector.tensor_copy(flag_i[:], fl[:, 3:4]).then_inc(s_flag, 1)

            dve.wait_ge(s_q, NCHUNK + 1)
            dve.wait_ge(s_k, KD * NCHUNK + 1)
            dve.wait_ge(s_flag, 1)
            short = dve.value_load(flag_i[0:1, 0:1], min_val=0, max_val=1)

            def diagonal(m, kt, g3):
                dve.wait_ge(s_fs, 2 * m + 1)
                blk = ps[:, score_bank(g3, kt) + kt // 4, (kt % 4) * P:(kt % 4 + 1) * P]
                nc.vector.tensor_tensor(blk, blk, within[:], ALU.mult).then_inc(s_diag, 1)

            def read_out(n, r):
                dve.wait_ge(s_pv, ST * (n + 1))
                after(dve, s_ot, n)
                nc.vector.tensor_copy(obT[:], ps[:, 6 + r, 0:256]).then_inc(s_ob, 1)

            def normalise(n, r):
                dve.wait_ge(s_ot, n + 1)
                o = ps[:, 6 + r, 256:512].rearrange("p (c g d) -> p g c d", c=2, g=4)
                nc.vector.reciprocal(rinv8[:].rearrange("p (g c) -> p g c", c=2), o[:, :, :, HD])
                nc.vector.drain()
                nc.vector.tensor_tensor(att[:, ds(n // H * ST, ST), ds(n % H * HD, HD)].rearrange("p (g c) d -> p g c d", c=2),
                                        o[:, :, :, 0:HD],
                                        rinv8[:].rearrange("p (g c) -> p g c", c=2).unsqueeze(3).to_broadcast([P, 4, 2, HD]),
                                        ALU.mult).then_inc(s_on, 1)

            def head_values(n, r):
                after(dve, s_pv, ST * (n - 1))
                nc.vector.tensor_copy(vcur[:, r, :, 0:HD], val[:, ds(n // H * ST, ST), ds(n % H * HD, HD)]).then_inc(s_vcur, 1)

            def head_steps(n, r, g3, first=False):
                for kt in range(ST):
                    diagonal(ST * n + kt, kt, g3)
                    if kt == 0:
                        head_values(n, r)
                    if kt == 2 and not first:
                        read_out(n - 1, 1 - r)
                    if kt == 4 and not first:
                        normalise(n - 1, 1 - r)

            dve.wait_ge(s_v, NCHUNK + 1)
            dve.wait_ge(s_pool, 8)
            with dve.If(short == 1):
                head_steps(0, 0, 0, first=True)
                head_steps(1, 1, 1)
                with dve.Fori(0, (B * H - 2) // 6) as i:
                    for h in range(2, 8):
                        head_steps(6 * i + h, h % 2, h % 3)
                read_out(B * H - 1, 1)
                normalise(B * H - 1, 1)

            def finish(b, half, j, n, qt):
                dve.wait_ge(s_prob, n * ST + qt + 2)
                nc.vector.reciprocal(rinv[:, qt:qt + 1], rsum[:, qt:qt + 1]).then_inc(s_rinv, 1)
                dve.wait_ge(s_rinv, n * ST + qt + 2)
                dve.wait_ge(s_o_ps, n * ST + qt + 2)
                nc.vector.tensor_scalar(att_g[:, ds(b * ST + qt, 1), ds(half * P + j * HD, HD)].rearrange("p a n -> p (a n)"),
                                        ps[:, 6, 0:HD], rinv[:, qt:qt + 1], None, ALU.mult).then_inc(s_o, 1)

            with dve.If(short == 0):
                dve.wait_ge(s_decay, 1)
                nc.vector.tensor_copy(decay, diff_i).then_inc(s_decay, 1)
                dve.wait_ge(s_decay, 2)
                nc.vector.scalar_tensor_tensor(out=decay, in0=decay, scalar=-1.0, in1=decay, op0=ALU.mult,
                                               op1=ALU.max).then_inc(s_decay, 1)
                dve.wait_ge(s_decay, 4)
                with dve.Fori(0, B) as b:
                    with dve.Fori(0, KD) as half:
                        with dve.Fori(0, HH) as j:
                            n = b * H + half * HH + j
                            dve.wait_ge(s_sc, n * ST + 1)
                            nc.vector.tensor_scalar(qm, qT[:, ds(half, 1), ds(b * S, S)].rearrange("p a n -> p (a n)"),
                                                    head_mask[:, ds(j, 1)], None, ALU.mult).then_inc(s_qm, 1)
                            for qt in range(ST):
                                dve.wait_ge(s_sc, n * ST + qt + 2)
                                dve.wait_ge(s_dec, n * ST + qt + 1)
                                nc.vector.tensor_scalar(sc_clip, ps[:, 2 * (qt % 2):2 * (qt % 2) + 2, :]
                                                        .rearrange("p a n -> p (a n)"), -CLAMP, CLAMP, ALU.max, ALU.min)\
                                    .then_inc(s_clip, 1)
                                settled()
                                dve.wait_ge(s_clip, n * ST + qt + 2)
                                dve.wait_ge(s_prob, (n * ST if qt < 2 else n * ST + qt - 1) + 1)
                                u0 = S - P - qt * P
                                nc.vector.tensor_tensor_reduce(sc_dec[:, qt % 2, :], sc_clip, decay[:, u0:u0 + S], 1.0,
                                                               -3.0e38, ALU.mult, ALU.max, rmax[:, qt:qt + 1]).then_inc(s_dec, 1)
                                dve.wait_ge(s_dec, n * ST + qt + 2)
                                nc.vector.tensor_scalar(nmax[:, qt:qt + 1], rmax[:, qt:qt + 1], -1.0, None, ALU.mult)\
                                    .then_inc(s_nmax, 1)
                                if qt >= 1:
                                    finish(b, half, j, n, qt - 1)
                            finish(b, half, j, n, ST - 1)
                nc.vector.drain()
                nc.vector.tensor_copy(att[:], att_g)
            nc.vector.drain()
            nc.vector.memset(fl[:, 8:9], 0.0).then_inc(s_att, 1)

            with dve.Fori(0, NCHUNK) as c:
                rc = resid[:, ds(c * CT, CT), :].rearrange("p t d -> p (t d)")
                settled()
                dve.wait_ge(s_wo, c + 2)
                nc.vector.tensor_tensor(rc, rc, ps[:, 2:4, :].rearrange("p a n -> p (a n)"), ALU.add).then_inc(s_res, 1)
                nc.vector.drain()
                for t in range(CT):
                    tile_stats(c * CT + t, t)
                rstds(c + 1, CT)
                settled()
                normed(c, NCHUNK + c, 0)

            def cross_shift(t, r):
                sc = ps[:, 2 * r:2 * r + 2, :].rearrange("p a (h s) -> p (a h) s", s=CS)
                dve.wait_ge(s_xs, RING + t + 1)
                nc.vector.tensor_reduce(xmax[:, r, :], sc, AX_X, ALU.max).then_inc(s_xmax, 1)
                dve.wait_ge(s_xmax, RING + t + 1)
                dve.wait_ge(s_xp, RING + t)
                nc.vector.tensor_tensor(xsc, sc, xmax[:, r, :].unsqueeze(2).to_broadcast([P, H, CS]), ALU.subtract)\
                    .then_inc(s_xsub, 1)

            def cross_divide(t):
                o = ps[:, 6, 0:H * (HD + 1)].rearrange("p (h d) -> p h d", d=HD + 1)
                dve.wait_ge(s_xo_ps, RING + t + 1)
                nc.vector.reciprocal(xinv[:], o[:, :, HD])
                nc.vector.drain()
                dve.wait_ge(s_xoT_ps, RING + t)
                nc.vector.tensor_tensor(xo_n.rearrange("p (h d) -> p h d", d=HD), o[:, :, 0:HD],
                                        xinv[:].unsqueeze(2).to_broadcast([P, H, HD]), ALU.mult).then_inc(s_xon, 1)

            def cross_add(t):
                rt = resid[:, ds(t, 1), :].rearrange("p a d -> p (a d)")
                dve.wait_ge(s_pj, RING + t + 1)
                nc.vector.tensor_tensor(rt, rt, ps[:, 7, D:2 * D], ALU.add).then_inc(s_res2, 1)
                nc.vector.drain()
                tile_stats(t, t)

            def cross_step(t, r, divide=True, add=True, shift_next=True):
                if divide:
                    cross_divide(t - 1)
                if add:
                    cross_add(t - 2)
                if shift_next:
                    cross_shift(t + 1, 1 - r)

            cross_shift(0, 0)
            cross_step(0, 0, divide=False, add=False)
            cross_step(1, 1, add=False)
            with dve.Fori(1, TILES // 2 - 1) as i:
                cross_step(2 * i, 0)
                cross_step(2 * i + 1, 1)
            cross_step(TILES - 2, 0)
            cross_step(TILES - 1, 1, shift_next=False)
            cross_step(TILES, 0, shift_next=False)
            cross_add(TILES - 1)

            dve.wait_ge(s_tri, 2)
            dve.wait_ge(s_eidx, 1)
            nc.vector.tensor_copy(jidx[:], jidx_i[:])
            nc.vector.drain()
            nc.vector.tensor_scalar(limit[:], eidx[:], float(P), None, ALU.mult)
            square = [P, E_ROUTED, E_ROUTED]
            nc.vector.tensor_tensor(earlier, eidx[:].unsqueeze(2).to_broadcast(square),
                                    eidx[:].unsqueeze(1).to_broadcast(square), ALU.is_gt)
            rstds(NCHUNK + 1, TILES)
            for c in range(NCHUNK):
                normed(c, 2 * NCHUNK + c, c * CT, xe[:, c * CT:(c + 1) * CT, :])

            dve.wait_ge(s_lg_ps, NCHUNK)
            nc.vector.tensor_copy(logit.rearrange("p t e -> p (t e)"), ps[:, 4, 0:TILES * E_ROUTED]).then_inc(s_lg, 1)
            nc.vector.drain()
            for t in range(TILES):
                nc.vector.max(top[:, t, :], logit[:, t, :])
            nc.vector.drain()
            nc.vector.tensor_tensor(wtop[:], top[:, :, 0:TOPK], top[:, :, 0:1].to_broadcast([P, TILES, TOPK]), ALU.subtract)
            nc.vector.tensor_tensor(below, logit, top[:, :, 0:1].to_broadcast([P, TILES, E_ROUTED]), ALU.subtract)\
                .then_inc(s_below, 1)
            for t in range(TILES):
                nc.vector.max_index(topi[:, t, :], top[:, t, :], logit[:, t, :])
            nc.vector.drain()
            nc.vector.tensor_copy(topf[:], topi[:, :, 0:2])
            dve.wait_ge(s_eidx, 1)
            nc.vector.drain()
            for r in range(TOPK):
                nc.vector.tensor_tensor(pick[r], eidx[:].unsqueeze(1).to_broadcast([P, TILES, E_ROUTED]),
                                        topf[:, :, r:r + 1].to_broadcast([P, TILES, E_ROUTED]), ALU.is_equal)
            nc.vector.drain()
            nc.vector.tensor_tensor(picked, pick[0], pick[1], ALU.add).then_inc(s_picked, 1)

            nc.vector.memset(before[:, 0, :], 0.0)
            dve.wait_ge(s_count_ps, 1)
            for t in range(TILES):
                nc.vector.drain()
                nc.vector.tensor_tensor(before[:, t + 1, :], before[:, t, :],
                                        ps[:, 5, TE + t * E_ROUTED:TE + (t + 1) * E_ROUTED], ALU.add)
            nc.vector.drain()
            nc.vector.tensor_tensor(over, before[:, TILES, :].unsqueeze(2).to_broadcast(square),
                                    limit[:].unsqueeze(1).to_broadcast(square), ALU.is_gt)
            nc.vector.tensor_tensor(place_of, before[:, 0:TILES, :],
                                    ps[:, 5, 0:TE].rearrange("p (t e) -> p t e", e=E_ROUTED), ALU.add)
            nc.vector.drain()
            nc.vector.tensor_reduce(ntiles[:], over, AX_X, ALU.add)
            nc.vector.drain()
            nc.vector.tensor_tensor(over, earlier, ntiles[:].unsqueeze(1).to_broadcast(square), ALU.mult)
            nc.vector.drain()
            nc.vector.tensor_reduce(start[:], over, AX_X, ALU.add)
            nc.vector.drain()
            nc.vector.tensor_scalar(start_slot[:], start[:], float(P), None, ALU.mult)
            nc.vector.tensor_tensor(stop[:], start[:], ntiles[:], ALU.add)
            nc.vector.drain()
            nc.vector.tensor_tensor(place_of, place_of, start_slot[:].unsqueeze(1).to_broadcast([P, TILES, E_ROUTED]),
                                    ALU.add)
            for r in range(TOPK):
                nc.vector.drain()
                nc.vector.tensor_tensor(mine, place_of, pick[r], ALU.mult)
                nc.vector.drain()
                nc.vector.tensor_reduce(place[:, r, :], mine, AX_X, ALU.add)
            nc.vector.drain()
            nc.vector.tensor_copy(place_i[:], place[:]).then_inc(s_place, 1)
            nc.vector.tensor_tensor(ended, jidx[:].unsqueeze(2).to_broadcast([P, SLOT_TILES, E_ROUTED]),
                                    stop[:].unsqueeze(1).to_broadcast([P, SLOT_TILES, E_ROUTED]), ALU.is_ge)
            nc.vector.drain()
            nc.vector.tensor_reduce(owner[:], ended, AX_X, ALU.add)
            nc.vector.drain()
            nc.vector.tensor_scalar(owner[:], owner[:], E_ROUTED - 1.0, float(WCOLS), ALU.min, ALU.mult)
            nc.vector.drain()
            nc.vector.tensor_copy(owner_i[:], owner[:])
            dve.wait_ge(s_rexp, 2)
            nc.vector.tensor_reduce(resum[:], rexp, AX_X, ALU.add)
            nc.vector.drain()
            nc.vector.reciprocal(reinv[:], resum[:])
            nc.vector.drain()
            nc.vector.tensor_tensor(wtop[:], wtop[:], reinv[:].unsqueeze(2).to_broadcast([P, TILES, TOPK]), ALU.mult)
            nc.vector.drain()

            def hidden(n):
                r = n % 2
                dve.wait_ge(s_silu, n + 2)
                dve.wait_ge(s_y, RING + n - 1)
                nc.vector.tensor_tensor(hid[:, r, :], silu[:, r, :], ps[:, 4 * r + 1, :], ALU.mult).then_inc(s_hid, 1)

            def accumulate(n):
                c = n % NCHUNK
                rc = resid[:, c * CT:(c + 1) * CT, :].rearrange("p t d -> p (t d)")
                dve.wait_ge(s_y, RING + n + 1)
                first = 4 * (c % 2) + 2
                nc.vector.tensor_tensor(rc, rc, ps[:, first:first + 2, :].rearrange("p a n -> p (a n)"), ALU.add)\
                    .then_inc(s_acc, 1)

            def shared_half(m, between):
                n = m * NCHUNK
                hidden(n)
                for c in range(NCHUNK):
                    if c + 1 < NCHUNK:
                        hidden(n + c + 1)
                    accumulate(n + c)
                    between(c)

            shared_half(0, lambda c: None)

            def tile_hidden(j, r):
                dve.wait_ge(s_tsilu, j + 1)
                after(dve, s_hT_ps, j - 1)
                nc.vector.tensor_tensor(hid_s[r % 2], silu_s[r % 2], ps[:, 2 + r % 2, F:2 * F], ALU.mult).then_inc(s_thid, 1)

            def tile_hidden_in(j, r):
                dve.wait_ge(s_hT_ps, j + 1)
                after(dve, s_ty_ps, j - 1)
                nc.vector.tensor_copy(hT[r % 2], ps[:, 4 + r % 2, 0:F]).then_inc(s_hT, 1)

            def tile_result(j, r):
                dve.wait_ge(s_ty_ps, j + 1)
                after(dve, s_yst[r % 4], 16 * (j // 4))
                nc.vector.tensor_copy(yt[r % 4], ps[:, 6 + r % 2, 0:D]).then_inc(s_yt, 1)

            def tile_step(j, r):
                if not isinstance(j, int) or j + 1 < SLOT_TILES:
                    tile_hidden(j + 1, r + 1)
                tile_hidden_in(j, r)
                if not isinstance(j, int) or j > 0:
                    tile_result(j - 1, r - 1)

            tile_hidden(0, 0)
            for j in range(4):
                tile_step(j, j)
            with dve.Fori(1, SLOT_TILES // 4 - 1) as i:
                for r in range(4):
                    tile_step(4 * i + r, r)
            for r in range(4):
                tile_step(SLOT_TILES - 4 + r, r)
            tile_result(SLOT_TILES - 1, 3)

            def combine(g):
                t, r = g // TOPK, g % TOPK
                dve.wait_ge(s_yg[g % YG], 16 * (g // YG + 1))
                after(dve, s_comb, g)
                nc.vector.scalar_tensor_tensor(out=resid[:, t, :], in0=xe[:, g % YG, :], scalar=wtop[:, t, r:r + 1],
                                               in1=resid[:, t, :], op0=ALU.mult, op1=ALU.add).then_inc(s_comb, 1)

            def some_combined(c):
                dve.wait_ge(s_acc, RING + NCHUNK + c + 1)
                for g in range(4 * c, 4 * (c + 1)):
                    combine(g)

            shared_half(1, some_combined)
            for g in range(4 * NCHUNK, TOPK * TILES):
                combine(g)


_INS = ["x", "ctx_768", "L0_attn_Wq", "L0_attn_Wk", "L0_attn_Wv", "L0_attn_Wo", "L0_attn_W_down_kv", "L0_attn_W_up_k",
        "L0_attn_W_up_v", "L0_xattn_q_w", "L0_xattn_q_b", "L0_xattn_kv_w", "L0_xattn_kv_b", "L0_xattn_proj_w",
        "L0_xattn_proj_b", "L0_ffn_Wr", "L0_ffn_Wg", "L0_ffn_Wu", "L0_ffn_Wd", "L0_ffn_Sg", "L0_ffn_Su", "L0_ffn_Sd"]
_OUTS = [((B, S, D), "float32")]


def kernel(**inputs):
    import numpy as _np
    import concourse.bacc as _bacc
    from concourse import mybir as _mybir
    from concourse.bass_utils import run_bass_kernel_spmd as _run

    nc = _bacc.Bacc("TRN2", target_bir_lowering=False, num_devices=1)
    arrays, args = {}, []
    for name in _INS:
        a = _np.ascontiguousarray(inputs[name])
        arrays[f"in_{name}_dram"] = a
        args.append(nc.dram_tensor(f"in_{name}_dram", a.shape, _mybir.dt.from_np(a.dtype), kind="ExternalInput").ap())
    for i, (shape, dtype) in enumerate(_OUTS):
        dt = _mybir.dt.from_np(_np.dtype(dtype))
        args.append(nc.dram_tensor(f"out_{i}_dram", shape, dt, kind="ExternalOutput").ap())
    decoder_layer(nc, *args)
    r = _run(nc, [arrays], core_ids=[0])
    return r.results[0]["out_0_dram"]
```
